# Optimizing a Trainium2 kernel written in Bass

```python
import numpy as np
import jax
import jax.numpy as jnp

def _softmax(x, axis=-1):
    return jax.nn.softmax(x, axis=axis)

def _gelu(x):
    return jax.nn.gelu(x, approximate=True)

def _silu(x):
    return jax.nn.silu(x)

def _sigmoid(x):
    return jax.nn.sigmoid(x)

def _layernorm(x, axis=-1, eps=1e-05):
    m = jnp.mean(x, axis=axis, keepdims=True)
    v = jnp.var(x, axis=axis, keepdims=True)
    return (x - m) / jnp.sqrt(v + eps)

def _scatter_add(tgt, idx, src, axis=0):
    return tgt.at[idx].add(src)

def _segment_sum(src, seg, n):
    return jax.ops.segment_sum(src, seg, n)
kernel_name = 'mk_adj_preln_d4_adj_r2_b913ac'

def setup_inputs(seed: int=0):
    np.random.seed(seed)
    _w = jnp.asarray

    def _rec_inputs():
        import jax
        import jax.numpy as jnp
        _gk = jax.random.key(seed)
        x = -0.000929 + 1 * jax.random.normal(jax.random.fold_in(_gk, 1), (2048, 256), jnp.float32)
        _w = (1.0 + jnp.arange(2048, dtype=jnp.float32)) ** (-0.5)
        _w = _w / _w.mean()
        _pij = jnp.clip(0.00195312 * _w[:, None] * _w[None, :], 0.0, 1.0)
        _a = jax.random.uniform(jax.random.fold_in(_gk, 2), (2048, 2048)) < _pij
        _af = _a.astype(jnp.float32)
        _af = _af * jax.random.uniform(jax.random.fold_in(_gk, 3), (2048, 2048), jnp.float32, 0.05, 5.22011)
        adj = _af
        return (x, adj)
    x, adj = _rec_inputs()

    def _L0_gnn_setup():
        import jax, jax.numpy as jnp
        import numpy as np
        N = 1024
        HID = 256
        H = 8
        key = jax.random.key(seed)
        ks = jax.random.split(key, 8)
        x = jax.random.normal(ks[0], (N, HID), dtype=jnp.float32)
        sp = jax.random.normal(ks[1], (N, N), dtype=jnp.float32)
        zero_mask = jax.random.uniform(ks[2], (N, N)) < 0.2
        spatial_encoding = jnp.where(zero_mask, 0.0, sp)
        edge_encoding = jax.random.normal(ks[3], (N, N), dtype=jnp.float32)
        s = 1.0 / np.sqrt(HID)
        Wq = jax.random.normal(ks[4], (HID, HID * H), dtype=jnp.float32) * s
        Wk = jax.random.normal(ks[5], (HID, HID * H), dtype=jnp.float32) * s
        Wv = jax.random.normal(ks[6], (HID, HID * H), dtype=jnp.float32) * s
        Wout = jax.random.normal(ks[7], (HID * H, HID), dtype=jnp.float32) * (1.0 / np.sqrt(HID * H))
        return {'x': x, 'spatial_encoding': spatial_encoding, 'edge_encoding': edge_encoding, 'Wq': Wq, 'Wk': Wk, 'Wv': Wv, 'Wout': Wout}
    _L0_gnn_all = _L0_gnn_setup()
    _L0_gnn_in = {k: v for k, v in _L0_gnn_all.items() if k in ('Wq', 'Wk', 'Wv', 'Wout')}
    del _L0_gnn_all

    def _L1_gnn_setup():
        import jax, jax.numpy as jnp
        import numpy as np
        N, D_IN, D_ATTN, STEPS, P_NUC, TAU = (2048, 256, 64, 2, 0.9, 1.0)
        LN_EPS = 1e-05

        def _xavier(key, shape):
            fan_in, fan_out = (shape[-2], shape[-1])
            lim = np.sqrt(6.0 / (fan_in + fan_out))
            return jax.random.uniform(key, shape, jnp.float32, -lim, lim)

        def _adj_from_feats(Xa, W1, W2, W3):
            Q = Xa @ W1
            K = Xa @ W3
            logits = Q @ W2 @ K.T / TAU
            idx = jnp.argsort(-logits, axis=1)
            vals = jnp.take_along_axis(logits, idx, axis=1)
            csum = jnp.cumsum(jax.nn.softmax(vals, axis=1), axis=1)
            k_i = jnp.sum(csum < P_NUC, axis=1) + 1
            ranks = jnp.arange(logits.shape[1])[None, :]
            keep_sorted = ranks < k_i[:, None]
            inv = jnp.argsort(idx, axis=1)
            keep = jnp.take_along_axis(keep_sorted, inv, axis=1)
            masked = jnp.where(keep, logits, -jnp.inf)
            return jax.nn.softmax(masked, axis=1)
        key = jax.random.key(seed)
        ks = jax.random.split(key, 9)
        return {'X': jax.random.normal(ks[0], (N, D_IN), jnp.float32), 'S': jax.random.uniform(ks[1], (N, N), jnp.float32), 'W1': _xavier(ks[2], (D_IN, D_ATTN)), 'W2': _xavier(ks[3], (D_ATTN, D_ATTN)), 'W3': _xavier(ks[4], (D_IN, D_ATTN)), 'U1': _xavier(ks[5], (STEPS, D_IN, D_IN)), 'U2': _xavier(ks[6], (STEPS, D_IN, D_IN)), 'U3': _xavier(ks[7], (STEPS, D_IN, D_IN)), 'gamma': jnp.ones((D_IN,), jnp.float32), 'beta': jnp.zeros((D_IN,), jnp.float32)}
    _L1_gnn_all = _L1_gnn_setup()
    _L1_gnn_in = {k: v for k, v in _L1_gnn_all.items() if k in ('W1', 'W2', 'W3', 'U1', 'U2', 'U3', 'gamma', 'beta')}
    del _L1_gnn_all

    def _L2_gnn_setup():
        import jax, jax.numpy as jnp
        import numpy as np
        EPS = 1e-08
        key = jax.random.key(seed)
        k1, k2, k3, k4 = jax.random.split(key, 4)
        N, IN, OUT = (4096, 256, 256)
        x = jax.random.normal(k1, (N, IN), dtype=jnp.float32)
        adj = jax.random.uniform(k2, (N, N), dtype=jnp.float32)
        W = jax.random.normal(k3, (OUT, IN), dtype=jnp.float32) * (1.0 / np.sqrt(IN))
        b = jax.random.normal(k4, (OUT,), dtype=jnp.float32) * 0.01
        return {'x': x, 'adj': adj, 'W': W, 'b': b}
    _L2_gnn_all = _L2_gnn_setup()
    _L2_gnn_in = {k: v for k, v in _L2_gnn_all.items() if k in ('W', 'b')}
    del _L2_gnn_all

    def _L3_gnn_setup():
        import jax, jax.numpy as jnp
        import numpy as np
        N = 4096
        IN_F = 256
        OUT_F = 256
        key = jax.random.key(seed)
        k_x, k_adj, k_w = jax.random.split(key, 3)
        x = jax.random.normal(k_x, (N, IN_F), dtype=jnp.float32)
        adj = jax.random.uniform(k_adj, (N, N), dtype=jnp.float32)
        stdv = 1.0 / np.sqrt(OUT_F)
        weight = jax.random.uniform(k_w, (IN_F, OUT_F), dtype=jnp.float32, minval=-stdv, maxval=stdv)
        return {'x': x, 'adj': adj, 'weight': weight}
    _L3_gnn_all = _L3_gnn_setup()
    _L3_gnn_in = {k: v for k, v in _L3_gnn_all.items() if k in ('weight',)}
    del _L3_gnn_all
    return {'x': x, 'adj': adj, 'L0_gnn_Wq': _L0_gnn_in['Wq'], 'L0_gnn_Wk': _L0_gnn_in['Wk'], 'L0_gnn_Wv': _L0_gnn_in['Wv'], 'L0_gnn_Wout': _L0_gnn_in['Wout'], 'L1_gnn_W1': _L1_gnn_in['W1'], 'L1_gnn_W2': _L1_gnn_in['W2'], 'L1_gnn_W3': _L1_gnn_in['W3'], 'L1_gnn_U1': _L1_gnn_in['U1'], 'L1_gnn_U2': _L1_gnn_in['U2'], 'L1_gnn_U3': _L1_gnn_in['U3'], 'L1_gnn_gamma': _L1_gnn_in['gamma'], 'L1_gnn_beta': _L1_gnn_in['beta'], 'L2_gnn_W': _L2_gnn_in['W'], 'L2_gnn_b': _L2_gnn_in['b'], 'L3_gnn_weight': _L3_gnn_in['weight']}

def reference(x, adj, L0_gnn_Wq, L0_gnn_Wk, L0_gnn_Wv, L0_gnn_Wout, L1_gnn_W1, L1_gnn_W2, L1_gnn_W3, L1_gnn_U1, L1_gnn_U2, L1_gnn_U3, L1_gnn_gamma, L1_gnn_beta, L2_gnn_W, L2_gnn_b, L3_gnn_weight):
    import jax
    import jax.numpy as jnp

    def _L0_gnn_ref(x, spatial_encoding, edge_encoding, Wq, Wk, Wv, Wout):
        import jax, jax.numpy as jnp
        import numpy as np
        N = 1024
        HID = 256
        H = 8
        n, d = x.shape
        h = Wq.shape[1] // d
        scale = d ** (-0.5)
        q = (x @ Wq).reshape(h, n, d)
        k = (x @ Wk).reshape(h, n, d)
        v = (x @ Wv).reshape(h, n, d)
        a = jnp.einsum('hnd,hmd->hnm', q, k) * scale
        a = a + spatial_encoding + edge_encoding
        mask = spatial_encoding == 0.0
        a = jnp.where(mask, -1000000.0, a)
        a = jax.nn.softmax(a, axis=-1)
        a = jnp.where(mask, 0.0, a)
        out = jnp.einsum('hnm,hmd->hnd', a, v)
        out = out.transpose(1, 0, 2).reshape(n, h * d)
        return out @ Wout

    def _L1_gnn_ref(X, S, W1, W2, W3, U1, U2, U3, gamma, beta):
        import jax, jax.numpy as jnp
        import numpy as np
        N, D_IN, D_ATTN, STEPS, P_NUC, TAU = (2048, 256, 64, 2, 0.9, 1.0)
        LN_EPS = 1e-05

        def _xavier(key, shape):
            fan_in, fan_out = (shape[-2], shape[-1])
            lim = np.sqrt(6.0 / (fan_in + fan_out))
            return jax.random.uniform(key, shape, jnp.float32, -lim, lim)

        def _adj_from_feats(Xa, W1, W2, W3):
            Q = Xa @ W1
            K = Xa @ W3
            logits = Q @ W2 @ K.T / TAU
            idx = jnp.argsort(-logits, axis=1)
            vals = jnp.take_along_axis(logits, idx, axis=1)
            csum = jnp.cumsum(jax.nn.softmax(vals, axis=1), axis=1)
            k_i = jnp.sum(csum < P_NUC, axis=1) + 1
            ranks = jnp.arange(logits.shape[1])[None, :]
            keep_sorted = ranks < k_i[:, None]
            inv = jnp.argsort(idx, axis=1)
            keep = jnp.take_along_axis(keep_sorted, inv, axis=1)
            masked = jnp.where(keep, logits, -jnp.inf)
            return jax.nn.softmax(masked, axis=1)
        n = X.shape[0]
        S = S + jnp.eye(n, dtype=X.dtype)
        Rf = S / jnp.clip(S.sum(axis=1, keepdims=True), 1e-12)
        Rb = S / jnp.clip(S.sum(axis=0), 1e-12)[:, None]
        Xf, Xb, Xa = (X, X, X)
        Z = jnp.zeros_like(X)
        for s in range(STEPS):
            A = _adj_from_feats(Xa, W1, W2, W3)
            Xf = Rf @ Xf
            Xb = Rb @ Xb
            Xa = A @ Xa
            Z = Z + (Xf @ U1[s] + Xb @ U2[s] + Xa @ U3[s])
        Y = X + Z
        mu = Y.mean(axis=-1, keepdims=True)
        var = Y.var(axis=-1, keepdims=True)
        return (Y - mu) / jnp.sqrt(var + LN_EPS) * gamma + beta

    def _L2_gnn_ref(x, adj, W, b):
        import jax, jax.numpy as jnp
        import numpy as np
        EPS = 1e-08
        deg = adj.sum(axis=1)
        dis = (deg + EPS) ** (-0.5)
        a_norm = dis[:, None] * adj * dis[None, :]
        h = a_norm @ x
        return h @ W.T + b

    def _L3_gnn_ref(x, adj, weight):
        import jax, jax.numpy as jnp
        import numpy as np
        N = 4096
        IN_F = 256
        OUT_F = 256
        n = adj.shape[0]
        adj_hat = adj + jnp.eye(n, dtype=adj.dtype)
        rowsum = adj_hat.sum(axis=1)
        d_inv_sqrt = jnp.power(rowsum, -0.5)
        d_inv_sqrt = jnp.where(jnp.isinf(d_inv_sqrt), 0.0, d_inv_sqrt)
        adj_norm = adj_hat * d_inv_sqrt[:, None] * d_inv_sqrt[None, :]
        support = x @ weight
        out = adj_norm @ support
        return jax.nn.relu(out)
    h = jnp.maximum(_layernorm(x, axis=-1), 0.0)
    x = x + _L0_gnn_ref(h, adj, adj, L0_gnn_Wq, L0_gnn_Wk, L0_gnn_Wv, L0_gnn_Wout)
    h = jnp.maximum(_layernorm(x, axis=-1), 0.0)
    x = x + _L1_gnn_ref(h, adj, L1_gnn_W1, L1_gnn_W2, L1_gnn_W3, L1_gnn_U1, L1_gnn_U2, L1_gnn_U3, L1_gnn_gamma, L1_gnn_beta)
    h = jnp.maximum(_layernorm(x, axis=-1), 0.0)
    x = x + _L2_gnn_ref(h, adj, L2_gnn_W, L2_gnn_b)
    h = jnp.maximum(_layernorm(x, axis=-1), 0.0)
    x = x + _L3_gnn_ref(h, adj, L3_gnn_weight)
    return x

_drawn_inputs = setup_inputs


def setup_inputs(seed=0):
    import zlib

    import numpy as np

    out = dict(_drawn_inputs(seed))
    spreads = {'L1_gnn_gamma': (1.0, 0.2), 'L1_gnn_beta': (0.0, 0.1)}
    factors = {}
    for name, (base, spread) in spreads.items():
        noise = np.random.default_rng([zlib.crc32(name.encode()), seed]).standard_normal(out[name].shape)
        drawn = base * np.exp(spread * noise) if base else spread * noise
        out[name] = jnp.asarray(drawn.astype(out[name].dtype))
    for name, factor in factors.items():
        out[name] = (out[name] * factor).astype(out[name].dtype)
    return out
```

```python
from contextlib import ExitStack

import concourse.bass as bass
from concourse import mybir

F32 = mybir.dt.float32
F16 = mybir.dt.float16
BF16 = mybir.dt.bfloat16
I32 = mybir.dt.int32
U32 = mybir.dt.uint32
ALU = mybir.AluOpType
ACT = mybir.ActivationFunctionType
X = mybir.AxisListType.X
ABSMAX = bass.bass_isa.ReduceOp.absmax
ds = bass.ds

P = 128
N, D, HEADS = 2048, 256, 8
T = N // P
KC = D // P
CH = N // (N // HEADS)
ROWS = N // HEADS
BANK = 512
MASKED = -1.0e6
FAR = -1.0e30
H_SCALE = 16.0
P_SCALE = 32768.0
VW_SCALE = 2.0 ** -7
LN_EPS = 1e-5
A_SCALE = 64.0
X_SCALE = 1024.0
P_NUC = 0.9
G = 4
BISECTIONS = 9
BW = N + 8


class Chain:

    def __init__(self, engine, sem, base=0):
        self.engine, self.sem, self.base, self.n = engine, sem, base, 0

    def __call__(self, ins):
        self.note(ins)
        self.wait()

    def wait(self):
        self.engine.wait_ge(self.sem, self.base + self.n)

    def note(self, ins):
        self.n += 1
        ins.then_inc(self.sem, 1)


def nodes(ap):
    return ap.rearrange("(q p c) d -> p c q d", q=2, p=P, c=CH)


def permuted(ap):
    return ap.rearrange("p (r c) -> p c r", c=CH)


def normalize_stats(nc, eng, chain, x, stats, mv):
    for t in range(T):
        chain.note(nc.vector.bn_stats(stats[:, t, :], x[:, t, :]))
    chain.wait()
    for t in range(T):
        chain.note(nc.vector.bn_aggr(mv[:, t, :], stats[:, t, :]))
    chain.wait()


def build(nc, a, out):
    g = ExitStack()

    def sb(stack, name, shape, dt=F32):
        return stack.enter_context(nc.sbuf_tensor(name, shape, dt))

    def ps(stack, name, shape, dt=F32):
        return stack.enter_context(nc.psum_tensor(name, shape, dt))

    with g:
        def phase(run, *args, **kwargs):
            own = []

            def sem(name):
                own.append(nc.alloc_semaphore(name))
                return own[-1]

            run(nc, sb, ps, sem, *args, **kwargs)
            nc.clear_and_free_semaphores(own)
            nc.all_engine_barrier()

        bias_d = nc.dram_tensor("bias_scratch", (T, P, BW), F32, kind="Internal").ap()
        at_d = nc.dram_tensor("adjT_scratch", (T, P, 2 * N), F16, kind="Internal").ap()

        acc = sb(g, "acc", [P, T, D])
        ident = sb(g, "ident", [P, P])
        am = sb(g, "am", [P, 4])
        winv = sb(g, "winv", [P, 4])
        sc = sb(g, "sc", [P, 8])
        halfp = sb(g, "halfp", [P, T])
        deg = sb(g, "deg", [P, 2, T])

        with ExitStack() as c:
            WH = [sb(c, f"w{n}_hi", [P, KC, N], F16) for n in "qkv"]
            WL = [sb(c, f"w{n}_lo", [P, KC, N], F16) for n in "qkv"]
            hT_hi = sb(c, "hT_hi", [P, KC, N], F16)
            hT_lo = sb(c, "hT_lo", [P, KC, N], F16)
            phase(setup, a, bias_d, acc, ident, am, winv, sc, halfp, WH, WL, hT_hi, hT_lo)
            phase(adjacency, a["adj"], bias_d, at_d, sc, ident, deg)
            phase(attend, a["L0_gnn_Wout"], bias_d, acc, ident, winv, sc, WH, WL, hT_hi, hT_lo)

        scales = sb(g, "scales", [P, 4, T])
        ident16 = sb(g, "ident16", [P, P], BF16)
        with ExitStack() as c:
            w1, w3 = sb(c, "w1", [P, KC, 64]), sb(c, "w3", [P, KC, 64])
            w2 = sb(c, "w2", [64, 64])
            U = [sb(c, f"u{n}", [P, 2, KC, D]) for n in range(3)]
            gb = sb(c, "gamma_beta", [P, 2, D])
            Y = sb(c, "y", [P, T, D])
            phase(prepare, a, deg, scales, ident, ident16, halfp, w1, w2, w3, U, gb)
            phase(normalize, "l1", acc, Y, halfp, 1.0)
            with ExitStack() as c1:
                Xp = [sb(c1, f"x_{n}", [P, T, D], F16) for n in ("hi", "lo")]
                Xf = [sb(c1, f"xf_{n}", [P, T, D], F16) for n in ("hi", "lo")]
                Xb = [sb(c1, f"xb_{n}", [P, T, D], BF16) for n in range(3)]
                phase(split_rows, "l1x", Y, Xp, X_SCALE)
                phase(diffuse, "s1", at_d, ident, ident16, Y, [
                    (Xp, X_SCALE, [(scales[:, 0, :], Xf, X_SCALE, U[0][:, 0, :, :]),
                                   (scales[:, 1, :], Xb, 1.0, U[1][:, 0, :, :])])])
                phase(diffuse, "s2", at_d, ident, ident16, Y, [
                    (Xf, X_SCALE, [(scales[:, 0, :], None, 1.0, U[0][:, 1, :, :])]),
                    (Xb, 1.0, [(scales[:, 1, :], None, 1.0, U[1][:, 1, :, :])])])
            with ExitStack() as c1:
                XA = sb(c1, "xa", [P, T, D])
                Xp = [sb(c1, f"xa_{n}", [P, T, D], F16) for n in ("hi", "lo")]
                QT, KT = sb(c1, "logit_q", [64, N]), sb(c1, "logit_k", [64, N])
                phase(normalize, "l1a", acc, XA, halfp, 1.0)
                for step in range(2):
                    phase(split_rows, f"xa{step}", XA, Xp, X_SCALE)
                    phase(features, f"qk{step}", XA, ident, [], (w1, w2, w3, QT, KT))
                    phase(nucleus, f"nuc{step}", QT, KT, Xp, XA, ident)
                    phase(features, f"u3{step}", XA, ident, [(U[2][:, step, :, :], Y)], None)
            phase(normalize, "l1out", Y, Y, halfp, None, gb, acc)
        with ExitStack() as c:
            H = sb(c, "h", [P, T, D])
            Hp = [sb(c, f"h_{n}", [P, T, D], BF16) for n in range(3)]
            wT, w = sb(c, "l2_wT", [P, KC, D]), sb(c, "l3_w", [P, KC, D])
            bb = sb(c, "l2_bias", [P, D])
            phase(last_weights, a, ident, wT, w, bb)
            phase(normalize, "l2", acc, H, halfp, 1.0)
            phase(split_rows, "l2h", H, Hp, 1.0, scales[:, 2, :])
            phase(diffuse, "l2d", at_d, ident, None, acc, [
                (Hp, 1.0, [(scales[:, 2, :], None, 1.0, wT[:, :, :])])])
            phase(add_row, "l2b", acc, bb)
            phase(normalize, "l3", acc, H, halfp, 1.0)
            phase(features, "l3w", H, ident, [(w[:, :, :], None)], None)
            phase(split_rows, "l3h", H, Hp, 1.0, scales[:, 3, :])
            phase(diffuse, "l3d", at_d, ident, ident16, acc, [
                (Hp, 1.0, [(scales[:, 3, :], None, 1.0, None)])], relu=True)
        phase(finish, acc, out)


def setup(nc, sb, ps, sem, a, bias_d, acc, ident, am, winv, sc, halfp, WH, WL, hT_hi, hT_lo):
    w_loaded, x_loaded, rest_loaded = sem("w_loaded"), sem("x_loaded"), sem("rest_loaded")
    dve, pool = sem("setup_dve"), sem("setup_pool")
    extremes, largest, powers, w_hi, stats_done = sem("extremes"), sem("largest"), sem("powers"), sem("w_hi"), sem("stats_done")
    rstd_done, centred, rectified, h_tp, h_hi, h_lo = (sem(s) for s in ("rstd_done", "centred", "rectified", "h_tp", "h_hi", "h_lo"))
    ident_made = sem("ident_made")
    with ExitStack() as c:
        stage = [sb(c, f"w_stage{n}", [P, KC, N]) for n in range(3)]
        hx = sb(c, "hx", [P, T, D])
        stats, mv = sb(c, "stats", [P, T, 6]), sb(c, "mv", [P, T, 2])
        rstd = sb(c, "rstd", [P, T])
        ext = sb(c, "ext", [P, 8])
        wo = acc
        tp = [ps(c, f"h_tp{n}", [P, BANK]) for n in range(2)]

        block = nc.Block()
        with block:
            @block.sync
            def _(sp):
                sp.dma_start(hx[:, :, :], a["x"].rearrange("(t p) d -> p t d", p=P)).then_inc(x_loaded, 16)
                for n, w in enumerate(("Wq", "Wk", "Wv")):
                    sp.dma_start(stage[n][:, :, :], a["L0_gnn_" + w].rearrange("(k p) n -> p k n", p=P)).then_inc(w_loaded, 16)
                sp.dma_start(wo[:, :, :], a["L0_gnn_Wout"].rearrange("(t p) d -> p t d", p=P)).then_inc(w_loaded, 16)
                sp.wait_ge(extremes, 1)
                for q in range(2):
                    sp.dma_start(acc[:, :, :].rearrange("p (c q) d -> p c q d", q=2)[:, :, q, :],
                                 nodes(a["x"])[:, :, q, :]).then_inc(rest_loaded, 16)
                sp.wait_ge(rest_loaded, 32)

            @block.gpsimd
            def _(pl):
                nc.gpsimd.memset(ident[:, :], 0.0).then_inc(pool, 1)
                pl.wait_ge(pool, 1)
                nc.gpsimd.affine_select(out=ident[:, :], in_=ident[:, :], compare_op=ALU.not_equal, fill=1.0, base=0,
                                        pattern=[[-1, P]], channel_multiplier=1).then_inc(ident_made, 1)
                nc.gpsimd.memset(halfp[:, :], -0.5).then_inc(pool, 1)
                pl.wait_ge(stats_done, 1)
                nc.gpsimd.tensor_scalar(rstd[:, :], mv[:, :, 1], LN_EPS, None, ALU.add).then_inc(pool, 1)
                pl.wait_ge(pool, 3)
                nc.gpsimd.tensor_tensor(rstd[:, :], rstd[:, :], halfp[:, :], ALU.pow).then_inc(rstd_done, 1)
                pl.wait_ge(extremes, 1)
                nc.gpsimd.partition_all_reduce(am[:, :], ext[:, 0:4], P, ABSMAX).then_inc(largest, 1)

            @block.vector
            def _(v):
                link = Chain(v, dve)
                v.wait_ge(x_loaded, 16)
                normalize_stats(nc, v, link, hx, stats, mv)
                nc.vector.memset(ext[:, :], 0.0).then_inc(stats_done, 1)
                v.wait_ge(rstd_done, 1)
                v.wait_ge(stats_done, 1)
                for t in range(T):
                    nc.vector.tensor_scalar(hx[:, t, :], hx[:, t, :], mv[:, t, 0:1], rstd[:, t:t + 1],
                                            ALU.subtract, ALU.mult).then_inc(centred, 1)
                v.wait_ge(w_loaded, 64)
                for n in range(4):
                    w = stage[n][:, :, :] if n < 3 else wo[:, :, :]
                    link.note(nc.vector.tensor_reduce(ext[:, n:n + 1], w, mybir.AxisListType.XY, ALU.max))
                    link.note(nc.vector.tensor_reduce(ext[:, 4 + n:5 + n], w, mybir.AxisListType.XY, ALU.min))
                link.wait()
                link(nc.vector.tensor_scalar(ext[:, 4:8], ext[:, 4:8], -1.0, 1e-30, ALU.mult, ALU.max))
                nc.vector.tensor_tensor(ext[:, 0:4], ext[:, 0:4], ext[:, 4:8], ALU.max).then_inc(extremes, 1)
                v.wait_ge(largest, 1)
                link(nc.vector.tensor_scalar(am[:, :].bitcast(U32), am[:, :].bitcast(U32), 0x7F800000, None, ALU.bitwise_and))
                nc.vector.reciprocal(winv[:, :], am[:, :]).then_inc(powers, 1)
                link(nc.vector.tensor_scalar(sc[:, 0:1], am[:, 0:1], am[:, 1:2], 2.0 ** -12, ALU.mult, ALU.mult))
                link(nc.vector.tensor_scalar(sc[:, 1:2], sc[:, 0:1], -1.0, None, ALU.mult))
                link(nc.vector.tensor_scalar(sc[:, 4:5], am[:, 2:3], am[:, 3:4], 2.0 ** -12, ALU.mult, ALU.mult))
                link(nc.vector.reciprocal(sc[:, 5:6], sc[:, 0:1]))
                link(nc.vector.tensor_scalar(sc[:, 2:3], sc[:, 5:6], 2.0, None, ALU.mult))
                link(nc.vector.tensor_scalar(sc[:, 3:4], sc[:, 5:6], MASKED, None, ALU.mult))
                v.wait_ge(powers, 1)
                for n in range(3):
                    v.wait_ge(w_hi, n + 1)
                    link(nc.vector.scalar_tensor_tensor(out=WL[n][:, :, :], in0=stage[n][:, :, :], scalar=winv[:, n:n + 1],
                                                        in1=WH[n][:, :, :], op0=ALU.mult, op1=ALU.subtract))
                for b in range(2 * T // 4):
                    k, t0 = b % KC, b // KC * BANK
                    v.wait_ge(h_hi, b + 1)
                    nc.vector.tensor_tensor(hT_lo[:, k, t0:t0 + BANK], tp[b % 2][:, :], hT_hi[:, k, t0:t0 + BANK],
                                            ALU.subtract).then_inc(h_lo, 1)

            @block.scalar
            def _(s):
                for t in range(T):
                    s.wait_ge(centred, t + 1)
                    nc.scalar.activation(hx[:, t, :], hx[:, t, :], ACT.Relu, scale=H_SCALE).then_inc(rectified, 1)
                s.wait_ge(powers, 1)
                for n in range(3):
                    nc.scalar.activation(WH[n][:, :, :], stage[n][:, :, :], ACT.Copy, scale=winv[:, n:n + 1]).then_inc(w_hi, 1)
                for b in range(2 * T // 4):
                    k, t0 = b % KC, b // KC * BANK
                    s.wait_ge(h_tp, b + 1)
                    nc.scalar.activation(hT_hi[:, k, t0:t0 + BANK], tp[b % 2][:, :], ACT.Copy).then_inc(h_hi, 1)

            @block.tensor
            def _(pe):
                pe.wait_ge(ident_made, 1)
                pe.wait_ge(rectified, T)
                for b in range(2 * T // 4):
                    k, t0 = b % KC, b // KC * 4
                    if b >= 2:
                        pe.wait_ge(h_lo, b - 1)
                    for t in range(4):
                        last = nc.tensor.transpose(tp[b % 2][:, t * P:(t + 1) * P], hx[:, t0 + t, k * P:(k + 1) * P], ident[:, :])
                    last.then_inc(h_tp, 1)


def adjacency(nc, sb, ps, sem, adj, bias_d, at_d, sc, ident, deg):
    loaded = [sem(f"adj_loaded{q}") for q in range(2)]
    (doubled, made, dve, tposed, hi_done, lo_done, out_free) = (
        sem("adj_" + s) for s in ("doubled", "made", "dve", "tposed", "hi", "lo", "out_free"))
    stored = [sem(f"bias_stored{q}") for q in range(2)]
    at_stored = [sem(f"at_stored{q}") for q in range(2)]
    rows = adj.rearrange("(q p c) m -> c q p m", q=2, p=P, c=CH)
    with ExitStack() as c:
        A = [sb(c, f"adj_rows{q}", [P, N]) for q in range(2)]
        W = [sb(c, f"adj_twice{q}", [P, N]) for q in range(2)]
        E = sb(c, "adj_zero", [P, N])
        B = [sb(c, f"adj_bias{q}", [P, BW]) for q in range(2)]
        AT = [sb(c, f"adjT{q}", [P, 2, T, P], F16) for q in range(2)]
        col = sb(c, "col_parts", [P, T, T])
        twice = sb(c, "row_twice", [P, T])
        TP = [ps(c, f"adj_tp{n}", [P, BANK]) for n in range(4)]
        FREE = 2
        block = nc.Block()
        with block:
            @block.sync
            def _(sp):
                def load(i, q):
                    sp.dma_start(A[q][:, :], rows[ds(i, 1), q, :, :].rearrange("a p m -> p (a m)")).then_inc(loaded[q], 16)

                def store(i, q):
                    sp.wait_ge(made, 2 * i + q + 1 + FREE)
                    sp.dma_start(bias_d[ds(2 * i + q, 1), :, :].rearrange("a p m -> p (a m)"), B[q][:, :]).then_inc(stored[q], 16)
                    sp.wait_ge(lo_done, 8 * i + 4 * q + 4 + 4)
                    sp.dma_start(at_d[ds(2 * i + q, 1), :, :].rearrange("a p m -> p (a m)"),
                                 AT[q][:, :, :, :].rearrange("p x m n -> p (x m n)")).then_inc(at_stored[q], 16)

                for q in range(2):
                    load(0, q)
                with sp.Fori(0, CH - 1) as i:
                    for q in range(2):
                        store(i, q)
                        load(i + 1, q)
                for q in range(2):
                    store(CH - 1, q)
                for q in range(2):
                    sp.wait_ge(stored[q], 16 * CH + 16)
                    sp.wait_ge(at_stored[q], 16 * CH + 16)

            @block.tensor
            def _(pe):
                with pe.Fori(0, CH) as i:
                    for q in range(2):
                        pe.wait_ge(loaded[q], 16 * i + 16)
                        rows_q = permuted(A[q][:, :])
                        for b in range(4):
                            pe.wait_ge(lo_done, 8 * i + 4 * q + b + 1)
                            for m in range(4):
                                t = 4 * b + m
                                last = nc.tensor.transpose(TP[b][:, m * P:(m + 1) * P], rows_q[:, t // 2, t % 2 * P:(t % 2 + 1) * P], ident[:, :])
                            last.then_inc(tposed, 1)

            @block.scalar
            def _(s):
                with s.Fori(0, CH) as i:
                    for q in range(2):
                        s.wait_ge(loaded[q], 16 * i + 16)
                        s.wait_ge(made, 2 * i + q + 1)
                        nc.scalar.activation(W[q][:, :], A[q][:, :], ACT.Copy, scale=sc[:, 2:3],
                                             accum_out=twice[:, ds(2 * i + q, 1)]).then_inc(doubled, 1)
                        s.wait_ge(at_stored[q], 16 * i + 16)
                        for b in range(4):
                            s.wait_ge(tposed, 8 * i + 4 * q + b + 1)
                            nc.scalar.activation(AT[q][:, 0, 4 * b:4 * b + 4, :].rearrange("p a b -> p (a b)"), TP[b][:, :], ACT.Copy,
                                                 scale=A_SCALE).then_inc(hi_done, 1)

            @block.vector
            def _(v):
                for q in range(2):
                    nc.vector.memset(B[q][:, N:BW], 0.0).then_inc(made, 1)
                v.wait_ge(made, FREE)
                for q in range(2):
                    nc.vector.memset(B[q][:, N:BW], 0.0).then_inc(stored[q], 16)
                    v.wait_ge(stored[q], 16)
                    nc.vector.memset(B[q][:, N:BW], 0.0).then_inc(at_stored[q], 16)
                    v.wait_ge(at_stored[q], 16)
                nc.vector.memset(B[0][:, N:BW], 0.0).then_inc(lo_done, 4)
                v.wait_ge(lo_done, 4)
                with v.Fori(0, CH) as i:
                    link = Chain(v, dve, i * 14)
                    for q in range(2):
                        v.wait_ge(stored[q], 16 * i + 16)
                        v.wait_ge(loaded[q], 16 * i + 16)
                        link(nc.vector.tensor_scalar(E[:, :], A[q][:, :], 0.0, 0.0, ALU.is_equal, ALU.add,
                                                     accum_out=B[q][:, N + 1:N + 2]))
                        v.wait_ge(doubled, 2 * i + q + 1)
                        link.note(nc.vector.scalar_tensor_tensor(out=B[q][:, 0:N].rearrange("p (c r) -> p c r", c=CH),
                                                                 in0=permuted(E[:, :]), scalar=FAR, in1=permuted(W[q][:, :]),
                                                                 op0=ALU.mult, op1=ALU.add))
                        link(nc.vector.tensor_scalar(B[q][:, N:N + 1], B[q][:, N + 1:N + 2], 0.0, FAR, ALU.is_equal, ALU.mult))
                        for b in range(4):
                            v.wait_ge(hi_done, 8 * i + 4 * q + b + 1)
                            link.note(nc.vector.tensor_reduce(col[:, 4 * b:4 * b + 4, ds(2 * i + q, 1)].rearrange("p m a -> p (m a)"),
                                                              TP[b][:, :].rearrange("p (m n) -> p m n", m=4), X, ALU.add))
                            nc.vector.scalar_tensor_tensor(out=AT[q][:, 1, 4 * b:4 * b + 4, :].rearrange("p a b -> p (a b)"), in0=TP[b][:, :],
                                                           scalar=A_SCALE, in1=AT[q][:, 0, 4 * b:4 * b + 4, :].rearrange("p a b -> p (a b)"),
                                                           op0=ALU.mult, op1=ALU.subtract).then_inc(lo_done, 1)
                        link.wait()
                        nc.vector.tensor_scalar(B[q][:, N:N + 1], B[q][:, N:N + 1], sc[:, 3:4], None, ALU.add).then_inc(made, 1)
                v.wait_ge(lo_done, 4 * T + 4)
                nc.vector.tensor_reduce(deg[:, 1, :], col[:, :, :], X, ALU.add).then_inc(out_free, 1)
                nc.vector.tensor_scalar(deg[:, 0, :], twice[:, :], sc[:, 0:1], 0.5, ALU.mult, ALU.mult).then_inc(out_free, 1)


def attend(nc, sb, ps, sem, wout, bias_d, acc, ident, winv, sc, WH, WL, hT_hi, hT_lo):
    (wo_loaded, wo_hi_s, wo_lo_s, proj, proj_hi, bank_free, scores, logits_read, bias_loaded, maxed, exped, tposed,
     pt_hi, pt_free, av_done, av_free, chain) = (sem("att_" + s) for s in (
        "wo_loaded", "wo_hi", "wo_lo", "proj", "proj_hi", "bank_free", "scores", "logits_read", "bias_loaded", "maxed",
        "exped", "tposed", "pt_hi", "pt_free", "av_done", "av_free", "chain"))
    bias_par = [bias_loaded, sem("att_bias_loaded1")]
    BANKS_FREE, READS_FREE, PT_FREE, AV_FREE = 4, 4, 2, 2
    BATCHES, PER_HEAD = 8, 32
    wo_rows = wout.rearrange("(h k p) d -> h p k d", k=KC, p=P)

    with ExitStack() as c:
        VT = [sb(c, f"qvT_{n}", [P, KC, N], F16) for n in ("hi", "lo")]
        KT = [sb(c, f"kT_{n}", [P, KC, N], F16) for n in ("hi", "lo")]
        VW = [sb(c, f"vw_{n}", [P, T, D], F16) for n in ("hi", "lo")]
        WO = [sb(c, f"wo_{n}", [P, KC, D], F16) for n in ("hi", "lo")]
        wo_st = sb(c, "wo_stage", [P, KC, D])
        B = [sb(c, f"bias{n}", [P, BW]) for n in range(2)]
        E = [sb(c, f"e{n}", [P, N]) for n in range(2)]
        PT = [sb(c, f"pT_{n}", [P, T, P], F16) for n in ("hi", "lo")]
        small = sb(c, "att_small", [P, 2, 8])
        minus = sb(c, "minus", [P, 1])
        L = [ps(c, f"logits{n}", [P, 2 * BANK]) for n in range(2)]
        TP = [ps(c, f"tp{n}", [P, BANK]) for n in range(2)]
        AV = [ps(c, f"av{n}", [P, D]) for n in range(2)]
        bank = [L[b // 2][:, b % 2 * BANK:(b % 2 + 1) * BANK] for b in range(4)]
        kinds = [(2, VT), (1, KT), None, (0, VT)]

        def m0(par): return small[:, par, 0:1]
        def m1(par): return small[:, par, 1:2]
        def nb(par): return small[:, par, 2:3]
        def ssum(par): return small[:, par, 3:4]
        def masked(par): return small[:, par, 4:5]
        def r(par): return small[:, par, 5:6]

        block = nc.Block()
        with block:
            @block.sync
            def _(sp):
                with sp.Fori(0, HEADS) as h:
                    sp.wait_ge(wo_lo_s, h + 1)
                    sp.dma_start(wo_st[:, :, :], wo_rows[ds(h, 1), :, :, :].rearrange("a p k d -> p (a k) d")).then_inc(wo_loaded, 16)
                    with sp.Fori(0, T // 2) as j:
                        for par in range(2):
                            i = 16 * h + 2 * j + par
                            sp.wait_ge(logits_read, 2 * i + 2)
                            sp.dma_start(B[par][:, :], bias_d[ds(2 * j + par, 1), :, :].rearrange("a p m -> p (a m)")).then_inc(bias_par[par], 16)

            @block.tensor
            def _(pe):
                def project(h):
                    for n, kind in enumerate(kinds):
                        with pe.Fori(0, 2) as u:
                            if n == 2:
                                pe.wait_ge(wo_hi_s, h + 1)
                                pe.wait_ge(wo_lo_s, h + 2)
                                pe.wait_ge(bank_free, PER_HEAD * h + 8 + BANKS_FREE)
                            if n == 0:
                                pe.wait_ge(logits_read, 32 * h + READS_FREE)
                            for b in range(4):
                                pe.wait_ge(bank_free, PER_HEAD * h + 8 * n + 4 * u + b + 1)
                                if kind is None:
                                    for m in range(2):
                                        o = bank[b][:, m * D:(m + 1) * D]
                                        for k in range(KC):
                                            for w, x in ((0, 0), (0, 1), (1, 0)):
                                                last = nc.tensor.matmul(o, VT[w][:, k, ds((4 * u + b) * 2 * P + m * P, P)], WO[x][:, k, :],
                                                                        start=(k == 0 and w == x == 0), stop=(k == 1 and w == 1))
                                else:
                                    for m in range(2):
                                        o = bank[b][:, m * ROWS:(m + 1) * ROWS]
                                        for k in range(KC):
                                            for w, x in ((0, 0), (0, 1), (1, 0)):
                                                W = (WH, WL)[w][kind[0]]
                                                hT = (hT_hi, hT_lo)[x]
                                                last = nc.tensor.matmul(o, W[:, k, ds((4 * u + b) * D + m * P, P)], hT[:, k, ds(h * ROWS, ROWS)],
                                                                        start=(k == 0 and w == x == 0), stop=(k == 1 and w == 1))
                                last.then_inc(proj, 1)

                def qk(i, t, half):
                    pe.wait_ge(logits_read, 2 * i + half + READS_FREE - 1)
                    for b in range(2):
                        o = L[half][:, b * BANK:(b + 1) * BANK]
                        c0 = half * 2 * BANK + b * BANK
                        for k in range(KC):
                            for w, x in ((0, 0), (0, 1), (1, 0)):
                                last = nc.tensor.matmul(o, VT[w][:, k, ds(t * P, P)], KT[x][:, k, c0:c0 + BANK],
                                                        start=(k == 0 and w == x == 0), stop=(k == 1 and w == 1))
                    last.then_inc(scores, 1)

                def turn(i, par, q):
                    if q == 0:
                        pe.wait_ge(exped, i + 1)
                    pe.wait_ge(pt_free, 4 * i + q + 1)
                    for m in range(4):
                        last = nc.tensor.transpose(TP[q % 2][:, m * P:(m + 1) * P], E[par][:, (4 * q + m) * P:(4 * q + m + 1) * P], ident[:, :])
                    last.then_inc(tposed, 1)

                def av(i, par, q):
                    pe.wait_ge(pt_free, 4 * i + q + 1 + PT_FREE)
                    if q == 0:
                        pe.wait_ge(av_free, i + 1)
                    for m in range(4 * q, 4 * q + 4):
                        for w, x in ((0, 0), (0, 1), (1, 0)):
                            last = nc.tensor.matmul(AV[par][:, :], PT[w][:, m, :], VW[x][:, m, :],
                                                    start=(m == 0 and w == x == 0), stop=(m == T - 1 and w == 1))
                    if q == 3:
                        last.then_inc(av_done, 1)

                def item(i, t, par, more):
                    if more:
                        qk(i + 1, t + 1, 0)
                    turn(i, par, 0)
                    turn(i, par, 1)
                    if more:
                        qk(i + 1, t + 1, 1)
                    av(i, par, 0)
                    turn(i, par, 2)
                    av(i, par, 1)
                    turn(i, par, 3)
                    av(i, par, 2)
                    av(i, par, 3)

                with pe.Fori(0, HEADS) as h:
                    project(h)
                    pe.wait_ge(bank_free, PER_HEAD * (h + 1) + BANKS_FREE)
                    qk(16 * h, 0, 0)
                    qk(16 * h, 0, 1)
                    with pe.Fori(0, T // 2 - 1) as j:
                        item(16 * h + 2 * j, 2 * j, 0, True)
                        item(16 * h + 2 * j + 1, 2 * j + 1, 1, True)
                    item(16 * h + T - 2, T - 2, 0, True)
                    item(16 * h + T - 1, T - 1, 1, False)

            def evacuated(kind, n, m):
                if kind is None:
                    return [VW[x][:, ds(2 * m, 2), :] for x in range(2)]
                return [kind[1][x][:, :, ds(m * ROWS, ROWS)] for x in range(2)]

            @block.scalar
            def _(s):
                def hi(i, q):
                    s.wait_ge(tposed, 4 * i + q + 1)
                    nc.scalar.activation(PT[0][:, 4 * q:4 * q + 4, :].rearrange("p a b -> p (a b)"), TP[q % 2][:, :], ACT.Copy,
                                         scale=P_SCALE).then_inc(pt_hi, 1)

                def exp(i, par):
                    s.wait_ge(maxed, i + 1)
                    nc.scalar.activation(masked(par), nb(par), ACT.Exp, bias=minus[:, 0:1], scale=1.0)
                    nc.scalar.activation(E[par][:, :], E[par][:, :], ACT.Exp, bias=nb(par), scale=sc[:, 0:1],
                                         accum_out=ssum(par)).then_inc(exped, 1)

                with s.Fori(0, HEADS) as h:
                    s.wait_ge(wo_loaded, 16 * (h + 1))
                    nc.scalar.activation(WO[0][:, :, :], wo_st[:, :, :], ACT.Copy, scale=winv[:, 3:4]).then_inc(wo_hi_s, 1)
                    for n, kind in enumerate(kinds):
                        with s.Fori(0, 2) as u:
                            for b in range(4):
                                s.wait_ge(proj, PER_HEAD * h + 8 * n + 4 * u + b + 1)
                                nc.scalar.activation(evacuated(kind, n, 4 * u + b)[0], bank[b].rearrange("p (a b) -> p a b", a=2), ACT.Copy,
                                                     scale=VW_SCALE if kind is None else 1.0).then_inc(proj_hi, 1)
                    exp(16 * h, 0)
                    with s.Fori(0, T // 2 - 1) as j:
                        for par in range(2):
                            i = 16 * h + 2 * j + par
                            for q in range(4):
                                hi(i, q)
                            exp(i + 1, 1 - par)
                    for q in range(4):
                        hi(16 * h + T - 2, q)
                    exp(16 * h + T - 1, 1)
                    for q in range(4):
                        hi(16 * h + T - 1, q)

            @block.vector
            def _(v):
                nc.vector.memset(minus[:, :], MASKED).then_inc(bank_free, BANKS_FREE)
                nc.vector.memset(small[:, :, :], 0.0).then_inc(wo_lo_s, 1)
                v.wait_ge(wo_lo_s, 1)
                v.wait_ge(bank_free, BANKS_FREE)
                nc.vector.memset(small[:, :, :], 0.0).then_inc(logits_read, READS_FREE)
                v.wait_ge(logits_read, READS_FREE)
                nc.vector.memset(small[:, :, :], 0.0).then_inc(pt_free, PT_FREE)
                v.wait_ge(pt_free, PT_FREE)
                nc.vector.memset(small[:, :, :], 0.0).then_inc(av_free, AV_FREE)
                v.wait_ge(av_free, AV_FREE)

                def peak(i, par, half, link):
                    v.wait_ge(scores, 2 * i + half + 1)
                    if half == 0:
                        v.wait_ge(bias_par[par], 8 * (i - par) + 16)
                    link.note(nc.vector.tensor_copy(small[:, par, 6 + half:7 + half], B[par][:, N + 1 - half:N + 2 - half]))
                    cols = slice(half * 2 * BANK, (half + 1) * 2 * BANK)
                    return nc.vector.tensor_tensor_reduce(
                        E[par][:, cols], L[half][:, :], B[par][:, cols], 1.0, (B[par][:, N:N + 1], m0(par))[half],
                        ALU.add, ALU.max, (m0(par), m1(par))[half])

                def peaks_end(i, par, link):
                    peak(i, par, 1, link).then_inc(logits_read, 1)
                    v.wait_ge(logits_read, 2 * i + 2 + READS_FREE)
                    nc.vector.tensor_scalar(nb(par), m1(par), sc[:, 1:2], None, ALU.mult).then_inc(maxed, 1)

                def lo(i, q):
                    v.wait_ge(pt_hi, 4 * i + q + 1)
                    nc.vector.scalar_tensor_tensor(out=PT[1][:, 4 * q:4 * q + 4, :].rearrange("p a b -> p (a b)"), in0=TP[q % 2][:, :],
                                                   scalar=P_SCALE, in1=PT[0][:, 4 * q:4 * q + 4, :].rearrange("p a b -> p (a b)"),
                                                   op0=ALU.mult, op1=ALU.subtract).then_inc(pt_free, 1)

                def add(i, t, par, link):
                    v.wait_ge(exped, i + 1)
                    link(nc.vector.scalar_tensor_tensor(out=r(par), in0=masked(par), scalar=small[:, par, 6:7], in1=ssum(par),
                                                        op0=ALU.mult, op1=ALU.add))
                    link(nc.vector.reciprocal(r(par), r(par)))
                    link(nc.vector.tensor_scalar(r(par), r(par), sc[:, 4:5], None, ALU.mult))
                    v.wait_ge(av_done, i + 1)
                    nc.vector.scalar_tensor_tensor(out=acc[:, ds(t, 1), :].rearrange("p a d -> p (a d)"), in0=AV[par][:, :], scalar=r(par),
                                                   in1=acc[:, ds(t, 1), :].rearrange("p a d -> p (a d)"),
                                                   op0=ALU.mult, op1=ALU.add).then_inc(av_free, 1)

                def item(i, t, par, more, link):
                    if more:
                        peak(i + 1, 1 - par, 0, link).then_inc(logits_read, 1)
                        v.wait_ge(logits_read, 2 * i + 3 + READS_FREE)
                    lo(i, 0)
                    lo(i, 1)
                    if more:
                        peaks_end(i + 1, 1 - par, link)
                    lo(i, 2)
                    lo(i, 3)
                    add(i, t, par, link)

                with v.Fori(0, HEADS) as h:
                    v.wait_ge(wo_hi_s, h + 1)
                    nc.vector.scalar_tensor_tensor(out=WO[1][:, :, :], in0=wo_st[:, :, :], scalar=winv[:, 3:4], in1=WO[0][:, :, :],
                                                   op0=ALU.mult, op1=ALU.subtract).then_inc(wo_lo_s, 1)
                    for n, kind in enumerate(kinds):
                        with v.Fori(0, 2) as u:
                            for b in range(4):
                                v.wait_ge(proj_hi, PER_HEAD * h + 8 * n + 4 * u + b + 1)
                                to = evacuated(kind, n, 4 * u + b)
                                nc.vector.scalar_tensor_tensor(out=to[1], in0=bank[b].rearrange("p (a b) -> p a b", a=2),
                                                               scalar=VW_SCALE if kind is None else 1.0, in1=to[0],
                                                               op0=ALU.mult, op1=ALU.subtract).then_inc(bank_free, 1)
                    link = Chain(v, chain, h * (5 * T))
                    peak(16 * h, 0, 0, link).then_inc(logits_read, 1)
                    v.wait_ge(logits_read, 32 * h + 1 + READS_FREE)
                    peaks_end(16 * h, 0, link)
                    with v.Fori(0, T // 2 - 1) as j:
                        link = Chain(v, chain, h * (5 * T) + 2 + j * 10)
                        item(16 * h + 2 * j, 2 * j, 0, True, link)
                        item(16 * h + 2 * j + 1, 2 * j + 1, 1, True, link)
                    link = Chain(v, chain, h * (5 * T) + 2 + (T // 2 - 1) * 10)
                    item(16 * h + T - 2, T - 2, 0, True, link)
                    item(16 * h + T - 1, T - 1, 1, False, link)


def prepare(nc, sb, ps, sem, a, deg, scales, ident, ident16, halfp, w1, w2, w3, U, gb):
    loaded, dve, bases, powed, vec_done, spread = (sem("prep_" + s) for s in ("loaded", "dve", "bases", "powed", "vec", "spread"))
    with ExitStack() as c:
        row = sb(c, "gamma_beta_row", [1, 2 * D])
        ones = sb(c, "ones_row", [1, P])
        base = sb(c, "deg_base", [P, 2, T])
        zero = sb(c, "deg_zero", [P, T])
        bc = ps(c, "gamma_beta_ps", [P, 2 * D])
        block = nc.Block()
        with block:
            @block.sync
            def _(sp):
                sp.dma_start(row[:, 0:D], a["L1_gnn_gamma"].rearrange("(a d) -> a d", a=1)).then_inc(loaded, 16)
                sp.dma_start(row[:, D:2 * D], a["L1_gnn_beta"].rearrange("(a d) -> a d", a=1)).then_inc(loaded, 16)
                sp.dma_start(w1[:, :, :], a["L1_gnn_W1"].rearrange("(k p) n -> p k n", p=P)).then_inc(loaded, 16)
                sp.dma_start(w3[:, :, :], a["L1_gnn_W3"].rearrange("(k p) n -> p k n", p=P)).then_inc(loaded, 16)
                sp.dma_start(w2[:, :], a["L1_gnn_W2"]).then_inc(loaded, 16)
                for n in range(3):
                    for s in range(2):
                        sp.dma_start(U[n][:, s, :, :], a[f"L1_gnn_U{n + 1}"][s].rearrange("(k p) d -> p k d", p=P)).then_inc(loaded, 16)
                sp.wait_ge(loaded, 16 * 11)

            @block.vector
            def _(v):
                link = Chain(v, dve)
                link(nc.vector.memset(ones[:, :], 1.0))
                link(nc.vector.tensor_scalar(ident16[:, :], ident[:, :], A_SCALE, None, ALU.mult))
                link(nc.vector.tensor_scalar(scales[:, 0:2, :], deg[:, :, :], 1.0, 1e-12, ALU.add, ALU.max))
                link(nc.vector.reciprocal(scales[:, 0:2, :], scales[:, 0:2, :]))
                link(nc.vector.tensor_scalar(base[:, 0, :], deg[:, 0, :], 1e-8, None, ALU.add))
                link(nc.vector.tensor_scalar(zero[:, :], deg[:, 0, :], 1.0, 0.0, ALU.add, ALU.is_equal))
                nc.vector.scalar_tensor_tensor(out=base[:, 1, :], in0=deg[:, 0, :], scalar=1.0, in1=zero[:, :],
                                               op0=ALU.add, op1=ALU.add).then_inc(bases, 1)
                v.wait_ge(powed, 1)
                link(nc.vector.tensor_scalar(zero[:, :], zero[:, :], -1.0, 1.0, ALU.mult, ALU.add))
                nc.vector.tensor_tensor(scales[:, 3, :], scales[:, 3, :], zero[:, :], ALU.mult).then_inc(vec_done, 1)
                v.wait_ge(spread, 1)
                nc.vector.tensor_copy(gb[:, :, :].rearrange("p a d -> p (a d)"), bc[:, :]).then_inc(vec_done, 1)

            @block.gpsimd
            def _(pl):
                pl.wait_ge(bases, 1)
                for n in range(2):
                    last = nc.gpsimd.tensor_tensor(scales[:, 2 + n, :], base[:, n, :], halfp[:, :], ALU.pow)
                last.then_inc(powed, 1)

            @block.tensor
            def _(pe):
                pe.wait_ge(loaded, 16 * 11)
                pe.wait_ge(dve, 1)
                nc.tensor.matmul(bc[:, :], ones[:, :], row[:, :], start=True, stop=True).then_inc(spread, 1)


def last_weights(nc, sb, ps, sem, a, ident, wT, w, bb):
    loaded, turned, copied, one = (sem("lastw_" + s) for s in ("loaded", "turned", "copied", "one"))
    with ExitStack() as c:
        w0 = sb(c, "l2_w", [P, KC, D])
        row, ones = sb(c, "l2_b_row", [1, D]), sb(c, "l2_ones", [1, P])
        tp, bc = ps(c, "l2_tp", [P, BANK]), ps(c, "l2_bc", [P, D])
        block = nc.Block()
        with block:
            @block.sync
            def _(sp):
                sp.dma_start(w0[:, :, :], a["L2_gnn_W"].rearrange("(k p) n -> p k n", p=P)).then_inc(loaded, 16)
                sp.dma_start(w[:, :, :], a["L3_gnn_weight"].rearrange("(k p) n -> p k n", p=P)).then_inc(loaded, 16)
                sp.dma_start(row[:, :], a["L2_gnn_b"].rearrange("(a d) -> a d", a=1)).then_inc(loaded, 16)
                sp.wait_ge(loaded, 48)

            @block.tensor
            def _(pe):
                pe.wait_ge(loaded, 48)
                pe.wait_ge(one, 1)
                for k in range(KC):
                    for o in range(KC):
                        nc.tensor.transpose(tp[:, k * D + o * P:k * D + (o + 1) * P], w0[:, o, k * P:(k + 1) * P], ident[:, :])
                nc.tensor.matmul(bc[:, :], ones[:, :], row[:, :], start=True, stop=True).then_inc(turned, 1)

            @block.vector
            def _(v):
                nc.vector.memset(ones[:, :], 1.0).then_inc(one, 1)
                v.wait_ge(turned, 1)
                nc.vector.tensor_copy(wT[:, :, :].rearrange("p k d -> p (k d)"), tp[:, :]).then_inc(copied, 1)
                nc.vector.tensor_copy(bb[:, :], bc[:, :]).then_inc(copied, 1)


def normalize(nc, sb, ps, sem, name, src, dst, halfp, scale, gb=None, add=None):
    stats_done, rstd_done, dve, centred, pool = (sem(f"{name}_{s}") for s in ("stats_done", "rstd_done", "dve", "centred", "pool"))
    with ExitStack() as c:
        stats, mv, rstd = sb(c, name + "_stats", [P, T, 6]), sb(c, name + "_mv", [P, T, 2]), sb(c, name + "_rstd", [P, T])
        block = nc.Block()
        with block:
            @block.vector
            def _(v):
                link = Chain(v, dve)
                normalize_stats(nc, v, link, src, stats, mv)
                link(nc.vector.tensor_scalar(rstd[:, :], mv[:, :, 1], LN_EPS, None, ALU.add))
                nc.vector.tensor_copy(stats[:, :, 0], mv[:, :, 0]).then_inc(stats_done, 1)
                v.wait_ge(rstd_done, 1)
                for t in range(T):
                    ins = nc.vector.tensor_scalar(dst[:, t, :], src[:, t, :], mv[:, t, 0:1], rstd[:, t:t + 1], ALU.subtract, ALU.mult)
                    if gb is None:
                        ins.then_inc(centred, 1)
                    else:
                        link(ins)
                        link(nc.vector.tensor_tensor(dst[:, t, :], dst[:, t, :], gb[:, 0, :], ALU.mult))
                        link(nc.vector.tensor_tensor(dst[:, t, :], dst[:, t, :], gb[:, 1, :], ALU.add))
                        nc.vector.tensor_tensor(add[:, t, :], add[:, t, :], dst[:, t, :], ALU.add).then_inc(centred, 1)

            @block.gpsimd
            def _(pl):
                pl.wait_ge(stats_done, 1)
                nc.gpsimd.tensor_tensor(rstd[:, :], rstd[:, :], halfp[:, :], ALU.pow).then_inc(rstd_done, 1)

            @block.scalar
            def _(s):
                if gb is None:
                    for t in range(T):
                        s.wait_ge(centred, t + 1)
                        nc.scalar.activation(dst[:, t, :], dst[:, t, :], ACT.Relu, scale=scale).then_inc(pool, 1)


def split_rows(nc, sb, ps, sem, name, src, parts, scale, row_scale=None):
    scaled, dve, cut = (sem(f"{name}_{s}") for s in ("scaled", "dve", "cut"))
    with ExitStack() as c:
        rest = sb(c, name + "_rest", [P, T, D])
        block = nc.Block()
        with block:
            @block.scalar
            def _(s):
                for t in range(T):
                    nc.scalar.activation(rest[:, t, :], src[:, t, :], ACT.Copy,
                                         scale=scale if row_scale is None else row_scale[:, t:t + 1]).then_inc(scaled, 1)

            @block.vector
            def _(v):
                link = Chain(v, dve)
                for t in range(T):
                    v.wait_ge(scaled, t + 1)
                    for n, part in enumerate(parts):
                        link(nc.vector.tensor_copy(part[:, t, :], rest[:, t, :]))
                        if n < len(parts) - 1:
                            link(nc.vector.tensor_tensor(rest[:, t, :], rest[:, t, :], part[:, t, :], ALU.subtract))


def add_row(nc, sb, ps, sem, name, acc, row):
    added = sem(name + "_added")
    block = nc.Block()
    with block:
        @block.vector
        def _(v):
            for t in range(T):
                nc.vector.tensor_tensor(acc[:, t, :], acc[:, t, :], row[:, :], ALU.add).then_inc(added, 1)


def features(nc, sb, ps, sem, name, src, ident, products, logits):
    tp_s, xt_s, u_s, done, q_s, qc_s = (sem(f"{name}_{s}") for s in ("turned", "xt", "product", "free", "q", "q_copied"))
    with ExitStack() as c:
        xT = [sb(c, f"{name}_xT{n}", [P, D]) for n in range(2)]
        qs = [sb(c, f"{name}_q{n}", [64, P]) for n in range(2)]
        TP = [ps(c, f"{name}_tp{n}", [P, D]) for n in range(2)]
        U = [ps(c, f"{name}_u{n}", [P, D]) for n in range(2)]
        QK = [ps(c, f"{name}_qk{n}", [64, 3 * P]) for n in range(2)]
        block = nc.Block()
        with block:
            @block.tensor
            def _(pe):
                for t in range(T):
                    b = t % 2
                    if t >= 2:
                        pe.wait_ge(done, t - 1)
                    for k in range(KC):
                        last = nc.tensor.transpose(TP[b][:, k * P:(k + 1) * P], src[:, t, k * P:(k + 1) * P], ident[:, :])
                    last.then_inc(tp_s, 1)
                    pe.wait_ge(xt_s, t + 1)
                    for w, _ in products:
                        for k in range(KC):
                            last = nc.tensor.matmul(U[b][:, :], xT[b][:, k * P:(k + 1) * P], w[:, k, :], start=(k == 0), stop=(k == 1))
                    if logits:
                        w1, w2, w3, QT, KT = logits
                        for n, w in ((0, w1), (1, w3)):
                            for k in range(KC):
                                last = nc.tensor.matmul(QK[b][:, n * P:(n + 1) * P], w[:, k, :], xT[b][:, k * P:(k + 1) * P],
                                                        start=(k == 0), stop=(k == 1))
                        last.then_inc(q_s, 1)
                        pe.wait_ge(qc_s, t + 1)
                        last = nc.tensor.matmul(QK[b][:, 2 * P:3 * P], w2[:, :], qs[b][:, :], start=True, stop=True)
                    last.then_inc(u_s, 1)

            @block.scalar
            def _(s):
                for t in range(T):
                    b = t % 2
                    s.wait_ge(tp_s, t + 1)
                    nc.scalar.activation(xT[b][:, :], TP[b][:, :], ACT.Copy).then_inc(xt_s, 1)
                    if logits:
                        s.wait_ge(q_s, t + 1)
                        nc.scalar.activation(qs[b][:, :], QK[b][:, 0:P], ACT.Copy).then_inc(qc_s, 1)

            @block.vector
            def _(v):
                for t in range(T):
                    b = t % 2
                    v.wait_ge(u_s, t + 1)
                    for _, to in products:
                        if to is None:
                            last = nc.vector.tensor_copy(src[:, t, :], U[b][:, :])
                        else:
                            last = nc.vector.tensor_tensor(to[:, t, :], to[:, t, :], U[b][:, :], ALU.add)
                    if logits:
                        cols = slice(t * P, (t + 1) * P)
                        nc.vector.tensor_copy(logits[4][:, cols], QK[b][:, P:2 * P])
                        last = nc.vector.tensor_copy(logits[3][:, cols], QK[b][:, 2 * P:3 * P])
                    last.then_inc(done, 1)


def diffuse(nc, sb, ps, sem, name, at_d, ident, ident16, target, jobs, relu=False):
    at_loaded = [sem(f"{name}_at_loaded{n}") for n in range(2)]
    prod, xs_s, tp_s, xt_s, u_s, u_free, dve = (sem(f"{name}_{s}") for s in (
        "product", "scaled", "turned", "xt", "weighted", "free", "dve"))
    R = sum(len(j[2]) for j in jobs)
    J = len(jobs)
    results = [(n, r) for n, j in enumerate(jobs) for r in j[2]]
    with ExitStack() as c:
        AT = [sb(c, f"{name}_at{n}", [P, 2, T, P], F16) for n in range(2)]
        xs = [sb(c, f"{name}_xs{n}", [P, D]) for n in range(2)]
        rest = sb(c, f"{name}_rest", [P, D])
        xT = [sb(c, f"{name}_xT{n}", [P, D]) for n in range(2)]
        rsc = sb(c, f"{name}_row_scales", [P, 2, T])
        PR = [[ps(c, f"{name}_pr{n}_{m}", [P, D]) for m in range(2)] for n in range(J)]
        TP = [ps(c, f"{name}_tp{n}", [P, D]) for n in range(2)]
        UP = [ps(c, f"{name}_up{n}", [P, D]) for n in range(2)]
        block = nc.Block()
        with block:
            @block.sync
            def _(sp):
                with sp.Fori(0, T // 2) as j:
                    for b in range(2):
                        sp.wait_ge(xs_s, R * (2 * j + b) + R)
                        sp.dma_start(AT[b][:, :, :, :].rearrange("p x m n -> p (x m n)"),
                                     at_d[ds(2 * j + b, 1), :, :].rearrange("a p m -> p (a m)")).then_inc(at_loaded[b], 16)

            @block.tensor
            def _(pe):
                def multiply(t, b, half):
                    for n, (parts, _, _) in enumerate(jobs):
                        pe.wait_ge(at_loaded[b], 16 * (half + 1))
                        pe.wait_ge(xs_s, R * t + sum(len(k[2]) for k in jobs[:n + 1]))
                        wide = len(parts) == 3
                        pairs = ((0, 0), (0, 1), (0, 2), (1, 0), (1, 1)) if wide else ((0, 0), (0, 1), (1, 0))
                        for m in range(T):
                            for x, y in pairs:
                                last = nc.tensor.matmul(PR[n][b][:, :], AT[b][:, x, m, :], parts[y][:, m, :],
                                                        start=(m == 0 and x == y == 0),
                                                        stop=(ident16 is None and m == T - 1 and (x, y) == pairs[-1]))
                        if ident16 is not None:
                            for y, part in enumerate(parts):
                                last = nc.tensor.matmul(PR[n][b][:, :], ident16[:, :], part[:, ds(t, 1), :].rearrange("p a d -> p (a d)"),
                                                        start=False, stop=(y == len(parts) - 1))
                        last.then_inc(prod, 1)

                def weigh(t, b):
                    for r, (_, (_, _, _, w)) in enumerate(results):
                        slot = r if R == 2 else b
                        i = R * t + r
                        if w is None:
                            continue
                        pe.wait_ge(xs_s, i + 1 + 2 * R)
                        pe.wait_ge(u_free, i + 1)
                        for k in range(KC):
                            last = nc.tensor.transpose(TP[slot][:, k * P:(k + 1) * P], xs[slot][:, k * P:(k + 1) * P], ident[:, :])
                        last.then_inc(tp_s, 1)
                    for r, (_, (_, _, _, w)) in enumerate(results):
                        slot = r if R == 2 else b
                        i = R * t + r
                        if w is None:
                            continue
                        pe.wait_ge(xt_s, i + 1)
                        for k in range(KC):
                            last = nc.tensor.matmul(UP[slot][:, :], xT[slot][:, k * P:(k + 1) * P], w[:, k, :], start=(k == 0), stop=(k == 1))
                        last.then_inc(u_s, 1)

                multiply(0, 0, 0)
                with pe.Fori(0, T // 2 - 1) as j:
                    multiply(2 * j + 1, 1, j)
                    weigh(2 * j, 0)
                    multiply(2 * j + 2, 0, j + 1)
                    weigh(2 * j + 1, 1)
                multiply(T - 1, 1, T // 2 - 1)
                weigh(T - 2, 0)
                weigh(T - 1, 1)

            @block.scalar
            def _(s):
                def scale_rows(t, b):
                    for r, (n, (rows, _, _, _)) in enumerate(results):
                        slot = r if R == 2 else b
                        s.wait_ge(prod, J * t + n + 1)
                        s.wait_ge(u_free, R * t + r + 1)
                        nc.scalar.activation(xs[slot][:, :], PR[n][b][:, :], ACT.Relu if relu else ACT.Copy,
                                             scale=rsc[:, r, ds(t, 1)]).then_inc(xs_s, 1)

                def weighted(t, b):
                    for r, (_, (_, _, _, w)) in enumerate(results):
                        slot = r if R == 2 else b
                        if w is None:
                            continue
                        s.wait_ge(tp_s, R * t + r + 1)
                        nc.scalar.activation(xT[slot][:, :], TP[slot][:, :], ACT.Copy).then_inc(xt_s, 1)

                s.wait_ge(u_free, 2)
                scale_rows(0, 0)
                with s.Fori(0, T // 2 - 1) as j:
                    weighted(2 * j, 0)
                    scale_rows(2 * j + 1, 1)
                    weighted(2 * j + 1, 1)
                    scale_rows(2 * j + 2, 0)
                weighted(T - 2, 0)
                scale_rows(T - 1, 1)
                weighted(T - 1, 1)

            @block.vector
            def _(v):
                link = Chain(v, dve)
                for r, (n, (rows, _, to_scale, _)) in enumerate(results):
                    link(nc.vector.tensor_scalar(rsc[:, r, :], rows, to_scale / (jobs[n][1] * A_SCALE), None, ALU.mult))
                link(nc.vector.memset(rest[:, :], 0.0))
                head = link.n
                nc.vector.memset(rest[:, :], 0.0).then_inc(xs_s, 2 * R)
                v.wait_ge(xs_s, 2 * R)
                nc.vector.memset(rest[:, :], 0.0).then_inc(u_free, 2)
                v.wait_ge(u_free, 2)

                def here(x, t):
                    return x[:, ds(t, 1), :].rearrange("p a d -> p (a d)")

                def cut(t, b, link):
                    for r, (_, (_, parts, to_scale, w)) in enumerate(results):
                        slot = r if R == 2 else b
                        v.wait_ge(xs_s, R * t + r + 1 + 2 * R)
                        if parts:
                            link(nc.vector.tensor_copy(here(parts[0], t), xs[slot][:, :]))
                            link(nc.vector.tensor_tensor(rest[:, :], xs[slot][:, :], here(parts[0], t), ALU.subtract))
                            link(nc.vector.tensor_copy(here(parts[1], t), rest[:, :]))
                            if len(parts) == 3:
                                link(nc.vector.tensor_tensor(rest[:, :], rest[:, :], here(parts[1], t), ALU.subtract))
                                link(nc.vector.tensor_copy(here(parts[2], t), rest[:, :]))
                        if w is None:
                            nc.vector.tensor_tensor(here(target, t), here(target, t), xs[slot][:, :], ALU.add).then_inc(u_free, 1)

                def add(t, b, link):
                    for r, (_, (_, _, to_scale, w)) in enumerate(results):
                        slot = r if R == 2 else b
                        i = R * t + r
                        if w is None:
                            continue
                        v.wait_ge(u_s, i + 1)
                        nc.vector.scalar_tensor_tensor(out=here(target, t), in0=UP[slot][:, :], scalar=1.0 / to_scale, in1=here(target, t),
                                                       op0=ALU.mult, op1=ALU.add).then_inc(u_free, 1)
                        v.wait_ge(u_free, i + 3)

                per = sum(0 if not p else 3 if len(p) == 2 else 5 for _, (_, p, _, w) in results)
                link = Chain(v, dve, head)
                cut(0, 0, link)
                with v.Fori(0, T // 2 - 1) as j:
                    link = Chain(v, dve, head + per + 2 * per * j)
                    add(2 * j, 0, link)
                    cut(2 * j + 1, 1, link)
                    add(2 * j + 1, 1, link)
                    cut(2 * j + 2, 0, link)
                    assert link.n == 2 * per
                link = Chain(v, dve, head + per + per * (T - 2))
                add(T - 2, 0, link)
                cut(T - 1, 1, link)
                add(T - 1, 1, link)


def nucleus(nc, sb, ps, sem, name, QT, KT, parts, out, ident):
    (scores, l_free, peaked, exped, masked_s, e_free, tp_s, hi_s, lo_s, prod_s, out_s, chain, q_s, dve0) = (
        sem(f"{name}_{s}") for s in ("scores", "l_free", "peaked", "exped", "masked", "e_free", "turned", "hi", "lo", "product",
                                     "out", "chain", "q", "dve0"))
    GROUPS = T // G
    with ExitStack() as c:
        e = sb(c, name + "_e", [P, 2, G, N])
        junk = sb(c, name + "_junk", [P, N])
        PT = [sb(c, f"{name}_pT{n}", [P, T, P], F16) for n in ("hi", "lo")]
        staging = [sb(c, f"{name}_stage{n}", [P, BANK]) for n in range(2)]
        nmax, Z = sb(c, name + "_nmax", [P, T]), sb(c, name + "_Z", [P, T])
        rs = sb(c, name + "_rs", [P, T])
        S = sb(c, name + "_small", [P, 16, G])
        top, kept = sb(c, name + "_top", [P, G, 8]), sb(c, name + "_kept", [P, G, 8])
        pre = sb(c, name + "_prefix", [P, G, 8])
        one = sb(c, name + "_one", [P, 8])
        und, undT = sb(c, name + "_und", [P, 32]), sb(c, name + "_undT", [P, 32])
        cell = sb(c, name + "_cell", [1, 8])
        flag = sb(c, name + "_flag", [1, 8], I32)
        L = ps(c, name + "_l", [P, N])
        TP = [ps(c, f"{name}_tp{n}", [P, BANK]) for n in range(2)]
        PR = [ps(c, f"{name}_pr{n}", [P, D]) for n in range(2)]
        lo, hi, t_, Gt, b_, target, M, R, tie, tstar, done, x_ = (S[:, k, :] for k in range(12))
        block = nc.Block()
        with block:
            @block.tensor
            def _(pe):
                def logits(g, k):
                    i = G * g + k
                    if i:
                        pe.wait_ge(exped, i)
                    for b in range(4):
                        last = nc.tensor.matmul(L[:, b * BANK:(b + 1) * BANK], QT[:, i * P:(i + 1) * P], KT[:, b * BANK:(b + 1) * BANK],
                                                start=True, stop=True)
                    last.then_inc(scores, 1)

                def multiply(g, k):
                    i = G * g + k
                    pe.wait_ge(masked_s, i + 1)
                    for q in range(4):
                        if 4 * i + q >= 2:
                            pe.wait_ge(lo_s, 4 * i + q - 1)
                        for m in range(4):
                            last = nc.tensor.transpose(TP[q % 2][:, m * P:(m + 1) * P], e[:, g % 2, k, (4 * q + m) * P:(4 * q + m + 1) * P], ident[:, :])
                        last.then_inc(tp_s, 1)
                    if i >= 2:
                        pe.wait_ge(out_s, i - 1)
                    for q in range(4):
                        pe.wait_ge(lo_s, 4 * i + q + 1)
                        for m in range(4 * q, 4 * q + 4):
                            for x, y in ((0, 0), (0, 1), (1, 0)):
                                last = nc.tensor.matmul(PR[k % 2][:, :], PT[x][:, m, :], parts[y][:, m, :],
                                                        start=(m == 0 and x == y == 0), stop=(m == T - 1 and x == 1))
                    last.then_inc(prod_s, 1)

                for k in range(G):
                    logits(0, k)
                for g in range(GROUPS):
                    for k in range(G):
                        if g:
                            multiply(g - 1, k)
                        if g + 1 < GROUPS:
                            logits(g + 1, k)
                for k in range(G):
                    multiply(GROUPS - 1, k)

            @block.scalar
            def _(s):
                def exp(g, k):
                    i = G * g + k
                    s.wait_ge(peaked, i + 1)
                    if g >= 2:
                        s.wait_ge(prod_s, G * (g - 2) + k + 1)
                    nc.scalar.activation(e[:, g % 2, k, :], L[:, :], ACT.Exp, bias=nmax[:, i:i + 1], scale=1.0,
                                         accum_out=Z[:, i:i + 1]).then_inc(exped, 1)

                def halves(g, k):
                    i = G * g + k
                    for q in range(4):
                        s.wait_ge(tp_s, 4 * i + q + 1)
                        nc.scalar.activation(PT[0][:, 4 * q:4 * q + 4, :].rearrange("p a b -> p (a b)"), TP[q % 2][:, :], ACT.Copy,
                                             scale=P_SCALE).then_inc(hi_s, 1)
                        stage = staging[q % 2]
                        if 4 * i + q >= 2:
                            s.wait_ge(lo_s, 4 * i + q - 1)
                        nc.scalar.activation(stage[:, :], TP[q % 2][:, :], ACT.Copy, scale=P_SCALE).then_inc(hi_s, 1)
                    s.wait_ge(prod_s, i + 1)
                    nc.scalar.activation(out[:, i, :], PR[k % 2][:, :], ACT.Copy, scale=rs[:, i:i + 1]).then_inc(out_s, 1)

                for k in range(G):
                    exp(0, k)
                for g in range(GROUPS):
                    for k in range(G):
                        if g:
                            halves(g - 1, k)
                        if g + 1 < GROUPS:
                            exp(g + 1, k)
                for k in range(G):
                    halves(GROUPS - 1, k)

            @block.gpsimd
            def _(pl):
                for i in range(T):
                    for q in range(4):
                        pl.wait_ge(hi_s, 2 * (4 * i + q + 1))
                        nc.gpsimd.tensor_tensor(PT[1][:, 4 * q:4 * q + 4, :].rearrange("p a b -> p (a b)"), staging[q % 2][:, :],
                                                PT[0][:, 4 * q:4 * q + 4, :].rearrange("p a b -> p (a b)"), ALU.subtract).then_inc(lo_s, 1)

            @block.vector
            def _(v):
                left = v.alloc_register(name + "_left")

                def link(ins):
                    v.drain()

                def peak(g, k):
                    i = G * g + k
                    v.wait_ge(scores, i + 1)
                    nc.vector.tensor_reduce(nmax[:, i:i + 1], L[:, :], X, ALU.max).then_inc(dve0, 1)
                    v.wait_ge(dve0, i + 1)
                    nc.vector.tensor_scalar(nmax[:, i:i + 1], nmax[:, i:i + 1], -1.0, None, ALU.mult).then_inc(peaked, 1)

                def mass(g, compare, bound, to, out_row=None):
                    for k in range(G):
                        dst = e[:, g % 2, k, :] if out_row == "e" else junk[:, :]
                        link(nc.vector.scalar_tensor_tensor(out=dst, in0=e[:, g % 2, k, :], scalar=bound[:, k:k + 1],
                                                            in1=e[:, g % 2, k, :], op0=compare, op1=ALU.mult, accum_out=to[:, k:k + 1]))

                def bisect(g):
                    link(nc.vector.tensor_tensor(x_.bitcast(I32), lo.bitcast(I32), hi.bitcast(I32), ALU.add))
                    link(nc.vector.tensor_scalar(t_.bitcast(I32), x_.bitcast(I32), 0.5, None, ALU.mult))
                    mass(g, ALU.is_gt, t_, Gt)
                    link(nc.vector.tensor_tensor(b_, Gt, target, ALU.is_ge))
                    link(nc.vector.tensor_tensor(x_, b_, t_, ALU.mult))
                    link(nc.vector.tensor_tensor(lo, lo, x_, ALU.max))
                    link(nc.vector.scalar_tensor_tensor(out=x_, in0=b_, scalar=4.0, in1=t_, op0=ALU.mult, op1=ALU.add))
                    link(nc.vector.tensor_tensor(hi, hi, x_, ALU.min))

                def look(g):
                    for k in range(G):
                        link(nc.vector.scalar_tensor_tensor(out=junk[:, :], in0=e[:, g % 2, k, :], scalar=hi[:, k:k + 1],
                                                            in1=e[:, g % 2, k, :], op0=ALU.is_le, op1=ALU.mult, accum_out=M[:, k:k + 1]))
                        link(nc.vector.max(top[:, k, :], junk[:, :]))
                        link(nc.vector.tensor_tensor_scan(pre[:, k, :], top[:, k, :], one[:, :], 0.0, ALU.add, ALU.mult))
                    link(nc.vector.tensor_tensor(R, target, Z[:, G * g:G * g + G], ALU.subtract))
                    link(nc.vector.tensor_tensor(R, R, M, ALU.add))
                    link(nc.vector.tensor_copy(kept[:, :, 0], top[:, :, 0]))
                    for k in range(G):
                        link(nc.vector.tensor_scalar(kept[:, k, 1:8], pre[:, k, 0:7], R[:, k:k + 1], 4.0, ALU.is_ge, ALU.mult))
                    link(nc.vector.tensor_tensor(kept[:, :, 1:8], kept[:, :, 1:8], top[:, :, 1:8], ALU.add))
                    link(nc.vector.tensor_reduce(tstar, kept[:, :, :], X, ALU.min))
                    link(nc.vector.tensor_tensor(done, pre[:, :, 7], R, ALU.is_ge))
                    link(nc.vector.tensor_tensor(done, done, tie, ALU.max))
                    link(nc.vector.tensor_reduce(und[:, 0:1], done, X, ALU.min))
                    link(nc.vector.tensor_scalar(und[:, 0:1], und[:, 0:1], -1.0, 1.0, ALU.mult, ALU.add))
                    link(nc.vector.transpose(undT[:, :], und[:, :]))
                    link(nc.vector.tensor_reduce(und[:, 0:1], undT[:, :], X, ALU.max))
                    for q in range(4):
                        link(nc.vector.tensor_copy(cell[0:1, q:q + 1], und[32 * q:32 * q + 1, 0:1]))
                    link(nc.vector.tensor_reduce(cell[0:1, 4:5], cell[0:1, 0:4], X, ALU.max))
                    link(nc.vector.tensor_copy(flag[0:1, 0:1], cell[0:1, 4:5]))

                def search(g):
                    v.wait_ge(exped, G * g + G)
                    link(nc.vector.tensor_scalar(target, Z[:, G * g:G * g + G], P_NUC, None, ALU.mult))
                    link(nc.vector.tensor_scalar(lo, Z[:, G * g:G * g + G], (1 - P_NUC) * 0.999 / N, None, ALU.mult))
                    link(nc.vector.memset(hi, 1.001))
                    link(nc.vector.memset(tie, 0.0))
                    for k in range(G):
                        bisect(g)
                        if k >= 0 and g + 1 < GROUPS:
                            peak(g + 1, k)
                    with v.Fori(G, BISECTIONS):
                        bisect(g)
                    look(g)
                    v.reg_load(left, flag[0:1, 0:1])
                    with v.While(lambda: v.snap(left) > 0):
                        v_8 = top[:, :, 7]
                        link(nc.vector.tensor_copy(x_, v_8))
                        mass(g, ALU.is_ge, x_, Gt)
                        link(nc.vector.tensor_tensor(b_, Gt, target, ALU.is_ge))
                        link(nc.vector.tensor_tensor(tie, tie, b_, ALU.max))
                        link(nc.vector.tensor_scalar(x_, x_, 1.0 - 2.0 ** -23, None, ALU.mult))
                        link(nc.vector.scalar_tensor_tensor(out=x_, in0=b_, scalar=4.0, in1=x_, op0=ALU.mult, op1=ALU.add))
                        link(nc.vector.tensor_tensor(hi, hi, x_, ALU.min))
                        bisect(g)
                        look(g)
                        v.reg_load(left, flag[0:1, 0:1])
                    for k in range(G):
                        i = G * g + k
                        link(nc.vector.scalar_tensor_tensor(out=e[:, g % 2, k, :], in0=e[:, g % 2, k, :], scalar=tstar[:, k:k + 1],
                                                            in1=e[:, g % 2, k, :], op0=ALU.is_ge, op1=ALU.mult, accum_out=rs[:, i:i + 1]))
                    link(nc.vector.reciprocal(rs[:, G * g:G * g + G], rs[:, G * g:G * g + G]))
                    nc.vector.tensor_scalar(rs[:, G * g:G * g + G], rs[:, G * g:G * g + G], 1.0 / (P_SCALE * X_SCALE), None,
                                            ALU.mult).then_inc(masked_s, G)
                    v.wait_ge(masked_s, G * g + G)

                link(nc.vector.memset(one[:, :], 1.0))
                link(nc.vector.memset(und[:, :], 0.0))
                for k in range(G):
                    peak(0, k)
                for g in range(GROUPS):
                    search(g)


def finish(nc, sb, ps, sem, acc, out):
    stored = sem("out_stored")
    block = nc.Block()
    with block:
        @block.sync
        def _(sp):
            for q in range(2):
                sp.dma_start(nodes(out)[:, :, q, :], acc[:, :, :].rearrange("p (c q) d -> p c q d", q=2)[:, :, q, :]).then_inc(stored, 16)
            sp.wait_ge(stored, 32)


_INS = ["x", "adj", "L0_gnn_Wq", "L0_gnn_Wk", "L0_gnn_Wv", "L0_gnn_Wout", "L1_gnn_W1", "L1_gnn_W2", "L1_gnn_W3", "L1_gnn_U1",
        "L1_gnn_U2", "L1_gnn_U3", "L1_gnn_gamma", "L1_gnn_beta", "L2_gnn_W", "L2_gnn_b", "L3_gnn_weight"]


def kernel(**inputs):
    import numpy as _np
    import concourse.bacc as _bacc
    from concourse import mybir as _mybir
    from concourse.bass_utils import run_bass_kernel_spmd as _run

    nc = _bacc.Bacc("TRN2", target_bir_lowering=False, num_devices=1)
    arrays, args = {}, {}
    for name in _INS:
        a = _np.ascontiguousarray(inputs[name])
        arrays[f"in_{name}_dram"] = a
        args[name] = nc.dram_tensor(f"in_{name}_dram", a.shape, _mybir.dt.from_np(a.dtype), kind="ExternalInput").ap()
    out = nc.dram_tensor("out_0_dram", (N, D), F32, kind="ExternalOutput").ap()
    build(nc, args, out)
    r = _run(nc, [arrays], core_ids=[0])
    return r.results[0]["out_0_dram"]
```

```python
from contextlib import ExitStack

import concourse.bass as bass
from concourse import mybir

F32 = mybir.dt.float32
F16 = mybir.dt.float16
BF16 = mybir.dt.bfloat16
I32 = mybir.dt.int32
U32 = mybir.dt.uint32
ALU = mybir.AluOpType
ACT = mybir.ActivationFunctionType
X = mybir.AxisListType.X
ABSMAX = bass.bass_isa.ReduceOp.absmax
ds = bass.ds

P = 128
N, D, HEADS = 2048, 256, 8
T = N // P
KC = D // P
CH = N // (N // HEADS)
ROWS = N // HEADS
BANK = 512
MASKED = -1.0e6
FAR = -1.0e30
H_SCALE = 16.0
P_SCALE = 32768.0
VW_SCALE = 2.0 ** -7
LN_EPS = 1e-5
A_SCALE = 64.0
X_SCALE = 1024.0
P_NUC = 0.9
G = 4
CUTS = "bbiibiib"
CLIP = 0.25
BW = N + 8


class Chain:

    def __init__(self, engine, sem, base=0):
        self.engine, self.sem, self.base, self.n = engine, sem, base, 0

    def __call__(self, ins):
        self.note(ins)
        self.wait()

    def wait(self):
        self.engine.wait_ge(self.sem, self.base + self.n)

    def note(self, ins):
        self.n += 1
        ins.then_inc(self.sem, 1)


def nodes(ap):
    return ap.rearrange("(q p c) d -> p c q d", q=2, p=P, c=CH)


def permuted(ap):
    return ap.rearrange("p (r c) -> p c r", c=CH)


def normalize_stats(nc, eng, chain, x, stats, mv):
    for t in range(T):
        chain.note(nc.vector.bn_stats(stats[:, t, :], x[:, t, :]))
    chain.wait()
    for t in range(T):
        chain.note(nc.vector.bn_aggr(mv[:, t, :], stats[:, t, :]))
    chain.wait()


def build(nc, a, out):
    g = ExitStack()

    def sb(stack, name, shape, dt=F32):
        return stack.enter_context(nc.sbuf_tensor(name, shape, dt))

    def ps(stack, name, shape, dt=F32):
        return stack.enter_context(nc.psum_tensor(name, shape, dt))

    with g:
        def phase(run, *args, **kwargs):
            own = []

            def sem(name):
                own.append(nc.alloc_semaphore(name))
                return own[-1]

            run(nc, sb, ps, sem, *args, **kwargs)
            nc.clear_and_free_semaphores(own)
            nc.all_engine_barrier()

        bias_d = nc.dram_tensor("bias_scratch", (T, P, BW), F32, kind="Internal").ap()
        at_d = nc.dram_tensor("adjT_scratch", (T, P, 2 * N), F16, kind="Internal").ap()

        x_d = nc.dram_tensor("x_scratch", (P, T, D), F32, kind="Internal").ap()

        acc = sb(g, "acc", [P, T, D])
        ident = sb(g, "ident", [P, P])
        am = sb(g, "am", [P, 4])
        winv = sb(g, "winv", [P, 4])
        sc = sb(g, "sc", [P, 8])
        halfp = sb(g, "halfp", [P, T])
        deg = sb(g, "deg", [P, 2, T])

        with ExitStack() as c:
            WH = [sb(c, f"w{n}_hi", [P, KC, N], F16) for n in "qkv"]
            WL = [sb(c, f"w{n}_lo", [P, KC, N], F16) for n in "qkv"]
            hT_hi = sb(c, "hT_hi", [P, KC, N], F16)
            hT_lo = sb(c, "hT_lo", [P, KC, N], F16)
            phase(setup, a, bias_d, acc, ident, am, winv, sc, halfp, WH, WL, hT_hi, hT_lo)
            phase(adjacency, a["adj"], bias_d, at_d, sc, ident, deg)
            phase(attend, a["L0_gnn_Wout"], bias_d, acc, ident, winv, sc, WH, WL, hT_hi, hT_lo)

        scales = sb(g, "scales", [P, 4, T])
        ident16 = sb(g, "ident16", [P, P], BF16)
        with ExitStack() as c:
            w1, w3 = sb(c, "w1", [P, KC, 64]), sb(c, "w3", [P, KC, 64])
            w2 = sb(c, "w2", [64, 64])
            gb = sb(c, "gamma_beta", [P, 2, D])
            Y = sb(c, "y", [P, T, D])
            XA = acc
            phase(prepare, a, deg, scales, ident, ident16, halfp, w1, w2, w3, gb, sc, acc, x_d)
            phase(normalize, "l1", acc, Y, halfp, 1.0)
            with ExitStack() as c1:
                Xp = [sb(c1, f"x_{n}", [P, T, D], F16) for n in ("hi", "lo")]
                Xf = [sb(c1, f"xf_{n}", [P, T, D], F16) for n in ("hi", "lo")]
                Xb = [sb(c1, f"xb_{n}", [P, T, D], F16) for n in ("hi", "lo")]
                QT, KT = sb(c1, "logit_q", [64, N]), sb(c1, "logit_k", [64, N])
                for step in range(2):
                    X_ = (Y, XA)[step]
                    phase(split_rows, f"xa{step}", X_, Xp, X_SCALE)
                    phase(features, f"qk{step}", X_, ident, [], (w1, w2, w3, QT, KT))
                    phase(nucleus, f"nuc{step}", QT, KT, Xp, XA, ident,
                          (a["L1_gnn_U1"][step], a["L1_gnn_U2"][step], at_d, scales, ident16, Y, sc, Xp, Xf, Xb, step))
                    phase(features, f"u3{step}", XA, ident, [(a["L1_gnn_U3"][step], Y)], None)
            phase(normalize, "l1out", Y, Y, halfp, None, gb, acc, x_d)
        with ExitStack() as c:
            H = sb(c, "h", [P, T, D])
            Hp = [sb(c, f"h_{n}", [P, T, D], BF16) for n in range(3)]
            wT = sb(c, "l2_wT", [P, KC, D])
            bb = sb(c, "l2_bias", [P, D])
            phase(last_weights, a, ident, wT, bb)
            phase(normalize, "l2", acc, H, halfp, 1.0)
            phase(split_rows, "l2h", H, Hp, 1.0, scales[:, 2, :])
            phase(diffuse, "l2d", at_d, ident, None, acc, [
                (Hp, 1.0, [(scales[:, 2, :], None, 1.0, wT[:, :, :])])])
            phase(add_row, "l2b", acc, bb)
            phase(normalize, "l3", acc, H, halfp, 1.0)
            phase(features, "l3w", H, ident, [(a["L3_gnn_weight"], None)], None)
            phase(split_rows, "l3h", H, Hp, 1.0, scales[:, 3, :])
            phase(diffuse, "l3d", at_d, ident, ident16, acc, [
                (Hp, 1.0, [(scales[:, 3, :], None, 1.0, None)])], relu=True)
        phase(finish, acc, out)


def setup(nc, sb, ps, sem, a, bias_d, acc, ident, am, winv, sc, halfp, WH, WL, hT_hi, hT_lo):
    w_loaded, x_loaded, rest_loaded = sem("w_loaded"), sem("x_loaded"), sem("rest_loaded")
    dve, pool = sem("setup_dve"), sem("setup_pool")
    extremes, largest, powers, w_hi, stats_done = sem("extremes"), sem("largest"), sem("powers"), sem("w_hi"), sem("stats_done")
    rstd_done, centred, rectified, h_tp, h_hi, h_lo = (sem(s) for s in ("rstd_done", "centred", "rectified", "h_tp", "h_hi", "h_lo"))
    ident_made = sem("ident_made")
    with ExitStack() as c:
        stage = [sb(c, f"w_stage{n}", [P, KC, N]) for n in range(3)]
        hx = sb(c, "hx", [P, T, D])
        stats, mv = sb(c, "stats", [P, T, 6]), sb(c, "mv", [P, T, 2])
        rstd = sb(c, "rstd", [P, T])
        ext = sb(c, "ext", [P, 8])
        wo = acc
        tp = [ps(c, f"h_tp{n}", [P, BANK]) for n in range(2)]

        block = nc.Block()
        with block:
            @block.sync
            def _(sp):
                sp.dma_start(hx[:, :, :], a["x"].rearrange("(t p) d -> p t d", p=P)).then_inc(x_loaded, 16)
                for n, w in enumerate(("Wq", "Wk", "Wv")):
                    sp.dma_start(stage[n][:, :, :], a["L0_gnn_" + w].rearrange("(k p) n -> p k n", p=P)).then_inc(w_loaded, 16)
                sp.dma_start(wo[:, :, :], a["L0_gnn_Wout"].rearrange("(t p) d -> p t d", p=P)).then_inc(w_loaded, 16)
                sp.wait_ge(extremes, 1)
                for q in range(2):
                    sp.dma_start(acc[:, :, :].rearrange("p (c q) d -> p c q d", q=2)[:, :, q, :],
                                 nodes(a["x"])[:, :, q, :]).then_inc(rest_loaded, 16)
                sp.wait_ge(rest_loaded, 32)

            @block.gpsimd
            def _(pl):
                nc.gpsimd.memset(ident[:, :], 0.0).then_inc(pool, 1)
                pl.wait_ge(pool, 1)
                nc.gpsimd.affine_select(out=ident[:, :], in_=ident[:, :], compare_op=ALU.not_equal, fill=1.0, base=0,
                                        pattern=[[-1, P]], channel_multiplier=1).then_inc(ident_made, 1)
                nc.gpsimd.memset(halfp[:, :], -0.5).then_inc(pool, 1)
                pl.wait_ge(stats_done, 1)
                nc.gpsimd.tensor_scalar(rstd[:, :], mv[:, :, 1], LN_EPS, None, ALU.add).then_inc(pool, 1)
                pl.wait_ge(pool, 3)
                nc.gpsimd.tensor_tensor(rstd[:, :], rstd[:, :], halfp[:, :], ALU.pow).then_inc(rstd_done, 1)
                pl.wait_ge(extremes, 1)
                nc.gpsimd.partition_all_reduce(am[:, :], ext[:, 0:4], P, ABSMAX).then_inc(largest, 1)

            @block.vector
            def _(v):
                link = Chain(v, dve)
                v.wait_ge(x_loaded, 16)
                normalize_stats(nc, v, link, hx, stats, mv)
                nc.vector.memset(ext[:, :], 0.0).then_inc(stats_done, 1)
                v.wait_ge(rstd_done, 1)
                v.wait_ge(stats_done, 1)
                for t in range(T):
                    nc.vector.tensor_scalar(hx[:, t, :], hx[:, t, :], mv[:, t, 0:1], rstd[:, t:t + 1],
                                            ALU.subtract, ALU.mult).then_inc(centred, 1)
                v.wait_ge(w_loaded, 64)
                for n in range(4):
                    w = stage[n][:, :, :] if n < 3 else wo[:, :, :]
                    link.note(nc.vector.tensor_reduce(ext[:, n:n + 1], w, mybir.AxisListType.XY, ALU.max))
                    link.note(nc.vector.tensor_reduce(ext[:, 4 + n:5 + n], w, mybir.AxisListType.XY, ALU.min))
                link.wait()
                link(nc.vector.tensor_scalar(ext[:, 4:8], ext[:, 4:8], -1.0, 1e-30, ALU.mult, ALU.max))
                nc.vector.tensor_tensor(ext[:, 0:4], ext[:, 0:4], ext[:, 4:8], ALU.max).then_inc(extremes, 1)
                v.wait_ge(largest, 1)
                link(nc.vector.tensor_scalar(am[:, :].bitcast(U32), am[:, :].bitcast(U32), 0x7F800000, None, ALU.bitwise_and))
                nc.vector.reciprocal(winv[:, :], am[:, :]).then_inc(powers, 1)
                link(nc.vector.tensor_scalar(sc[:, 0:1], am[:, 0:1], am[:, 1:2], 2.0 ** -12, ALU.mult, ALU.mult))
                link(nc.vector.tensor_scalar(sc[:, 1:2], sc[:, 0:1], -1.0, None, ALU.mult))
                link(nc.vector.tensor_scalar(sc[:, 4:5], am[:, 2:3], am[:, 3:4], 2.0 ** -12, ALU.mult, ALU.mult))
                link(nc.vector.reciprocal(sc[:, 5:6], sc[:, 0:1]))
                link(nc.vector.tensor_scalar(sc[:, 2:3], sc[:, 5:6], 2.0, None, ALU.mult))
                link(nc.vector.tensor_scalar(sc[:, 3:4], sc[:, 5:6], MASKED, None, ALU.mult))
                v.wait_ge(powers, 1)
                for n in range(3):
                    v.wait_ge(w_hi, n + 1)
                    link(nc.vector.scalar_tensor_tensor(out=WL[n][:, :, :], in0=stage[n][:, :, :], scalar=winv[:, n:n + 1],
                                                        in1=WH[n][:, :, :], op0=ALU.mult, op1=ALU.subtract))
                for b in range(2 * T // 4):
                    k, t0 = b % KC, b // KC * BANK
                    v.wait_ge(h_hi, b + 1)
                    nc.vector.tensor_tensor(hT_lo[:, k, t0:t0 + BANK], tp[b % 2][:, :], hT_hi[:, k, t0:t0 + BANK],
                                            ALU.subtract).then_inc(h_lo, 1)

            @block.scalar
            def _(s):
                for t in range(T):
                    s.wait_ge(centred, t + 1)
                    nc.scalar.activation(hx[:, t, :], hx[:, t, :], ACT.Relu, scale=H_SCALE).then_inc(rectified, 1)
                s.wait_ge(powers, 1)
                for n in range(3):
                    nc.scalar.activation(WH[n][:, :, :], stage[n][:, :, :], ACT.Copy, scale=winv[:, n:n + 1]).then_inc(w_hi, 1)
                for b in range(2 * T // 4):
                    k, t0 = b % KC, b // KC * BANK
                    s.wait_ge(h_tp, b + 1)
                    nc.scalar.activation(hT_hi[:, k, t0:t0 + BANK], tp[b % 2][:, :], ACT.Copy).then_inc(h_hi, 1)

            @block.tensor
            def _(pe):
                pe.wait_ge(ident_made, 1)
                pe.wait_ge(rectified, T)
                for b in range(2 * T // 4):
                    k, t0 = b % KC, b // KC * 4
                    if b >= 2:
                        pe.wait_ge(h_lo, b - 1)
                    for t in range(4):
                        last = nc.tensor.transpose(tp[b % 2][:, t * P:(t + 1) * P], hx[:, t0 + t, k * P:(k + 1) * P], ident[:, :])
                    last.then_inc(h_tp, 1)


def adjacency(nc, sb, ps, sem, adj, bias_d, at_d, sc, ident, deg):
    loaded = [sem(f"adj_loaded{q}") for q in range(2)]
    (doubled, made, dve, tposed, hi_done, lo_done, out_free) = (
        sem("adj_" + s) for s in ("doubled", "made", "dve", "tposed", "hi", "lo", "out_free"))
    stored = [sem(f"bias_stored{q}") for q in range(2)]
    at_stored = [sem(f"at_stored{q}") for q in range(2)]
    rows = adj.rearrange("(q p c) m -> c q p m", q=2, p=P, c=CH)
    with ExitStack() as c:
        A = [sb(c, f"adj_rows{q}", [P, N]) for q in range(2)]
        W = [sb(c, f"adj_twice{q}", [P, N]) for q in range(2)]
        E = sb(c, "adj_zero", [P, N])
        B = [sb(c, f"adj_bias{q}", [P, BW]) for q in range(2)]
        AT = [sb(c, f"adjT{q}", [P, 2, T, P], F16) for q in range(2)]
        col = sb(c, "col_parts", [P, T, T])
        twice = sb(c, "row_twice", [P, T])
        TP = [ps(c, f"adj_tp{n}", [P, BANK]) for n in range(4)]
        FREE = 2
        block = nc.Block()
        with block:
            @block.sync
            def _(sp):
                def load(i, q):
                    sp.dma_start(A[q][:, :], rows[ds(i, 1), q, :, :].rearrange("a p m -> p (a m)")).then_inc(loaded[q], 16)

                def store(i, q):
                    sp.wait_ge(made, 2 * i + q + 1 + FREE)
                    sp.dma_start(bias_d[ds(2 * i + q, 1), :, :].rearrange("a p m -> p (a m)"), B[q][:, :]).then_inc(stored[q], 16)
                    sp.wait_ge(lo_done, 8 * i + 4 * q + 4 + 4)
                    sp.dma_start(at_d[ds(2 * i + q, 1), :, :].rearrange("a p m -> p (a m)"),
                                 AT[q][:, :, :, :].rearrange("p x m n -> p (x m n)")).then_inc(at_stored[q], 16)

                for q in range(2):
                    load(0, q)
                with sp.Fori(0, CH - 1) as i:
                    for q in range(2):
                        store(i, q)
                        load(i + 1, q)
                for q in range(2):
                    store(CH - 1, q)
                for q in range(2):
                    sp.wait_ge(stored[q], 16 * CH + 16)
                    sp.wait_ge(at_stored[q], 16 * CH + 16)

            @block.tensor
            def _(pe):
                with pe.Fori(0, CH) as i:
                    for q in range(2):
                        pe.wait_ge(loaded[q], 16 * i + 16)
                        rows_q = permuted(A[q][:, :])
                        for b in range(4):
                            pe.wait_ge(lo_done, 8 * i + 4 * q + b + 1)
                            for m in range(4):
                                t = 4 * b + m
                                last = nc.tensor.transpose(TP[b][:, m * P:(m + 1) * P], rows_q[:, t // 2, t % 2 * P:(t % 2 + 1) * P], ident[:, :])
                            last.then_inc(tposed, 1)

            @block.scalar
            def _(s):
                with s.Fori(0, CH) as i:
                    for q in range(2):
                        s.wait_ge(loaded[q], 16 * i + 16)
                        s.wait_ge(made, 2 * i + q + 1)
                        nc.scalar.activation(W[q][:, :], A[q][:, :], ACT.Copy, scale=sc[:, 2:3],
                                             accum_out=twice[:, ds(2 * i + q, 1)]).then_inc(doubled, 1)
                        s.wait_ge(at_stored[q], 16 * i + 16)
                        for b in range(4):
                            s.wait_ge(tposed, 8 * i + 4 * q + b + 1)
                            nc.scalar.activation(AT[q][:, 0, 4 * b:4 * b + 4, :].rearrange("p a b -> p (a b)"), TP[b][:, :], ACT.Copy,
                                                 scale=A_SCALE).then_inc(hi_done, 1)

            @block.vector
            def _(v):
                for q in range(2):
                    nc.vector.memset(B[q][:, N:BW], 0.0).then_inc(made, 1)
                v.wait_ge(made, FREE)
                for q in range(2):
                    nc.vector.memset(B[q][:, N:BW], 0.0).then_inc(stored[q], 16)
                    v.wait_ge(stored[q], 16)
                    nc.vector.memset(B[q][:, N:BW], 0.0).then_inc(at_stored[q], 16)
                    v.wait_ge(at_stored[q], 16)
                nc.vector.memset(B[0][:, N:BW], 0.0).then_inc(lo_done, 4)
                v.wait_ge(lo_done, 4)
                with v.Fori(0, CH) as i:
                    link = Chain(v, dve, i * 14)
                    for q in range(2):
                        v.wait_ge(stored[q], 16 * i + 16)
                        v.wait_ge(loaded[q], 16 * i + 16)
                        link(nc.vector.tensor_scalar(E[:, :], A[q][:, :], 0.0, 0.0, ALU.is_equal, ALU.add,
                                                     accum_out=B[q][:, N + 1:N + 2]))
                        v.wait_ge(doubled, 2 * i + q + 1)
                        link.note(nc.vector.scalar_tensor_tensor(out=B[q][:, 0:N].rearrange("p (c r) -> p c r", c=CH),
                                                                 in0=permuted(E[:, :]), scalar=FAR, in1=permuted(W[q][:, :]),
                                                                 op0=ALU.mult, op1=ALU.add))
                        link(nc.vector.tensor_scalar(B[q][:, N:N + 1], B[q][:, N + 1:N + 2], 0.0, FAR, ALU.is_equal, ALU.mult))
                        for b in range(4):
                            v.wait_ge(hi_done, 8 * i + 4 * q + b + 1)
                            link.note(nc.vector.tensor_reduce(col[:, 4 * b:4 * b + 4, ds(2 * i + q, 1)].rearrange("p m a -> p (m a)"),
                                                              TP[b][:, :].rearrange("p (m n) -> p m n", m=4), X, ALU.add))
                            nc.vector.scalar_tensor_tensor(out=AT[q][:, 1, 4 * b:4 * b + 4, :].rearrange("p a b -> p (a b)"), in0=TP[b][:, :],
                                                           scalar=A_SCALE, in1=AT[q][:, 0, 4 * b:4 * b + 4, :].rearrange("p a b -> p (a b)"),
                                                           op0=ALU.mult, op1=ALU.subtract).then_inc(lo_done, 1)
                        link.wait()
                        nc.vector.tensor_scalar(B[q][:, N:N + 1], B[q][:, N:N + 1], sc[:, 3:4], None, ALU.add).then_inc(made, 1)
                v.wait_ge(lo_done, 4 * T + 4)
                nc.vector.tensor_reduce(deg[:, 1, :], col[:, :, :], X, ALU.add).then_inc(out_free, 1)
                nc.vector.tensor_scalar(deg[:, 0, :], twice[:, :], sc[:, 0:1], 0.5, ALU.mult, ALU.mult).then_inc(out_free, 1)


def attend(nc, sb, ps, sem, wout, bias_d, acc, ident, winv, sc, WH, WL, hT_hi, hT_lo):
    (wo_loaded, wo_hi_s, wo_lo_s, proj, proj_hi, bank_free, scores, logits_read, bias_loaded, maxed, exped, tposed,
     pt_hi, pt_free, av_done, av_free, chain) = (sem("att_" + s) for s in (
        "wo_loaded", "wo_hi", "wo_lo", "proj", "proj_hi", "bank_free", "scores", "logits_read", "bias_loaded", "maxed",
        "exped", "tposed", "pt_hi", "pt_free", "av_done", "av_free", "chain"))
    bias_par = [bias_loaded, sem("att_bias_loaded1")]
    BANKS_FREE, READS_FREE, PT_FREE, AV_FREE = 4, 4, 2, 2
    BATCHES, PER_HEAD = 8, 32
    wo_rows = wout.rearrange("(h k p) d -> h p k d", k=KC, p=P)

    with ExitStack() as c:
        VT = [sb(c, f"qvT_{n}", [P, KC, N], F16) for n in ("hi", "lo")]
        KT = [sb(c, f"kT_{n}", [P, KC, N], F16) for n in ("hi", "lo")]
        VW = [sb(c, f"vw_{n}", [P, T, D], F16) for n in ("hi", "lo")]
        WO = [sb(c, f"wo_{n}", [P, KC, D], F16) for n in ("hi", "lo")]
        wo_st = sb(c, "wo_stage", [P, KC, D])
        B = [sb(c, f"bias{n}", [P, BW]) for n in range(2)]
        E = [sb(c, f"e{n}", [P, N]) for n in range(2)]
        PT = [sb(c, f"pT_{n}", [P, T, P], F16) for n in ("hi", "lo")]
        small = sb(c, "att_small", [P, 2, 8])
        minus = sb(c, "minus", [P, 1])
        L = [ps(c, f"logits{n}", [P, 2 * BANK]) for n in range(2)]
        TP = [ps(c, f"tp{n}", [P, BANK]) for n in range(2)]
        AV = [ps(c, f"av{n}", [P, D]) for n in range(2)]
        bank = [L[b // 2][:, b % 2 * BANK:(b % 2 + 1) * BANK] for b in range(4)]
        kinds = [(2, VT), (1, KT), None, (0, VT)]

        def m0(par): return small[:, par, 0:1]
        def m1(par): return small[:, par, 1:2]
        def nb(par): return small[:, par, 2:3]
        def ssum(par): return small[:, par, 3:4]
        def masked(par): return small[:, par, 4:5]
        def r(par): return small[:, par, 5:6]

        block = nc.Block()
        with block:
            @block.sync
            def _(sp):
                with sp.Fori(0, HEADS) as h:
                    sp.wait_ge(wo_lo_s, h + 1)
                    sp.dma_start(wo_st[:, :, :], wo_rows[ds(h, 1), :, :, :].rearrange("a p k d -> p (a k) d")).then_inc(wo_loaded, 16)
                    with sp.Fori(0, T // 2) as j:
                        for par in range(2):
                            i = 16 * h + 2 * j + par
                            sp.wait_ge(logits_read, 2 * i + 2)
                            sp.dma_start(B[par][:, :], bias_d[ds(2 * j + par, 1), :, :].rearrange("a p m -> p (a m)")).then_inc(bias_par[par], 16)

            @block.tensor
            def _(pe):
                def project(h):
                    for n, kind in enumerate(kinds):
                        with pe.Fori(0, 2) as u:
                            if n == 2:
                                pe.wait_ge(wo_hi_s, h + 1)
                                pe.wait_ge(wo_lo_s, h + 2)
                                pe.wait_ge(bank_free, PER_HEAD * h + 8 + BANKS_FREE)
                            if n == 0:
                                pe.wait_ge(logits_read, 32 * h + READS_FREE)
                            for b in range(4):
                                pe.wait_ge(bank_free, PER_HEAD * h + 8 * n + 4 * u + b + 1)
                                if kind is None:
                                    for m in range(2):
                                        o = bank[b][:, m * D:(m + 1) * D]
                                        for k in range(KC):
                                            for w, x in ((0, 0), (0, 1), (1, 0)):
                                                last = nc.tensor.matmul(o, VT[w][:, k, ds((4 * u + b) * 2 * P + m * P, P)], WO[x][:, k, :],
                                                                        start=(k == 0 and w == x == 0), stop=(k == 1 and w == 1))
                                else:
                                    for m in range(2):
                                        o = bank[b][:, m * ROWS:(m + 1) * ROWS]
                                        for k in range(KC):
                                            for w, x in ((0, 0), (0, 1), (1, 0)):
                                                W = (WH, WL)[w][kind[0]]
                                                hT = (hT_hi, hT_lo)[x]
                                                last = nc.tensor.matmul(o, W[:, k, ds((4 * u + b) * D + m * P, P)], hT[:, k, ds(h * ROWS, ROWS)],
                                                                        start=(k == 0 and w == x == 0), stop=(k == 1 and w == 1))
                                last.then_inc(proj, 1)

                def qk(i, t, half):
                    pe.wait_ge(logits_read, 2 * i + half + READS_FREE - 1)
                    for b in range(2):
                        o = L[half][:, b * BANK:(b + 1) * BANK]
                        c0 = half * 2 * BANK + b * BANK
                        for k in range(KC):
                            for w, x in ((0, 0), (0, 1), (1, 0)):
                                last = nc.tensor.matmul(o, VT[w][:, k, ds(t * P, P)], KT[x][:, k, c0:c0 + BANK],
                                                        start=(k == 0 and w == x == 0), stop=(k == 1 and w == 1))
                    last.then_inc(scores, 1)

                def turn(i, par, q):
                    if q == 0:
                        pe.wait_ge(exped, i + 1)
                    pe.wait_ge(pt_free, 4 * i + q + 1)
                    for m in range(4):
                        last = nc.tensor.transpose(TP[q % 2][:, m * P:(m + 1) * P], E[par][:, (4 * q + m) * P:(4 * q + m + 1) * P], ident[:, :])
                    last.then_inc(tposed, 1)

                def av(i, par, q):
                    pe.wait_ge(pt_free, 4 * i + q + 1 + PT_FREE)
                    if q == 0:
                        pe.wait_ge(av_free, i + 1)
                    for m in range(4 * q, 4 * q + 4):
                        for w, x in ((0, 0), (0, 1), (1, 0)):
                            last = nc.tensor.matmul(AV[par][:, :], PT[w][:, m, :], VW[x][:, m, :],
                                                    start=(m == 0 and w == x == 0), stop=(m == T - 1 and w == 1))
                    if q == 3:
                        last.then_inc(av_done, 1)

                def item(i, t, par, more):
                    if more:
                        qk(i + 1, t + 1, 0)
                    turn(i, par, 0)
                    turn(i, par, 1)
                    if more:
                        qk(i + 1, t + 1, 1)
                    av(i, par, 0)
                    turn(i, par, 2)
                    av(i, par, 1)
                    turn(i, par, 3)
                    av(i, par, 2)
                    av(i, par, 3)

                with pe.Fori(0, HEADS) as h:
                    project(h)
                    pe.wait_ge(bank_free, PER_HEAD * (h + 1) + BANKS_FREE)
                    qk(16 * h, 0, 0)
                    qk(16 * h, 0, 1)
                    with pe.Fori(0, T // 2 - 1) as j:
                        item(16 * h + 2 * j, 2 * j, 0, True)
                        item(16 * h + 2 * j + 1, 2 * j + 1, 1, True)
                    item(16 * h + T - 2, T - 2, 0, True)
                    item(16 * h + T - 1, T - 1, 1, False)

            def evacuated(kind, n, m):
                if kind is None:
                    return [VW[x][:, ds(2 * m, 2), :] for x in range(2)]
                return [kind[1][x][:, :, ds(m * ROWS, ROWS)] for x in range(2)]

            @block.scalar
            def _(s):
                def hi(i, q):
                    s.wait_ge(tposed, 4 * i + q + 1)
                    nc.scalar.activation(PT[0][:, 4 * q:4 * q + 4, :].rearrange("p a b -> p (a b)"), TP[q % 2][:, :], ACT.Copy,
                                         scale=P_SCALE).then_inc(pt_hi, 1)

                def exp(i, par):
                    s.wait_ge(maxed, i + 1)
                    nc.scalar.activation(masked(par), nb(par), ACT.Exp, bias=minus[:, 0:1], scale=1.0)
                    nc.scalar.activation(E[par][:, :], E[par][:, :], ACT.Exp, bias=nb(par), scale=sc[:, 0:1],
                                         accum_out=ssum(par)).then_inc(exped, 1)

                with s.Fori(0, HEADS) as h:
                    s.wait_ge(wo_loaded, 16 * (h + 1))
                    nc.scalar.activation(WO[0][:, :, :], wo_st[:, :, :], ACT.Copy, scale=winv[:, 3:4]).then_inc(wo_hi_s, 1)
                    for n, kind in enumerate(kinds):
                        with s.Fori(0, 2) as u:
                            for b in range(4):
                                s.wait_ge(proj, PER_HEAD * h + 8 * n + 4 * u + b + 1)
                                nc.scalar.activation(evacuated(kind, n, 4 * u + b)[0], bank[b].rearrange("p (a b) -> p a b", a=2), ACT.Copy,
                                                     scale=VW_SCALE if kind is None else 1.0).then_inc(proj_hi, 1)
                    exp(16 * h, 0)
                    with s.Fori(0, T // 2 - 1) as j:
                        for par in range(2):
                            i = 16 * h + 2 * j + par
                            for q in range(4):
                                hi(i, q)
                            exp(i + 1, 1 - par)
                    for q in range(4):
                        hi(16 * h + T - 2, q)
                    exp(16 * h + T - 1, 1)
                    for q in range(4):
                        hi(16 * h + T - 1, q)

            @block.vector
            def _(v):
                nc.vector.memset(minus[:, :], MASKED).then_inc(bank_free, BANKS_FREE)
                nc.vector.memset(small[:, :, :], 0.0).then_inc(wo_lo_s, 1)
                v.wait_ge(wo_lo_s, 1)
                v.wait_ge(bank_free, BANKS_FREE)
                nc.vector.memset(small[:, :, :], 0.0).then_inc(logits_read, READS_FREE)
                v.wait_ge(logits_read, READS_FREE)
                nc.vector.memset(small[:, :, :], 0.0).then_inc(pt_free, PT_FREE)
                v.wait_ge(pt_free, PT_FREE)
                nc.vector.memset(small[:, :, :], 0.0).then_inc(av_free, AV_FREE)
                v.wait_ge(av_free, AV_FREE)

                def peak(i, par, half, link):
                    v.wait_ge(scores, 2 * i + half + 1)
                    if half == 0:
                        v.wait_ge(bias_par[par], 8 * (i - par) + 16)
                    link.note(nc.vector.tensor_copy(small[:, par, 6 + half:7 + half], B[par][:, N + 1 - half:N + 2 - half]))
                    cols = slice(half * 2 * BANK, (half + 1) * 2 * BANK)
                    return nc.vector.tensor_tensor_reduce(
                        E[par][:, cols], L[half][:, :], B[par][:, cols], 1.0, (B[par][:, N:N + 1], m0(par))[half],
                        ALU.add, ALU.max, (m0(par), m1(par))[half])

                def peaks_end(i, par, link):
                    peak(i, par, 1, link).then_inc(logits_read, 1)
                    v.wait_ge(logits_read, 2 * i + 2 + READS_FREE)
                    nc.vector.tensor_scalar(nb(par), m1(par), sc[:, 1:2], None, ALU.mult).then_inc(maxed, 1)

                def lo(i, q):
                    v.wait_ge(pt_hi, 4 * i + q + 1)
                    nc.vector.scalar_tensor_tensor(out=PT[1][:, 4 * q:4 * q + 4, :].rearrange("p a b -> p (a b)"), in0=TP[q % 2][:, :],
                                                   scalar=P_SCALE, in1=PT[0][:, 4 * q:4 * q + 4, :].rearrange("p a b -> p (a b)"),
                                                   op0=ALU.mult, op1=ALU.subtract).then_inc(pt_free, 1)

                def add(i, t, par, link):
                    v.wait_ge(exped, i + 1)
                    link(nc.vector.scalar_tensor_tensor(out=r(par), in0=masked(par), scalar=small[:, par, 6:7], in1=ssum(par),
                                                        op0=ALU.mult, op1=ALU.add))
                    link(nc.vector.reciprocal(r(par), r(par)))
                    link(nc.vector.tensor_scalar(r(par), r(par), sc[:, 4:5], None, ALU.mult))
                    v.wait_ge(av_done, i + 1)
                    nc.vector.scalar_tensor_tensor(out=acc[:, ds(t, 1), :].rearrange("p a d -> p (a d)"), in0=AV[par][:, :], scalar=r(par),
                                                   in1=acc[:, ds(t, 1), :].rearrange("p a d -> p (a d)"),
                                                   op0=ALU.mult, op1=ALU.add).then_inc(av_free, 1)

                def item(i, t, par, more, link):
                    if more:
                        peak(i + 1, 1 - par, 0, link).then_inc(logits_read, 1)
                        v.wait_ge(logits_read, 2 * i + 3 + READS_FREE)
                    lo(i, 0)
                    lo(i, 1)
                    if more:
                        peaks_end(i + 1, 1 - par, link)
                    lo(i, 2)
                    lo(i, 3)
                    add(i, t, par, link)

                with v.Fori(0, HEADS) as h:
                    v.wait_ge(wo_hi_s, h + 1)
                    nc.vector.scalar_tensor_tensor(out=WO[1][:, :, :], in0=wo_st[:, :, :], scalar=winv[:, 3:4], in1=WO[0][:, :, :],
                                                   op0=ALU.mult, op1=ALU.subtract).then_inc(wo_lo_s, 1)
                    for n, kind in enumerate(kinds):
                        with v.Fori(0, 2) as u:
                            for b in range(4):
                                v.wait_ge(proj_hi, PER_HEAD * h + 8 * n + 4 * u + b + 1)
                                to = evacuated(kind, n, 4 * u + b)
                                nc.vector.scalar_tensor_tensor(out=to[1], in0=bank[b].rearrange("p (a b) -> p a b", a=2),
                                                               scalar=VW_SCALE if kind is None else 1.0, in1=to[0],
                                                               op0=ALU.mult, op1=ALU.subtract).then_inc(bank_free, 1)
                    link = Chain(v, chain, h * (5 * T))
                    peak(16 * h, 0, 0, link).then_inc(logits_read, 1)
                    v.wait_ge(logits_read, 32 * h + 1 + READS_FREE)
                    peaks_end(16 * h, 0, link)
                    with v.Fori(0, T // 2 - 1) as j:
                        link = Chain(v, chain, h * (5 * T) + 2 + j * 10)
                        item(16 * h + 2 * j, 2 * j, 0, True, link)
                        item(16 * h + 2 * j + 1, 2 * j + 1, 1, True, link)
                    link = Chain(v, chain, h * (5 * T) + 2 + (T // 2 - 1) * 10)
                    item(16 * h + T - 2, T - 2, 0, True, link)
                    item(16 * h + T - 1, T - 1, 1, False, link)


def prepare(nc, sb, ps, sem, a, deg, scales, ident, ident16, halfp, w1, w2, w3, gb, sc, acc, x_d):
    loaded, stored, dve, bases, powed, vec_done, spread, ratios, largest = (sem("prep_" + s) for s in (
        "loaded", "stored", "dve", "bases", "powed", "vec", "spread", "ratios", "largest"))
    with ExitStack() as c:
        row = sb(c, "gamma_beta_row", [1, 2 * D])
        ones = sb(c, "ones_row", [1, P])
        base = sb(c, "deg_base", [P, 2, T])
        zero = sb(c, "deg_zero", [P, T])
        ratio, top = sb(c, "deg_ratio", [P, T]), sb(c, "deg_ratio_top", [P, 2])
        bc = ps(c, "gamma_beta_ps", [P, 2 * D])
        block = nc.Block()
        with block:
            @block.sync
            def _(sp):
                sp.dma_start(row[:, 0:D], a["L1_gnn_gamma"].rearrange("(a d) -> a d", a=1)).then_inc(loaded, 16)
                sp.dma_start(row[:, D:2 * D], a["L1_gnn_beta"].rearrange("(a d) -> a d", a=1)).then_inc(loaded, 16)
                sp.dma_start(w1[:, :, :], a["L1_gnn_W1"].rearrange("(k p) n -> p k n", p=P)).then_inc(loaded, 16)
                sp.dma_start(w3[:, :, :], a["L1_gnn_W3"].rearrange("(k p) n -> p k n", p=P)).then_inc(loaded, 16)
                sp.dma_start(w2[:, :], a["L1_gnn_W2"]).then_inc(loaded, 16)
                sp.dma_start(x_d, acc[:, :, :]).then_inc(stored, 16)
                sp.wait_ge(loaded, 16 * 5)
                sp.wait_ge(stored, 16)

            @block.vector
            def _(v):
                link = Chain(v, dve)
                link(nc.vector.memset(ones[:, :], 1.0))
                link(nc.vector.tensor_scalar(ident16[:, :], ident[:, :], A_SCALE, None, ALU.mult))
                link(nc.vector.tensor_scalar(scales[:, 0:2, :], deg[:, :, :], 1.0, 1e-12, ALU.add, ALU.max))
                link(nc.vector.reciprocal(scales[:, 0:2, :], scales[:, 0:2, :]))
                link(nc.vector.scalar_tensor_tensor(out=ratio[:, :], in0=deg[:, 0, :], scalar=1.0, in1=scales[:, 1, :],
                                                    op0=ALU.add, op1=ALU.mult))
                nc.vector.tensor_reduce(top[:, 0:1], ratio[:, :], X, ALU.max).then_inc(ratios, 1)
                link(nc.vector.tensor_scalar(base[:, 0, :], deg[:, 0, :], 1e-8, None, ALU.add))
                link(nc.vector.tensor_scalar(zero[:, :], deg[:, 0, :], 1.0, 0.0, ALU.add, ALU.is_equal))
                nc.vector.scalar_tensor_tensor(out=base[:, 1, :], in0=deg[:, 0, :], scalar=1.0, in1=zero[:, :],
                                               op0=ALU.add, op1=ALU.add).then_inc(bases, 1)
                v.wait_ge(powed, 1)
                link(nc.vector.tensor_scalar(zero[:, :], zero[:, :], -1.0, 1.0, ALU.mult, ALU.add))
                nc.vector.tensor_tensor(scales[:, 3, :], scales[:, 3, :], zero[:, :], ALU.mult).then_inc(vec_done, 1)
                v.wait_ge(largest, 1)
                link(nc.vector.tensor_scalar(top[:, 1:2].bitcast(U32), top[:, 1:2].bitcast(U32), 0x7F800000, None, ALU.bitwise_and))
                link(nc.vector.tensor_scalar(sc[:, 7:8], top[:, 1:2], 1.0 / X_SCALE, None, ALU.mult))
                nc.vector.reciprocal(sc[:, 6:7], sc[:, 7:8]).then_inc(vec_done, 1)
                v.wait_ge(spread, 1)
                nc.vector.tensor_copy(gb[:, :, :].rearrange("p a d -> p (a d)"), bc[:, :]).then_inc(vec_done, 1)

            @block.gpsimd
            def _(pl):
                pl.wait_ge(bases, 1)
                for n in range(2):
                    last = nc.gpsimd.tensor_tensor(scales[:, 2 + n, :], base[:, n, :], halfp[:, :], ALU.pow)
                last.then_inc(powed, 1)
                pl.wait_ge(ratios, 1)
                nc.gpsimd.partition_all_reduce(top[:, 1:2], top[:, 0:1], P, ABSMAX).then_inc(largest, 1)

            @block.tensor
            def _(pe):
                pe.wait_ge(loaded, 16 * 5)
                pe.wait_ge(dve, 1)
                nc.tensor.matmul(bc[:, :], ones[:, :], row[:, :], start=True, stop=True).then_inc(spread, 1)


def last_weights(nc, sb, ps, sem, a, ident, wT, bb):
    loaded, turned, copied, one = (sem("lastw_" + s) for s in ("loaded", "turned", "copied", "one"))
    with ExitStack() as c:
        w0 = sb(c, "l2_w", [P, KC, D])
        row, ones = sb(c, "l2_b_row", [1, D]), sb(c, "l2_ones", [1, P])
        tp, bc = ps(c, "l2_tp", [P, BANK]), ps(c, "l2_bc", [P, D])
        block = nc.Block()
        with block:
            @block.sync
            def _(sp):
                sp.dma_start(w0[:, :, :], a["L2_gnn_W"].rearrange("(k p) n -> p k n", p=P)).then_inc(loaded, 16)
                sp.dma_start(row[:, :], a["L2_gnn_b"].rearrange("(a d) -> a d", a=1)).then_inc(loaded, 16)
                sp.wait_ge(loaded, 32)

            @block.tensor
            def _(pe):
                pe.wait_ge(loaded, 32)
                pe.wait_ge(one, 1)
                for k in range(KC):
                    for o in range(KC):
                        nc.tensor.transpose(tp[:, k * D + o * P:k * D + (o + 1) * P], w0[:, o, k * P:(k + 1) * P], ident[:, :])
                nc.tensor.matmul(bc[:, :], ones[:, :], row[:, :], start=True, stop=True).then_inc(turned, 1)

            @block.vector
            def _(v):
                nc.vector.memset(ones[:, :], 1.0).then_inc(one, 1)
                v.wait_ge(turned, 1)
                nc.vector.tensor_copy(wT[:, :, :].rearrange("p k d -> p (k d)"), tp[:, :]).then_inc(copied, 1)
                nc.vector.tensor_copy(bb[:, :], bc[:, :]).then_inc(copied, 1)


def normalize(nc, sb, ps, sem, name, src, dst, halfp, scale, gb=None, add=None, stored=None):
    stats_done, rstd_done, dve, centred, pool, loaded = (
        sem(f"{name}_{s}") for s in ("stats_done", "rstd_done", "dve", "centred", "pool", "loaded"))
    with ExitStack() as c:
        stats, mv, rstd = sb(c, name + "_stats", [P, T, 6]), sb(c, name + "_mv", [P, T, 2]), sb(c, name + "_rstd", [P, T])
        block = nc.Block()
        with block:
            if stored is not None:
                @block.sync
                def _(sp):
                    sp.dma_start(add[:, :, :], stored).then_inc(loaded, 16)

            @block.vector
            def _(v):
                link = Chain(v, dve)
                normalize_stats(nc, v, link, src, stats, mv)
                link(nc.vector.tensor_scalar(rstd[:, :], mv[:, :, 1], LN_EPS, None, ALU.add))
                nc.vector.tensor_copy(stats[:, :, 0], mv[:, :, 0]).then_inc(stats_done, 1)
                v.wait_ge(rstd_done, 1)
                if stored is not None:
                    v.wait_ge(loaded, 16)
                for t in range(T):
                    ins = nc.vector.tensor_scalar(dst[:, t, :], src[:, t, :], mv[:, t, 0:1], rstd[:, t:t + 1], ALU.subtract, ALU.mult)
                    if gb is None:
                        ins.then_inc(centred, 1)
                    else:
                        link(ins)
                        link(nc.vector.tensor_tensor(dst[:, t, :], dst[:, t, :], gb[:, 0, :], ALU.mult))
                        link(nc.vector.tensor_tensor(dst[:, t, :], dst[:, t, :], gb[:, 1, :], ALU.add))
                        nc.vector.tensor_tensor(add[:, t, :], add[:, t, :], dst[:, t, :], ALU.add).then_inc(centred, 1)

            @block.gpsimd
            def _(pl):
                pl.wait_ge(stats_done, 1)
                nc.gpsimd.tensor_tensor(rstd[:, :], rstd[:, :], halfp[:, :], ALU.pow).then_inc(rstd_done, 1)

            @block.scalar
            def _(s):
                if gb is None:
                    for t in range(T):
                        s.wait_ge(centred, t + 1)
                        nc.scalar.activation(dst[:, t, :], dst[:, t, :], ACT.Relu, scale=scale).then_inc(pool, 1)


def split_rows(nc, sb, ps, sem, name, src, parts, scale, row_scale=None):
    scaled, dve, cut = (sem(f"{name}_{s}") for s in ("scaled", "dve", "cut"))
    with ExitStack() as c:
        rest = sb(c, name + "_rest", [P, T, D])
        block = nc.Block()
        with block:
            @block.scalar
            def _(s):
                for t in range(T):
                    nc.scalar.activation(rest[:, t, :], src[:, t, :], ACT.Copy,
                                         scale=scale if row_scale is None else row_scale[:, t:t + 1]).then_inc(scaled, 1)

            @block.vector
            def _(v):
                link = Chain(v, dve)
                for t in range(T):
                    v.wait_ge(scaled, t + 1)
                    for n, part in enumerate(parts):
                        link(nc.vector.tensor_copy(part[:, t, :], rest[:, t, :]))
                        if n < len(parts) - 1:
                            link(nc.vector.tensor_tensor(rest[:, t, :], rest[:, t, :], part[:, t, :], ALU.subtract))


def add_row(nc, sb, ps, sem, name, acc, row):
    added = sem(name + "_added")
    block = nc.Block()
    with block:
        @block.vector
        def _(v):
            for t in range(T):
                nc.vector.tensor_tensor(acc[:, t, :], acc[:, t, :], row[:, :], ALU.add).then_inc(added, 1)


def features(nc, sb, ps, sem, name, src, ident, products, logits):
    tp_s, xt_s, u_s, done, q_s, qc_s, w_loaded = (
        sem(f"{name}_{s}") for s in ("turned", "xt", "product", "free", "q", "q_copied", "w_loaded"))
    with ExitStack() as c:
        xT = [sb(c, f"{name}_xT{n}", [P, D]) for n in range(2)]
        qs = [sb(c, f"{name}_q{n}", [64, P]) for n in range(2)]
        TP = [ps(c, f"{name}_tp{n}", [P, D]) for n in range(2)]
        U = [ps(c, f"{name}_u{n}", [P, D]) for n in range(2)]
        QK = [ps(c, f"{name}_qk{n}", [64, 3 * P]) for n in range(2)]
        W = [sb(c, f"{name}_w{n}", [P, KC, D]) for n in range(len(products))]
        block = nc.Block()
        with block:
            @block.sync
            def _(sp):
                for (w, _), to in zip(products, W):
                    sp.dma_start(to[:, :, :], w.rearrange("(k p) d -> p k d", p=P)).then_inc(w_loaded, 16)

            @block.tensor
            def _(pe):
                if products:
                    pe.wait_ge(w_loaded, 16 * len(products))
                for t in range(T):
                    b = t % 2
                    if t >= 2:
                        pe.wait_ge(done, t - 1)
                    for k in range(KC):
                        last = nc.tensor.transpose(TP[b][:, k * P:(k + 1) * P], src[:, t, k * P:(k + 1) * P], ident[:, :])
                    last.then_inc(tp_s, 1)
                    pe.wait_ge(xt_s, t + 1)
                    for w in W:
                        for k in range(KC):
                            last = nc.tensor.matmul(U[b][:, :], xT[b][:, k * P:(k + 1) * P], w[:, k, :], start=(k == 0), stop=(k == 1))
                    if logits:
                        w1, w2, w3, QT, KT = logits
                        for n, w in ((0, w1), (1, w3)):
                            for k in range(KC):
                                last = nc.tensor.matmul(QK[b][:, n * P:(n + 1) * P], w[:, k, :], xT[b][:, k * P:(k + 1) * P],
                                                        start=(k == 0), stop=(k == 1))
                        last.then_inc(q_s, 1)
                        pe.wait_ge(qc_s, t + 1)
                        last = nc.tensor.matmul(QK[b][:, 2 * P:3 * P], w2[:, :], qs[b][:, :], start=True, stop=True)
                    last.then_inc(u_s, 1)

            @block.scalar
            def _(s):
                for t in range(T):
                    b = t % 2
                    s.wait_ge(tp_s, t + 1)
                    nc.scalar.activation(xT[b][:, :], TP[b][:, :], ACT.Copy).then_inc(xt_s, 1)
                    if logits:
                        s.wait_ge(q_s, t + 1)
                        nc.scalar.activation(qs[b][:, :], QK[b][:, 0:P], ACT.Copy).then_inc(qc_s, 1)

            @block.vector
            def _(v):
                for t in range(T):
                    b = t % 2
                    v.wait_ge(u_s, t + 1)
                    for _, to in products:
                        if to is None:
                            last = nc.vector.tensor_copy(src[:, t, :], U[b][:, :])
                        else:
                            last = nc.vector.tensor_tensor(to[:, t, :], to[:, t, :], U[b][:, :], ALU.add)
                    if logits:
                        cols = slice(t * P, (t + 1) * P)
                        nc.vector.tensor_copy(logits[4][:, cols], QK[b][:, P:2 * P])
                        last = nc.vector.tensor_copy(logits[3][:, cols], QK[b][:, 2 * P:3 * P])
                    last.then_inc(done, 1)


def diffuse(nc, sb, ps, sem, name, at_d, ident, ident16, target, jobs, relu=False):
    at_loaded = [sem(f"{name}_at_loaded{n}") for n in range(2)]
    prod, xs_s, tp_s, xt_s, u_s, u_free, dve = (sem(f"{name}_{s}") for s in (
        "product", "scaled", "turned", "xt", "weighted", "free", "dve"))
    R = sum(len(j[2]) for j in jobs)
    J = len(jobs)
    results = [(n, r) for n, j in enumerate(jobs) for r in j[2]]
    with ExitStack() as c:
        AT = [sb(c, f"{name}_at{n}", [P, 2, T, P], F16) for n in range(2)]
        xs = [sb(c, f"{name}_xs{n}", [P, D]) for n in range(2)]
        rest = sb(c, f"{name}_rest", [P, D])
        xT = [sb(c, f"{name}_xT{n}", [P, D]) for n in range(2)]
        rsc = sb(c, f"{name}_row_scales", [P, 2, T])
        PR = [[ps(c, f"{name}_pr{n}_{m}", [P, D]) for m in range(2)] for n in range(J)]
        TP = [ps(c, f"{name}_tp{n}", [P, D]) for n in range(2)]
        UP = [ps(c, f"{name}_up{n}", [P, D]) for n in range(2)]
        block = nc.Block()
        with block:
            @block.sync
            def _(sp):
                with sp.Fori(0, T // 2) as j:
                    for b in range(2):
                        sp.wait_ge(xs_s, R * (2 * j + b) + R)
                        sp.dma_start(AT[b][:, :, :, :].rearrange("p x m n -> p (x m n)"),
                                     at_d[ds(2 * j + b, 1), :, :].rearrange("a p m -> p (a m)")).then_inc(at_loaded[b], 16)

            @block.tensor
            def _(pe):
                def multiply(t, b, half):
                    for n, (parts, _, _) in enumerate(jobs):
                        pe.wait_ge(at_loaded[b], 16 * (half + 1))
                        pe.wait_ge(xs_s, R * t + sum(len(k[2]) for k in jobs[:n + 1]))
                        wide = len(parts) == 3
                        pairs = ((0, 0), (0, 1), (0, 2), (1, 0), (1, 1)) if wide else ((0, 0), (0, 1), (1, 0))
                        for m in range(T):
                            for x, y in pairs:
                                last = nc.tensor.matmul(PR[n][b][:, :], AT[b][:, x, m, :], parts[y][:, m, :],
                                                        start=(m == 0 and x == y == 0),
                                                        stop=(ident16 is None and m == T - 1 and (x, y) == pairs[-1]))
                        if ident16 is not None:
                            for y, part in enumerate(parts):
                                last = nc.tensor.matmul(PR[n][b][:, :], ident16[:, :], part[:, ds(t, 1), :].rearrange("p a d -> p (a d)"),
                                                        start=False, stop=(y == len(parts) - 1))
                        last.then_inc(prod, 1)

                def weigh(t, b):
                    for r, (_, (_, _, _, w)) in enumerate(results):
                        slot = r if R == 2 else b
                        i = R * t + r
                        if w is None:
                            continue
                        pe.wait_ge(xs_s, i + 1 + 2 * R)
                        pe.wait_ge(u_free, i + 1)
                        for k in range(KC):
                            last = nc.tensor.transpose(TP[slot][:, k * P:(k + 1) * P], xs[slot][:, k * P:(k + 1) * P], ident[:, :])
                        last.then_inc(tp_s, 1)
                    for r, (_, (_, _, _, w)) in enumerate(results):
                        slot = r if R == 2 else b
                        i = R * t + r
                        if w is None:
                            continue
                        pe.wait_ge(xt_s, i + 1)
                        for k in range(KC):
                            last = nc.tensor.matmul(UP[slot][:, :], xT[slot][:, k * P:(k + 1) * P], w[:, k, :], start=(k == 0), stop=(k == 1))
                        last.then_inc(u_s, 1)

                multiply(0, 0, 0)
                with pe.Fori(0, T // 2 - 1) as j:
                    multiply(2 * j + 1, 1, j)
                    weigh(2 * j, 0)
                    multiply(2 * j + 2, 0, j + 1)
                    weigh(2 * j + 1, 1)
                multiply(T - 1, 1, T // 2 - 1)
                weigh(T - 2, 0)
                weigh(T - 1, 1)

            @block.scalar
            def _(s):
                def scale_rows(t, b):
                    for r, (n, (rows, _, _, _)) in enumerate(results):
                        slot = r if R == 2 else b
                        s.wait_ge(prod, J * t + n + 1)
                        s.wait_ge(u_free, R * t + r + 1)
                        nc.scalar.activation(xs[slot][:, :], PR[n][b][:, :], ACT.Relu if relu else ACT.Copy,
                                             scale=rsc[:, r, ds(t, 1)]).then_inc(xs_s, 1)

                def weighted(t, b):
                    for r, (_, (_, _, _, w)) in enumerate(results):
                        slot = r if R == 2 else b
                        if w is None:
                            continue
                        s.wait_ge(tp_s, R * t + r + 1)
                        nc.scalar.activation(xT[slot][:, :], TP[slot][:, :], ACT.Copy).then_inc(xt_s, 1)

                s.wait_ge(u_free, 2)
                scale_rows(0, 0)
                with s.Fori(0, T // 2 - 1) as j:
                    weighted(2 * j, 0)
                    scale_rows(2 * j + 1, 1)
                    weighted(2 * j + 1, 1)
                    scale_rows(2 * j + 2, 0)
                weighted(T - 2, 0)
                scale_rows(T - 1, 1)
                weighted(T - 1, 1)

            @block.vector
            def _(v):
                link = Chain(v, dve)
                for r, (n, (rows, _, to_scale, _)) in enumerate(results):
                    link(nc.vector.tensor_scalar(rsc[:, r, :], rows, to_scale / (jobs[n][1] * A_SCALE), None, ALU.mult))
                link(nc.vector.memset(rest[:, :], 0.0))
                head = link.n
                nc.vector.memset(rest[:, :], 0.0).then_inc(xs_s, 2 * R)
                v.wait_ge(xs_s, 2 * R)
                nc.vector.memset(rest[:, :], 0.0).then_inc(u_free, 2)
                v.wait_ge(u_free, 2)

                def here(x, t):
                    return x[:, ds(t, 1), :].rearrange("p a d -> p (a d)")

                def cut(t, b, link):
                    for r, (_, (_, parts, to_scale, w)) in enumerate(results):
                        slot = r if R == 2 else b
                        v.wait_ge(xs_s, R * t + r + 1 + 2 * R)
                        if parts:
                            link(nc.vector.tensor_copy(here(parts[0], t), xs[slot][:, :]))
                            link(nc.vector.tensor_tensor(rest[:, :], xs[slot][:, :], here(parts[0], t), ALU.subtract))
                            link(nc.vector.tensor_copy(here(parts[1], t), rest[:, :]))
                            if len(parts) == 3:
                                link(nc.vector.tensor_tensor(rest[:, :], rest[:, :], here(parts[1], t), ALU.subtract))
                                link(nc.vector.tensor_copy(here(parts[2], t), rest[:, :]))
                        if w is None:
                            nc.vector.tensor_tensor(here(target, t), here(target, t), xs[slot][:, :], ALU.add).then_inc(u_free, 1)

                def add(t, b, link):
                    for r, (_, (_, _, to_scale, w)) in enumerate(results):
                        slot = r if R == 2 else b
                        i = R * t + r
                        if w is None:
                            continue
                        v.wait_ge(u_s, i + 1)
                        nc.vector.scalar_tensor_tensor(out=here(target, t), in0=UP[slot][:, :], scalar=1.0 / to_scale, in1=here(target, t),
                                                       op0=ALU.mult, op1=ALU.add).then_inc(u_free, 1)
                        v.wait_ge(u_free, i + 3)

                per = sum(0 if not p else 3 if len(p) == 2 else 5 for _, (_, p, _, w) in results)
                link = Chain(v, dve, head)
                cut(0, 0, link)
                with v.Fori(0, T // 2 - 1) as j:
                    link = Chain(v, dve, head + per + 2 * per * j)
                    add(2 * j, 0, link)
                    cut(2 * j + 1, 1, link)
                    add(2 * j + 1, 1, link)
                    cut(2 * j + 2, 0, link)
                    assert link.n == 2 * per
                link = Chain(v, dve, head + per + per * (T - 2))
                add(T - 2, 0, link)
                cut(T - 1, 1, link)
                add(T - 1, 1, link)


def nucleus(nc, sb, ps, sem, name, QT, KT, parts, out, ident, diffusion):
    u1, u2, at_d, scales, ident16, y, sc, Xp, Xf, Xb, step = diffusion
    jobs = [(Xp, 2)] if step == 0 else [(Xf, 1), (Xb, 1)]
    (u_loaded, hi_loaded, lo_loaded, s_prod, rsc_s, xs_s, s_tp, s_xt, weighted, us_s, cut_s, added, pchain) = (
        sem(f"{name}_{s}") for s in ("u_loaded", "at_hi", "at_lo", "s_product", "row_scales", "xs", "xs_turned", "xs_T",
                                     "weighted", "us", "cut", "added", "pool_chain"))
    (scores, l_free, peaked, exped, masked_s, e_free, tp_s, hi_s, lo_s, prod_s, out_s, dve0) = (
        sem(f"{name}_{s}") for s in ("scores", "l_free", "peaked", "exped", "masked", "e_free", "turned", "hi", "lo", "product",
                                     "out", "dve0"))
    GROUPS = T // G
    with ExitStack() as c:
        e = sb(c, name + "_e", [P, 2, G, N])
        junk = sb(c, name + "_junk", [P, N])
        void = junk[:, :].bitcast(BF16).rearrange("p (a n) -> p a n", a=2)
        PT = [sb(c, f"{name}_pT{n}", [P, T, P], F16) for n in ("hi", "lo")]
        staging = [sb(c, f"{name}_stage{n}", [P, BANK]) for n in range(2)]
        nmax, Z = sb(c, name + "_nmax", [P, T]), sb(c, name + "_Z", [P, T])
        rs = sb(c, name + "_rs", [P, T])
        S = sb(c, name + "_small", [P, 18, G])
        top, kept = sb(c, name + "_top", [P, G, 8]), sb(c, name + "_kept", [P, G, 8])
        pre = sb(c, name + "_prefix", [P, G, 8])
        one = sb(c, name + "_one", [P, 8])
        und, undT = sb(c, name + "_und", [P, 32]), sb(c, name + "_undT", [P, 32])
        cell = sb(c, name + "_cell", [1, 8])
        flag = sb(c, name + "_flag", [1, 8], I32)
        U = sb(c, name + "_u", [P, 2, KC, D])
        AH, AL = sb(c, name + "_at_hi", [P, T, P], F16), sb(c, name + "_at_lo", [P, T, P], F16)
        rsc = sb(c, name + "_rsc", [P, 2, T])
        xs, xT = sb(c, name + "_xs", [P, 2, D]), sb(c, name + "_xsT", [P, 2 * D])
        us = sb(c, name + "_us", [P, D])
        scaled = sb(c, name + "_scaled", [P, D])
        L = ps(c, name + "_l", [P, N])
        TP = [ps(c, f"{name}_tp{n}", [P, BANK]) for n in range(2)]
        both = ps(c, f"{name}_pr", [P, BANK])
        PR = [both[:, n * D:(n + 1) * D] for n in range(2)]
        SP = ps(c, f"{name}_s", [P, BANK])
        lo, hi, t_, Gt, b_, target, M, R, tie, tstar, done, x_, m_lo, m_hi, short, y_, z_, w_ = (S[:, k, :] for k in range(18))
        block = nc.Block()
        with block:
            @block.sync
            def _(sp):
                for n, u in enumerate((u1, u2)):
                    sp.dma_start(U[:, n, :, :], u.rearrange("(k p) d -> p k d", p=P)).then_inc(u_loaded, 16)
                for t in range(T):
                    if t:
                        sp.wait_ge(s_prod, len(jobs) * t)
                    sp.dma_start(AH[:, :, :].rearrange("p m n -> p (m n)"), at_d[t, :, 0:N]).then_inc(hi_loaded, 16)
                    sp.dma_start(AL[:, :, :].rearrange("p m n -> p (m n)"), at_d[t, :, N:2 * N]).then_inc(lo_loaded, 16)

            @block.tensor
            def _(pe):
                def diffuse_tile(t):
                    pe.wait_ge(hi_loaded, 16 * t + 16)
                    pe.wait_ge(lo_loaded, 16 * t + 16)
                    if t:
                        pe.wait_ge(us_s, t)
                    for n, (rows, _) in enumerate(jobs):
                        o = SP[:, n * D:(n + 1) * D]
                        for x, A_ in enumerate((AH, AL)):
                            for m in range(T):
                                for y_part in rows[:2 - x]:
                                    nc.tensor.matmul(o, A_[:, m, :], y_part[:, m, :], start=(m == x == 0 and y_part is rows[0]), stop=False)
                        for part in rows:
                            last = nc.tensor.matmul(o, ident16[:, :], part[:, t, :], start=False, stop=(part is rows[1]))
                        last.then_inc(s_prod, 1)
                    pe.wait_ge(xs_s, 2 * t + 2)
                    for r in range(2):
                        for k in range(KC):
                            last = nc.tensor.transpose(TP[0][:, r * D + k * P:r * D + (k + 1) * P], xs[:, r, k * P:(k + 1) * P], ident[:, :])
                    last.then_inc(s_tp, 1)
                    pe.wait_ge(s_xt, t + 1)
                    if t == 0:
                        pe.wait_ge(u_loaded, 32)
                    for r in range(2):
                        for k in range(KC):
                            last = nc.tensor.matmul(SP[:, 0:D], xT[:, r * D + k * P:r * D + (k + 1) * P], U[:, r, k, :],
                                                    start=(r == k == 0), stop=(r == k == 1))
                    last.then_inc(weighted, 1)

                def logits(g, k):
                    i = G * g + k
                    if i:
                        pe.wait_ge(exped, i)
                    for b in range(4):
                        last = nc.tensor.matmul(L[:, b * BANK:(b + 1) * BANK], QT[:, i * P:(i + 1) * P], KT[:, b * BANK:(b + 1) * BANK],
                                                start=True, stop=True)
                    last.then_inc(scores, 1)

                def multiply(g, k):
                    i = G * g + k
                    pe.wait_ge(masked_s, i + 1)
                    for q in range(4):
                        if 4 * i + q >= 2:
                            pe.wait_ge(lo_s, 4 * i + q - 1)
                        for m in range(4):
                            last = nc.tensor.transpose(TP[q % 2][:, m * P:(m + 1) * P], e[:, g % 2, k, (4 * q + m) * P:(4 * q + m + 1) * P], ident[:, :])
                        last.then_inc(tp_s, 1)
                    if i:
                        pe.wait_ge(out_s, i)
                    for q in range(4):
                        pe.wait_ge(lo_s, 4 * i + q + 1)
                        for m in range(4 * q, 4 * q + 4):
                            for x, y in ((0, 0), (0, 1), (1, 0)):
                                last = nc.tensor.matmul(PR[k % 2], PT[x][:, m, :], parts[y][:, m, :],
                                                        start=(m == 0 and x == y == 0), stop=(m == T - 1 and x == 1))
                    last.then_inc(prod_s, 1)

                for k in range(G):
                    logits(0, k)
                for g in range(GROUPS):
                    for k in range(G):
                        if g + 1 < GROUPS:
                            logits(g + 1, k)
                        if g:
                            multiply(g - 1, k)
                        diffuse_tile(G * g + k)
                for k in range(G):
                    multiply(GROUPS - 1, k)

            @block.scalar
            def _(s):
                def results(t):
                    if t == 0:
                        s.wait_ge(rsc_s, 2)
                    if t and step == 0:
                        s.wait_ge(cut_s, t)
                    s.wait_ge(s_prod, len(jobs) * (t + 1))
                    for r in range(2):
                        n = r if step else 0
                        nc.scalar.activation(xs[:, r, :], SP[:, n * D:(n + 1) * D], ACT.Copy, scale=rsc[:, r, t:t + 1]).then_inc(xs_s, 1)
                    s.wait_ge(s_tp, t + 1)
                    nc.scalar.activation(xT[:, :], TP[0][:, :], ACT.Copy).then_inc(s_xt, 1)
                    s.wait_ge(weighted, t + 1)
                    if t:
                        s.wait_ge(added, t)
                    nc.scalar.activation(us[:, :], SP[:, 0:D], ACT.Copy).then_inc(us_s, 1)

                def exp(g, k):
                    i = G * g + k
                    s.wait_ge(peaked, i + 1)
                    if g >= 2:
                        s.wait_ge(prod_s, G * (g - 2) + k + 1)
                    nc.scalar.activation(e[:, g % 2, k, :], L[:, :], ACT.Exp, bias=nmax[:, i:i + 1], scale=1.0,
                                         accum_out=Z[:, i:i + 1]).then_inc(exped, 1)

                def halves(g, k):
                    i = G * g + k
                    for q in range(4):
                        s.wait_ge(tp_s, 4 * i + q + 1)
                        nc.scalar.activation(PT[0][:, 4 * q:4 * q + 4, :].rearrange("p a b -> p (a b)"), TP[q % 2][:, :], ACT.Copy,
                                             scale=P_SCALE).then_inc(hi_s, 1)
                        stage = staging[q % 2]
                        if 4 * i + q >= 2:
                            s.wait_ge(lo_s, 4 * i + q - 1)
                        nc.scalar.activation(stage[:, :], TP[q % 2][:, :], ACT.Copy, scale=P_SCALE).then_inc(hi_s, 1)
                    s.wait_ge(prod_s, i + 1)
                    nc.scalar.activation(out[:, i, :], PR[k % 2], ACT.Copy, scale=rs[:, i:i + 1]).then_inc(out_s, 1)

                for k in range(G):
                    exp(0, k)
                for g in range(GROUPS):
                    for k in range(G):
                        if g:
                            halves(g - 1, k)
                        if g + 1 < GROUPS:
                            exp(g + 1, k)
                        results(G * g + k)
                for k in range(G):
                    halves(GROUPS - 1, k)

            @block.gpsimd
            def _(pl):
                def lows(i):
                    for q in range(4):
                        pl.wait_ge(hi_s, 2 * (4 * i + q + 1))
                        nc.gpsimd.tensor_tensor(PT[1][:, 4 * q:4 * q + 4, :].rearrange("p a b -> p (a b)"), staging[q % 2][:, :],
                                                PT[0][:, 4 * q:4 * q + 4, :].rearrange("p a b -> p (a b)"), ALU.subtract).then_inc(lo_s, 1)

                def cut_and_add(t, link):
                    pl.wait_ge(xs_s, 2 * t + 2)
                    if step == 0:
                        for r, (hi_part, lo_part) in enumerate((Xf, Xb)):
                            link(nc.gpsimd.tensor_scalar(scaled[:, :], xs[:, r, :], X_SCALE if r == 0 else sc[:, 6:7], None, ALU.mult))
                            link(nc.gpsimd.tensor_copy(hi_part[:, t, :], scaled[:, :]))
                            nc.gpsimd.tensor_tensor(lo_part[:, t, :], scaled[:, :], hi_part[:, t, :], ALU.subtract).then_inc(link.sem if r == 0 else cut_s, 1)
                            if r == 0:
                                link.n += 1
                                link.wait()
                            else:
                                pl.wait_ge(cut_s, t + 1)
                    pl.wait_ge(us_s, t + 1)
                    nc.gpsimd.tensor_tensor(y[:, t, :], y[:, t, :], us[:, :], ALU.add).then_inc(added, 1)

                link = Chain(pl, pchain)
                for t in range(T):
                    if t >= G:
                        lows(t - G)
                    cut_and_add(t, link)
                for k in range(G):
                    lows(T - G + k)

            @block.vector
            def _(v):
                left = v.alloc_register(name + "_left")

                def link(ins):
                    v.drain()

                def peak(g, k):
                    i = G * g + k
                    v.wait_ge(scores, i + 1)
                    nc.vector.tensor_reduce(nmax[:, i:i + 1], L[:, :], X, ALU.max).then_inc(dve0, 1)
                    v.wait_ge(dve0, i + 1)
                    nc.vector.tensor_scalar(nmax[:, i:i + 1], nmax[:, i:i + 1], -1.0, None, ALU.mult).then_inc(peaked, 1)

                def mass(g, compare, bound, to):
                    for k in range(G):
                        nc.vector.scalar_tensor_tensor(out=void[:, k % 2, :], in0=e[:, g % 2, k, :], scalar=bound[:, k:k + 1],
                                                       in1=e[:, g % 2, k, :], op0=compare, op1=ALU.mult, accum_out=to[:, k:k + 1])
                        if k % 2:
                            v.drain()

                def together(*instructions):
                    v.drain()

                def evaluate(g):
                    mass(g, ALU.is_gt, t_, Gt)
                    together(nc.vector.tensor_tensor(b_, Gt, target, ALU.is_ge),
                             nc.vector.tensor_tensor(short, Gt, target, ALU.is_lt))
                    together(nc.vector.tensor_tensor(x_, b_, t_, ALU.mult),
                             nc.vector.scalar_tensor_tensor(out=y_, in0=b_, scalar=4.0, in1=t_, op0=ALU.mult, op1=ALU.add),
                             nc.vector.tensor_tensor(z_, short, Gt, ALU.mult),
                             nc.vector.scalar_tensor_tensor(out=w_, in0=short, scalar=4.0 * N, in1=Gt, op0=ALU.mult, op1=ALU.add))
                    together(nc.vector.tensor_tensor(lo, lo, x_, ALU.max),
                             nc.vector.tensor_tensor(hi, hi, y_, ALU.min),
                             nc.vector.tensor_tensor(m_hi, m_hi, z_, ALU.max),
                             nc.vector.tensor_tensor(m_lo, m_lo, w_, ALU.min))

                def bisect(g):
                    link(nc.vector.tensor_tensor(x_.bitcast(I32), lo.bitcast(I32), hi.bitcast(I32), ALU.add))
                    link(nc.vector.tensor_scalar(t_.bitcast(I32), x_.bitcast(I32), 0.5, None, ALU.mult))
                    evaluate(g)

                def interpolate(g):
                    together(nc.vector.tensor_tensor(x_, m_lo, m_hi, ALU.subtract),
                             nc.vector.tensor_tensor(y_, m_lo, target, ALU.subtract),
                             nc.vector.tensor_tensor(z_, hi.bitcast(I32), lo.bitcast(I32), ALU.subtract))
                    link(nc.vector.reciprocal(x_, x_))
                    link(nc.vector.tensor_tensor(x_, x_, y_, ALU.mult))
                    link(nc.vector.tensor_scalar(x_, x_, CLIP, 1.0 - CLIP, ALU.max, ALU.min))
                    link(nc.vector.tensor_tensor(x_, x_, z_, ALU.mult))
                    link(nc.vector.tensor_tensor(t_.bitcast(I32), x_, lo.bitcast(I32), ALU.add))
                    evaluate(g)

                def ties(g):
                    link(nc.vector.tensor_copy(x_, top[:, :, 7]))
                    mass(g, ALU.is_ge, x_, Gt)
                    together(nc.vector.tensor_tensor(b_, Gt, target, ALU.is_ge),
                             nc.vector.tensor_scalar(x_, x_, 1.0 - 2.0 ** -23, None, ALU.mult))
                    together(nc.vector.tensor_tensor(tie, tie, b_, ALU.max),
                             nc.vector.scalar_tensor_tensor(out=x_, in0=b_, scalar=4.0, in1=x_, op0=ALU.mult, op1=ALU.add))
                    link(nc.vector.tensor_tensor(hi, hi, x_, ALU.min))

                def look(g):
                    for k in range(G):
                        link(nc.vector.scalar_tensor_tensor(out=junk[:, :], in0=e[:, g % 2, k, :], scalar=hi[:, k:k + 1],
                                                            in1=e[:, g % 2, k, :], op0=ALU.is_le, op1=ALU.mult, accum_out=M[:, k:k + 1]))
                        link(nc.vector.max(top[:, k, :], junk[:, :]))
                    together(*[nc.vector.tensor_tensor_scan(pre[:, k, :], top[:, k, :], one[:, :], 0.0, ALU.add, ALU.mult) for k in range(G)],
                             nc.vector.tensor_tensor(x_, target, Z[:, G * g:G * g + G], ALU.subtract),
                             nc.vector.tensor_copy(kept[:, :, 0], top[:, :, 0]))
                    link(nc.vector.tensor_tensor(R, x_, M, ALU.add))
                    together(*[nc.vector.tensor_scalar(kept[:, k, 1:8], pre[:, k, 0:7], R[:, k:k + 1], 4.0, ALU.is_ge, ALU.mult) for k in range(G)],
                             nc.vector.tensor_tensor(done, pre[:, :, 7], R, ALU.is_ge))
                    together(nc.vector.tensor_tensor(kept[:, :, 1:8], kept[:, :, 1:8], top[:, :, 1:8], ALU.add),
                             nc.vector.tensor_tensor(done, done, tie, ALU.max))
                    link(nc.vector.tensor_reduce(tstar, kept[:, :, :], X, ALU.min))
                    link(nc.vector.tensor_reduce(und[:, 0:1], done, X, ALU.min))
                    link(nc.vector.tensor_scalar(und[:, 0:1], und[:, 0:1], -1.0, 1.0, ALU.mult, ALU.add))
                    link(nc.vector.transpose(undT[:, :], und[:, :]))
                    link(nc.vector.tensor_reduce(und[:, 0:1], undT[:, :], X, ALU.max))
                    together(*[nc.vector.tensor_copy(cell[0:1, q:q + 1], und[32 * q:32 * q + 1, 0:1]) for q in range(4)])
                    link(nc.vector.tensor_reduce(cell[0:1, 4:5], cell[0:1, 0:4], X, ALU.max))
                    link(nc.vector.tensor_copy(flag[0:1, 0:1], cell[0:1, 4:5]))

                def search(g):
                    v.wait_ge(exped, G * g + G)
                    link(nc.vector.tensor_scalar(target, Z[:, G * g:G * g + G], P_NUC, None, ALU.mult))
                    link(nc.vector.tensor_scalar(lo, Z[:, G * g:G * g + G], (1 - P_NUC) * 0.999 / N, None, ALU.mult))
                    link(nc.vector.memset(hi, 1.001))
                    link(nc.vector.memset(tie, 0.0))
                    link(nc.vector.tensor_copy(m_lo, Z[:, G * g:G * g + G]))
                    link(nc.vector.memset(m_hi, 0.0))
                    for n, cut in enumerate(CUTS):
                        (bisect if cut == "b" else interpolate)(g)
                        if n % 2 and g + 1 < GROUPS:
                            peak(g + 1, n // 2)
                    look(g)
                    v.reg_load(left, flag[0:1, 0:1])
                    with v.If(v.snap(left) > 0):
                        ties(g)
                        look(g)
                        v.reg_load(left, flag[0:1, 0:1])
                    with v.While(lambda: v.snap(left) > 0):
                        ties(g)
                        bisect(g)
                        look(g)
                        v.reg_load(left, flag[0:1, 0:1])
                    for k in range(G):
                        i = G * g + k
                        nc.vector.scalar_tensor_tensor(out=e[:, g % 2, k, :], in0=e[:, g % 2, k, :], scalar=tstar[:, k:k + 1],
                                                       in1=e[:, g % 2, k, :], op0=ALU.is_ge, op1=ALU.mult, accum_out=rs[:, i:i + 1])
                    v.drain()
                    link(nc.vector.reciprocal(rs[:, G * g:G * g + G], rs[:, G * g:G * g + G]))
                    nc.vector.tensor_scalar(rs[:, G * g:G * g + G], rs[:, G * g:G * g + G], 1.0 / (P_SCALE * X_SCALE), None,
                                            ALU.mult).then_inc(masked_s, G)
                    v.wait_ge(masked_s, G * g + G)

                nc.vector.tensor_scalar(rsc[:, 0, :], scales[:, 0, :], 1.0 / (X_SCALE * A_SCALE), None, ALU.mult).then_inc(rsc_s, 1)
                nc.vector.tensor_scalar(rsc[:, 1, :], scales[:, 1, :], 1.0 / (X_SCALE * A_SCALE) if step == 0 else sc[:, 7:8],
                                        1.0 if step == 0 else 1.0 / A_SCALE, ALU.mult, ALU.mult).then_inc(rsc_s, 1)
                link(nc.vector.memset(one[:, :], 1.0))
                link(nc.vector.memset(und[:, :], 0.0))
                for k in range(G):
                    peak(0, k)
                for g in range(GROUPS):
                    search(g)


def finish(nc, sb, ps, sem, acc, out):
    stored = sem("out_stored")
    block = nc.Block()
    with block:
        @block.sync
        def _(sp):
            for q in range(2):
                sp.dma_start(nodes(out)[:, :, q, :], acc[:, :, :].rearrange("p (c q) d -> p c q d", q=2)[:, :, q, :]).then_inc(stored, 16)
            sp.wait_ge(stored, 32)


_INS = ["x", "adj", "L0_gnn_Wq", "L0_gnn_Wk", "L0_gnn_Wv", "L0_gnn_Wout", "L1_gnn_W1", "L1_gnn_W2", "L1_gnn_W3", "L1_gnn_U1",
        "L1_gnn_U2", "L1_gnn_U3", "L1_gnn_gamma", "L1_gnn_beta", "L2_gnn_W", "L2_gnn_b", "L3_gnn_weight"]


def kernel(**inputs):
    import numpy as _np
    import concourse.bacc as _bacc
    from concourse import mybir as _mybir
    from concourse.bass_utils import run_bass_kernel_spmd as _run

    nc = _bacc.Bacc("TRN2", target_bir_lowering=False, num_devices=1)
    arrays, args = {}, {}
    for name in _INS:
        a = _np.ascontiguousarray(inputs[name])
        arrays[f"in_{name}_dram"] = a
        args[name] = nc.dram_tensor(f"in_{name}_dram", a.shape, _mybir.dt.from_np(a.dtype), kind="ExternalInput").ap()
    out = nc.dram_tensor("out_0_dram", (N, D), F32, kind="ExternalOutput").ap()
    build(nc, args, out)
    r = _run(nc, [arrays], core_ids=[0])
    return r.results[0]["out_0_dram"]
```

```python
from contextlib import ExitStack

import concourse.bass as bass
from concourse import mybir

F32 = mybir.dt.float32
F16 = mybir.dt.float16
BF16 = mybir.dt.bfloat16
I32 = mybir.dt.int32
U32 = mybir.dt.uint32
ALU = mybir.AluOpType
ACT = mybir.ActivationFunctionType
X = mybir.AxisListType.X
ABSMAX = bass.bass_isa.ReduceOp.absmax
ds = bass.ds

P = 128
N, D, HEADS = 2048, 256, 8
T = N // P
KC = D // P
CH = N // (N // HEADS)
ROWS = N // HEADS
BANK = 512
MASKED = -1.0e6
FAR = -2.0 ** 100
H_SCALE = 16.0
P_SCALE = 32768.0
VW_SCALE = 2.0 ** -7
LN_EPS = 1e-5
LO_GAIN = 2048.0
DEG_SCALE = 0.25
A_SCALE = 64.0
X_SCALE = 1024.0
P_NUC = 0.9
G = 4
CUTS = 7
CLIP = 0.3
PEAK_AFTER = (1, 3, 4, 6)
BW = N + 8


class Chain:

    def __init__(self, engine, sem, base=0):
        self.engine, self.sem, self.base, self.n = engine, sem, base, 0

    def __call__(self, ins):
        self.note(ins)
        self.wait()

    def wait(self):
        self.engine.wait_ge(self.sem, self.base + self.n)

    def note(self, ins):
        self.n += 1
        ins.then_inc(self.sem, 1)


def nodes(ap):
    return ap.rearrange("(q p c) d -> p c q d", q=2, p=P, c=CH)


def permuted(ap):
    return ap.rearrange("p (r c) -> p c r", c=CH)


def in_order(ap):
    return ap.rearrange("d (q p c) -> d c q p", q=2, p=P, c=CH)


def normalize_stats(nc, eng, chain, x, stats, mv):
    for t in range(T):
        chain.note(nc.vector.bn_stats(stats[:, t, :], x[:, t, :]))
    chain.wait()
    for t in range(T):
        chain.note(nc.vector.bn_aggr(mv[:, t, :], stats[:, t, :]))
    chain.wait()


def build(nc, a, out):
    g = ExitStack()

    def sb(stack, name, shape, dt=F32):
        return stack.enter_context(nc.sbuf_tensor(name, shape, dt))

    def ps(stack, name, shape, dt=F32):
        return stack.enter_context(nc.psum_tensor(name, shape, dt))

    with g:
        def phase(run, *args, **kwargs):
            own = []

            def sem(name):
                own.append(nc.alloc_semaphore(name))
                return own[-1]

            run(nc, sb, ps, sem, *args, **kwargs)
            nc.clear_and_free_semaphores(own)
            nc.all_engine_barrier()

        bias_d = nc.dram_tensor("bias_scratch", (T, P, BW), F32, kind="Internal").ap()
        at_d = nc.dram_tensor("adjT_scratch", (T, P, 2 * N), F16, kind="Internal").ap()

        x_d = nc.dram_tensor("x_scratch", (P, T, D), F32, kind="Internal").ap()

        acc = sb(g, "acc", [P, T, D])
        ident = sb(g, "ident", [P, P])
        am = sb(g, "am", [P, 4])
        winv = sb(g, "winv", [P, 4])
        sc = sb(g, "sc", [P, 8])
        halfp = sb(g, "halfp", [P, T])
        deg = sb(g, "deg", [P, 2, T])

        with ExitStack() as c:
            WH = [sb(c, f"w{n}_hi", [P, KC, N], F16) for n in "qkv"]
            WL = [sb(c, f"w{n}_lo", [P, KC, N], F16) for n in "qkv"]
            hT_hi = sb(c, "hT_hi", [P, KC, N], F16)
            hT_lo = sb(c, "hT_lo", [P, KC, N], F16)
            phase(setup, a, bias_d, acc, ident, am, winv, sc, halfp, WH, WL, hT_hi, hT_lo)
            phase(adjacency, a["adj"], bias_d, at_d, sc, ident, deg)
            phase(attend, a["L0_gnn_Wout"], bias_d, acc, ident, winv, sc, WH, WL, hT_hi, hT_lo)

        scales = sb(g, "scales", [P, 4, T])
        ident16 = sb(g, "ident16", [P, P], BF16)
        with ExitStack() as c:
            w1, w3 = sb(c, "w1", [P, KC, 64]), sb(c, "w3", [P, KC, 64])
            w2 = sb(c, "w2", [64, 64])
            gb = sb(c, "gamma_beta", [P, 2, D])
            Y = sb(c, "y", [P, T, D])
            XA = acc
            phase(prepare, a, deg, scales, ident, ident16, halfp, w1, w2, w3, gb, sc, acc, x_d)
            with ExitStack() as c1:
                Xp = [sb(c1, f"x_{n}", [P, T, D], F16) for n in ("hi", "lo")]
                Xf = [sb(c1, f"xf_{n}", [P, T, D], F16) for n in ("hi", "lo")]
                Xb = [sb(c1, f"xb_{n}", [P, T, D], F16) for n in ("hi", "lo")]
                QT, KT = sb(c1, "logit_q", [64, N]), sb(c1, "logit_k", [64, N])
                for step in range(2):
                    X_ = (Y, XA)[step]
                    phase(refresh, f"qk{step}", acc if step == 0 else XA, X_, ident, halfp, norm=(step == 0),
                          logits=(w1, w2, w3, QT, KT), parts=Xp, rows=X_SCALE)
                    phase(nucleus, f"nuc{step}", QT, KT, Xp, XA, ident,
                          ([a["L1_gnn_U1"][step], a["L1_gnn_U2"][step]] + [a["L1_gnn_U3"][0]] * step, at_d, scales, ident16, Y, sc,
                           Xp, Xf, Xb, step))
                phase(refresh, "u3", XA, XA, ident, halfp, weight=a["L1_gnn_U3"][1], onto=Y)
            phase(normalize_onto, "l1out", Y, halfp, gb, acc, x_d)
        with ExitStack() as c:
            H = sb(c, "h", [P, T, D])
            wT = sb(c, "l2_wT", [P, KC, D])
            bb = sb(c, "l2_bias", [P, D])
            l2_in, l3_in, l3_out = (sb(c, n, [P, T]) for n in ("l2_in", "l3_in", "l3_out"))
            Hq = [sb(c, f"h_{n}", [P, T, D], F16) for n in ("hi", "lo")]
            phase(last_weights, a, ident, wT, bb, scales, l2_in, l3_in, l3_out)
            phase(refresh, "l2h", acc, H, ident, halfp, norm=True, parts=Hq, rows=l2_in[:, :], bias=(acc, bb), lo_gain=LO_GAIN)
            phase(diffuse, "l2d", at_d, ident, None, acc, Hq, DEG_SCALE, scales[:, 2, :], wT, LO_GAIN)
            phase(refresh, "l3h", acc, H, ident, halfp, norm=True, weight=a["L3_gnn_weight"], parts=Hq, rows=l3_in[:, :])
            phase(diffuse, "l3d", at_d, ident, ident16, acc, Hq, 1.0, l3_out[:, :], None, None)
        phase(finish, acc, out)


def setup(nc, sb, ps, sem, a, bias_d, acc, ident, am, winv, sc, halfp, WH, WL, hT_hi, hT_lo):
    w_loaded = [sem(f"{w}_loaded") for w in ("wq", "wk", "wv", "wout")]
    x_loaded, rest_loaded = sem("x_loaded"), sem("rest_loaded")
    dve, pool = sem("setup_dve"), sem("setup_pool")
    extremes, largest, powers, w_hi, stats_done = sem("extremes"), sem("largest"), sem("powers"), sem("w_hi"), sem("stats_done")
    rstd_done, centred, rectified, h_tp, h_hi, h_lo = (sem(s) for s in ("rstd_done", "centred", "rectified", "h_tp", "h_hi", "h_lo"))
    ident_made = sem("ident_made")
    with ExitStack() as c:
        stage = [sb(c, f"w_stage{n}", [P, KC, N]) for n in range(3)]
        hx = sb(c, "hx", [P, T, D])
        stats, mv = sb(c, "stats", [P, T, 6]), sb(c, "mv", [P, T, 2])
        rstd = sb(c, "rstd", [P, T])
        ext = sb(c, "ext", [P, 8])
        wo = acc
        tp = [ps(c, f"h_tp{n}", [P, BANK]) for n in range(2)]

        block = nc.Block()
        with block:
            @block.sync
            def _(sp):
                sp.dma_start(hx[:, :, :], a["x"].rearrange("(t p) d -> p t d", p=P)).then_inc(x_loaded, 16)
                for n, w in enumerate(("Wq", "Wk", "Wv")):
                    sp.dma_start(stage[n][:, :, :], a["L0_gnn_" + w].rearrange("(k p) n -> p k n", p=P)).then_inc(w_loaded[n], 16)
                sp.dma_start(wo[:, :, :], a["L0_gnn_Wout"].rearrange("(t p) d -> p t d", p=P)).then_inc(w_loaded[3], 16)
                sp.wait_ge(extremes, 1)
                for q in range(2):
                    sp.dma_start(acc[:, :, :].rearrange("p (c q) d -> p c q d", q=2)[:, :, q, :],
                                 nodes(a["x"])[:, :, q, :]).then_inc(rest_loaded, 16)
                sp.wait_ge(rest_loaded, 32)

            @block.gpsimd
            def _(pl):
                nc.gpsimd.memset(ident[:, :], 0.0).then_inc(pool, 1)
                pl.wait_ge(pool, 1)
                nc.gpsimd.affine_select(out=ident[:, :], in_=ident[:, :], compare_op=ALU.not_equal, fill=1.0, base=0,
                                        pattern=[[-1, P]], channel_multiplier=1).then_inc(ident_made, 1)
                nc.gpsimd.memset(halfp[:, :], -0.5).then_inc(pool, 1)
                pl.wait_ge(stats_done, 1)
                nc.gpsimd.tensor_scalar(rstd[:, :], mv[:, :, 1], LN_EPS, None, ALU.add).then_inc(pool, 1)
                pl.wait_ge(pool, 3)
                nc.gpsimd.tensor_tensor(rstd[:, :], rstd[:, :], halfp[:, :], ALU.pow).then_inc(rstd_done, 1)
                pl.wait_ge(extremes, 1)
                nc.gpsimd.partition_all_reduce(am[:, :], ext[:, 0:4], P, ABSMAX).then_inc(largest, 1)

            @block.vector
            def _(v):
                link = Chain(v, dve)
                v.wait_ge(x_loaded, 16)
                normalize_stats(nc, v, link, hx, stats, mv)
                nc.vector.memset(ext[:, :], 0.0).then_inc(stats_done, 1)
                v.wait_ge(rstd_done, 1)
                v.wait_ge(stats_done, 1)
                for t in range(T):
                    nc.vector.tensor_scalar(hx[:, t, :], hx[:, t, :], mv[:, t, 0:1], rstd[:, t:t + 1],
                                            ALU.subtract, ALU.mult).then_inc(centred, 1)
                for n in range(4):
                    v.wait_ge(w_loaded[n], 16)
                    w = stage[n][:, :, :] if n < 3 else wo[:, :, :]
                    link.note(nc.vector.tensor_reduce(ext[:, 4 + n:5 + n], w, mybir.AxisListType.XY, ALU.max, apply_absolute_value=True))
                link.wait()
                nc.vector.tensor_scalar(ext[:, 0:4], ext[:, 4:8], 1e-30, None, ALU.max).then_inc(extremes, 1)
                v.wait_ge(largest, 1)
                link(nc.vector.tensor_scalar(am[:, :].bitcast(U32), am[:, :].bitcast(U32), 0x7F800000, None, ALU.bitwise_and))
                nc.vector.reciprocal(winv[:, :], am[:, :]).then_inc(powers, 1)
                link(nc.vector.tensor_scalar(sc[:, 0:1], am[:, 0:1], am[:, 1:2], 2.0 ** -12, ALU.mult, ALU.mult))
                link(nc.vector.tensor_scalar(sc[:, 1:2], sc[:, 0:1], -1.0, None, ALU.mult))
                link(nc.vector.tensor_scalar(sc[:, 4:5], am[:, 2:3], am[:, 3:4], 2.0 ** -12, ALU.mult, ALU.mult))
                link(nc.vector.reciprocal(sc[:, 5:6], sc[:, 0:1]))
                link(nc.vector.tensor_scalar(sc[:, 2:3], sc[:, 5:6], 2.0, None, ALU.mult))
                link(nc.vector.tensor_scalar(sc[:, 3:4], sc[:, 5:6], MASKED, None, ALU.mult))
                v.wait_ge(powers, 1)
                for n in range(3):
                    v.wait_ge(w_hi, n + 1)
                    link(nc.vector.scalar_tensor_tensor(out=WL[n][:, :, :], in0=stage[n][:, :, :], scalar=winv[:, n:n + 1],
                                                        in1=WH[n][:, :, :], op0=ALU.mult, op1=ALU.subtract))
                for b in range(2 * T // 4):
                    k, t0 = b % KC, b // KC * BANK
                    v.wait_ge(h_hi, b + 1)
                    nc.vector.tensor_tensor(hT_lo[:, k, t0:t0 + BANK], tp[b % 2][:, :], hT_hi[:, k, t0:t0 + BANK],
                                            ALU.subtract).then_inc(h_lo, 1)

            @block.scalar
            def _(s):
                for t in range(T):
                    s.wait_ge(centred, t + 1)
                    nc.scalar.activation(hx[:, t, :], hx[:, t, :], ACT.Relu, scale=H_SCALE).then_inc(rectified, 1)
                s.wait_ge(powers, 1)
                for n in range(3):
                    nc.scalar.activation(WH[n][:, :, :], stage[n][:, :, :], ACT.Copy, scale=winv[:, n:n + 1]).then_inc(w_hi, 1)
                for b in range(2 * T // 4):
                    k, t0 = b % KC, b // KC * BANK
                    s.wait_ge(h_tp, b + 1)
                    nc.scalar.activation(hT_hi[:, k, t0:t0 + BANK], tp[b % 2][:, :], ACT.Copy).then_inc(h_hi, 1)

            @block.tensor
            def _(pe):
                pe.wait_ge(ident_made, 1)
                pe.wait_ge(rectified, T)
                for b in range(2 * T // 4):
                    k, t0 = b % KC, b // KC * 4
                    if b >= 2:
                        pe.wait_ge(h_lo, b - 1)
                    for t in range(4):
                        last = nc.tensor.transpose(tp[b % 2][:, t * P:(t + 1) * P], hx[:, t0 + t, k * P:(k + 1) * P], ident[:, :])
                    last.then_inc(h_tp, 1)


def adjacency(nc, sb, ps, sem, adj, bias_d, at_d, sc, ident, deg):
    loaded = [sem(f"adj_loaded{q}") for q in range(2)]
    (doubled, zeroed, made, dve, tposed, hi_done, lo_done, summed) = (
        sem("adj_" + s) for s in ("doubled", "zeroed", "made", "dve", "tposed", "hi", "lo", "summed"))
    stored = [sem(f"bias_stored{q}") for q in range(2)]
    at_stored = [sem(f"at_stored{q}") for q in range(2)]
    rows = adj.rearrange("(q p c) m -> c q p m", q=2, p=P, c=CH)
    with ExitStack() as c:
        A = [sb(c, f"adj_rows{q}", [P, N]) for q in range(2)]
        W = [sb(c, f"adj_twice{q}", [P, N]) for q in range(2)]
        E = sb(c, "adj_zero", [P, N])
        masks = sb(c, "adj_masks", [P, 1])
        B = [sb(c, f"adj_bias{q}", [P, BW]) for q in range(2)]
        AT = [sb(c, f"adjT{q}", [P, 2, T, P], F16) for q in range(2)]
        col = sb(c, "col_parts", [P, T, T])
        twice = sb(c, "row_twice", [P, T])
        TP = [ps(c, f"adj_tp{n}", [P, BANK]) for n in range(4)]
        FREE = 2
        block = nc.Block()
        with block:
            @block.sync
            def _(sp):
                def store(i, q):
                    sp.wait_ge(made, 2 * i + q + 1 + FREE)
                    sp.dma_start(bias_d[ds(2 * i + q, 1), :, :].rearrange("a p m -> p (a m)"), B[q][:, :]).then_inc(stored[q], 16)
                    sp.wait_ge(lo_done, 8 * i + 4 * q + 4 + 4)
                    sp.dma_start(at_d[ds(2 * i + q, 1), :, :].rearrange("a p m -> p (a m)"),
                                 AT[q][:, :, :, :].rearrange("p x m n -> p (x m n)")).then_inc(at_stored[q], 16)

                for q in range(2):
                    sp.dma_start(A[q][:, :], rows[0, q, :, :]).then_inc(loaded[q], 16)
                with sp.Fori(0, CH) as i:
                    for q in range(2):
                        store(i, q)
                for q in range(2):
                    sp.wait_ge(stored[q], 16 * CH + 16)
                    sp.wait_ge(at_stored[q], 16 * CH + 16)

            @block.tensor
            def _(pe):
                with pe.Fori(0, CH) as i:
                    for q in range(2):
                        pe.wait_ge(loaded[q], 16 * i + 16)
                        rows_q = permuted(A[q][:, :])
                        for b in range(4):
                            pe.wait_ge(lo_done, 8 * i + 4 * q + b + 1)
                            for m in range(4):
                                t = 4 * b + m
                                last = nc.tensor.transpose(TP[b][:, m * P:(m + 1) * P], rows_q[:, t // 2, t % 2 * P:(t % 2 + 1) * P], ident[:, :])
                            last.then_inc(tposed, 1)

            @block.scalar
            def _(s):
                def tile(i, q):
                    s.wait_ge(loaded[q], 16 * i + 16)
                    s.wait_ge(made, 2 * i + q + 1)
                    nc.scalar.activation(W[q][:, :], A[q][:, :], ACT.Copy, scale=sc[:, 2:3],
                                         accum_out=twice[:, ds(2 * i + q, 1)]).then_inc(doubled, 1)
                    s.wait_ge(at_stored[q], 16 * i + 16)
                    for b in range(4):
                        s.wait_ge(tposed, 8 * i + 4 * q + b + 1)
                        nc.scalar.activation(AT[q][:, 0, 4 * b:4 * b + 4, :].rearrange("p a b -> p (a b)"), TP[b][:, :], ACT.Copy,
                                             scale=A_SCALE).then_inc(hi_done, 1)

                with s.Fori(0, CH - 1) as i:
                    for q in range(2):
                        tile(i, q)
                        s.wait_ge(doubled, 2 * i + q + 1)
                        s.wait_ge(zeroed, 2 * i + q + 1)
                        s.dma_start(A[q][:, :], rows[ds(i + 1, 1), q, :, :].rearrange("a p m -> p (a m)")).then_inc(loaded[q], 16)
                for q in range(2):
                    tile(CH - 1, q)

            @block.vector
            def _(v):
                for q in range(2):
                    nc.vector.memset(B[q][:, N:BW], 0.0).then_inc(made, 1)
                v.wait_ge(made, FREE)
                for q in range(2):
                    nc.vector.memset(B[q][:, N:BW], 0.0).then_inc(stored[q], 16)
                    v.wait_ge(stored[q], 16)
                    nc.vector.memset(B[q][:, N:BW], 0.0).then_inc(at_stored[q], 16)
                    v.wait_ge(at_stored[q], 16)
                nc.vector.memset(B[0][:, N:BW], 0.0).then_inc(lo_done, 4)
                v.wait_ge(lo_done, 4)
                with v.Fori(0, CH) as i:
                    link = Chain(v, dve, i * 16)
                    for q in range(2):
                        v.wait_ge(stored[q], 16 * i + 16)
                        v.wait_ge(loaded[q], 16 * i + 16)
                        nc.vector.tensor_scalar(E[:, :], A[q][:, :], 0.0, FAR, ALU.is_equal, ALU.mult).then_inc(zeroed, 1)
                        v.wait_ge(zeroed, 2 * i + q + 1)
                        v.wait_ge(doubled, 2 * i + q + 1)
                        link.note(nc.vector.scalar_tensor_tensor(out=B[q][:, 0:N].rearrange("p (c r) -> p c r", c=CH),
                                                                 in0=permuted(E[:, :]), scalar=0.0, in1=permuted(W[q][:, :]),
                                                                 op0=ALU.add, op1=ALU.add, accum_out=masks[:, :]))
                        for b in range(4):
                            v.wait_ge(hi_done, 8 * i + 4 * q + b + 1)
                            link.note(nc.vector.tensor_reduce(col[:, 4 * b:4 * b + 4, ds(2 * i + q, 1)].rearrange("p m a -> p (m a)"),
                                                              TP[b][:, :].rearrange("p (m n) -> p m n", m=4), X, ALU.add))
                            nc.vector.scalar_tensor_tensor(out=AT[q][:, 1, 4 * b:4 * b + 4, :].rearrange("p a b -> p (a b)"), in0=TP[b][:, :],
                                                           scalar=A_SCALE, in1=AT[q][:, 0, 4 * b:4 * b + 4, :].rearrange("p a b -> p (a b)"),
                                                           op0=ALU.mult, op1=ALU.subtract).then_inc(lo_done, 1)
                        link.wait()
                        link(nc.vector.tensor_scalar(masks[:, :], masks[:, :], 1.0 / FAR, None, ALU.mult))
                        link(nc.vector.scalar_tensor_tensor(out=B[q][:, N + 1:N + 2], in0=masks[:, :], scalar=0.5, in1=masks[:, :],
                                                            op0=ALU.is_ge, op1=ALU.mult))
                        link(nc.vector.tensor_scalar(B[q][:, N:N + 1], B[q][:, N + 1:N + 2], 0.0, FAR, ALU.is_equal, ALU.mult))
                        nc.vector.tensor_scalar(B[q][:, N:N + 1], B[q][:, N:N + 1], sc[:, 3:4], None, ALU.add).then_inc(made, 1)
                v.wait_ge(lo_done, 4 * T + 4)
                nc.vector.tensor_reduce(deg[:, 1, :], col[:, :, :], X, ALU.add).then_inc(summed, 1)
                nc.vector.tensor_scalar(deg[:, 0, :], twice[:, :], sc[:, 0:1], 0.5, ALU.mult, ALU.mult).then_inc(summed, 1)


def attend(nc, sb, ps, sem, wout, bias_d, acc, ident, winv, sc, WH, WL, hT_hi, hT_lo):
    (wo_loaded, wo_hi_s, wo_lo_s, proj, proj_hi, bank_free, scores, logits_read, bias_loaded, maxed, exped, tposed,
     pt_hi, pt_free, av_done, av_free, chain) = (sem("att_" + s) for s in (
        "wo_loaded", "wo_hi", "wo_lo", "proj", "proj_hi", "bank_free", "scores", "logits_read", "bias_loaded", "maxed",
        "exped", "tposed", "pt_hi", "pt_free", "av_done", "av_free", "chain"))
    bias_par = [bias_loaded, sem("att_bias_loaded1")]
    BANKS_FREE, READS_FREE, PT_FREE, AV_FREE = 4, 4, 2, 2
    BATCHES, PER_HEAD = 8, 32
    wo_rows = wout.rearrange("(h k p) d -> h p k d", k=KC, p=P)

    with ExitStack() as c:
        VT = [sb(c, f"vT_{n}", [P, KC, N], F16) for n in ("hi", "lo")]
        QT = [sb(c, f"qT_{n}", [P, KC, N], F16) for n in ("hi", "lo")]
        KT = [sb(c, f"kT_{n}", [P, KC, N], F16) for n in ("hi", "lo")]
        VW = [sb(c, f"vw_{n}", [P, T, D], F16) for n in ("hi", "lo")]
        WO = [sb(c, f"wo_{n}", [P, KC, D], F16) for n in ("hi", "lo")]
        wo_st = sb(c, "wo_stage", [P, KC, D])
        B = [sb(c, f"bias{n}", [P, BW]) for n in range(2)]
        E = [sb(c, f"e{n}", [P, N]) for n in range(2)]
        PT = [sb(c, f"pT_{n}", [P, T, P], F16) for n in ("hi", "lo")]
        small = sb(c, "att_small", [P, 2, 8])
        minus = sb(c, "minus", [P, 1])
        L = [ps(c, f"logits{n}", [P, 2 * BANK]) for n in range(2)]
        TP = [ps(c, f"tp{n}", [P, BANK]) for n in range(2)]
        AV = [ps(c, f"av{n}", [P, D]) for n in range(2)]
        bank = [L[b // 2][:, b % 2 * BANK:(b % 2 + 1) * BANK] for b in range(4)]
        kinds = [(2, VT), (1, KT), (0, QT), None]

        def m0(par): return small[:, par, 0:1]
        def m1(par): return small[:, par, 1:2]
        def nb(par): return small[:, par, 2:3]
        def ssum(par): return small[:, par, 3:4]
        def masked(par): return small[:, par, 4:5]
        def r(par): return small[:, par, 5:6]

        block = nc.Block()
        with block:
            @block.sync
            def _(sp):
                with sp.Fori(0, HEADS) as h:
                    sp.wait_ge(wo_lo_s, h + 1)
                    sp.dma_start(wo_st[:, :, :], wo_rows[ds(h, 1), :, :, :].rearrange("a p k d -> p (a k) d")).then_inc(wo_loaded, 16)
                    with sp.Fori(0, T // 2) as j:
                        for par in range(2):
                            i = 16 * h + 2 * j + par
                            sp.wait_ge(logits_read, 2 * i + 2)
                            sp.dma_start(B[par][:, :], bias_d[ds(2 * j + par, 1), :, :].rearrange("a p m -> p (a m)")).then_inc(bias_par[par], 16)

            @block.tensor
            def _(pe):
                def project(h, n):
                    kind = kinds[n]
                    with pe.Fori(0, 2) as u:
                        if n == 0:
                            pe.wait_ge(logits_read, 32 * h + READS_FREE)
                        if n == 3:
                            pe.wait_ge(wo_hi_s, h + 1)
                            pe.wait_ge(wo_lo_s, h + 2)
                            pe.wait_ge(logits_read, 32 * h + 2 + READS_FREE)
                        for b in range(4):
                            pe.wait_ge(bank_free, PER_HEAD * h + 8 * n + 4 * u + b + 1)
                            if kind is None:
                                for m in range(2):
                                    o = bank[b][:, m * D:(m + 1) * D]
                                    for k in range(KC):
                                        for w, x in ((0, 0), (0, 1), (1, 0)):
                                            last = nc.tensor.matmul(o, VT[w][:, k, ds((4 * u + b) * 2 * P + m * P, P)], WO[x][:, k, :],
                                                                    start=(k == 0 and w == x == 0), stop=(k == 1 and w == 1))
                            else:
                                for m in range(2):
                                    o = bank[b][:, m * ROWS:(m + 1) * ROWS]
                                    for k in range(KC):
                                        for w, x in ((0, 0), (0, 1), (1, 0)):
                                            W = (WH, WL)[w][kind[0]]
                                            hT = (hT_hi, hT_lo)[x]
                                            last = nc.tensor.matmul(o, W[:, k, ds((4 * u + b) * D + m * P, P)], hT[:, k, ds(h * ROWS, ROWS)],
                                                                    start=(k == 0 and w == x == 0), stop=(k == 1 and w == 1))
                            last.then_inc(proj, 1)
                    if n == 2:
                        pe.wait_ge(bank_free, PER_HEAD * h + 8 * 3 + BANKS_FREE)

                def qk(i, t, half):
                    pe.wait_ge(logits_read, 2 * i + half + READS_FREE - 1)
                    for b in range(2):
                        o = L[half][:, b * BANK:(b + 1) * BANK]
                        c0 = half * 2 * BANK + b * BANK
                        for k in range(KC):
                            for w, x in ((0, 0), (0, 1), (1, 0)):
                                last = nc.tensor.matmul(o, QT[w][:, k, ds(t * P, P)], KT[x][:, k, c0:c0 + BANK],
                                                        start=(k == 0 and w == x == 0), stop=(k == 1 and w == 1))
                    last.then_inc(scores, 1)

                def turn(i, par, q):
                    if q == 0:
                        pe.wait_ge(exped, i + 1)
                    pe.wait_ge(pt_free, 4 * i + q + 1)
                    for m in range(4):
                        last = nc.tensor.transpose(TP[q % 2][:, m * P:(m + 1) * P], E[par][:, (4 * q + m) * P:(4 * q + m + 1) * P], ident[:, :])
                    last.then_inc(tposed, 1)

                def av(i, par, q):
                    pe.wait_ge(pt_free, 4 * i + q + 1 + PT_FREE)
                    if q == 0:
                        pe.wait_ge(av_free, i + 1)
                    for m in range(4 * q, 4 * q + 4):
                        for w, x in ((0, 0), (0, 1), (1, 0)):
                            last = nc.tensor.matmul(AV[par][:, :], PT[w][:, m, :], VW[x][:, m, :],
                                                    start=(m == 0 and w == x == 0), stop=(m == T - 1 and w == 1))
                    if q == 3:
                        last.then_inc(av_done, 1)

                def item(i, t, par, more):
                    after = (t + 1) % T if isinstance(t, int) else t + 1
                    if more:
                        qk(i + 1, after, 0)
                    turn(i, par, 0)
                    turn(i, par, 1)
                    if more:
                        qk(i + 1, after, 1)
                    av(i, par, 0)
                    turn(i, par, 2)
                    av(i, par, 1)
                    turn(i, par, 3)
                    av(i, par, 2)
                    av(i, par, 3)

                def items(h):
                    with pe.Fori(0, T // 2 - 1) as j:
                        pe.wait_ge(bank_free, PER_HEAD * (h + 1) + BANKS_FREE)
                        item(16 * h + 2 * j, 2 * j, 0, True)
                        item(16 * h + 2 * j + 1, 2 * j + 1, 1, True)
                    item(16 * h + T - 2, T - 2, 0, True)

                for n in range(3):
                    project(0, n)
                qk(0, 0, 0)
                qk(0, 0, 1)
                project(0, 3)
                with pe.Fori(0, HEADS - 1) as h:
                    items(h)
                    for n in range(3):
                        project(h + 1, n)
                    item(16 * h + T - 1, T - 1, 1, True)
                    project(h + 1, 3)
                items(HEADS - 1)
                item(16 * HEADS - 1, T - 1, 1, False)

            def evacuated(kind, n, m):
                if kind is None:
                    return [VW[x][:, ds(2 * m, 2), :] for x in range(2)]
                return [kind[1][x][:, :, ds(m * ROWS, ROWS)] for x in range(2)]

            @block.scalar
            def _(s):
                def hi(i, q):
                    s.wait_ge(tposed, 4 * i + q + 1)
                    nc.scalar.activation(PT[0][:, 4 * q:4 * q + 4, :].rearrange("p a b -> p (a b)"), TP[q % 2][:, :], ACT.Copy,
                                         scale=P_SCALE).then_inc(pt_hi, 1)

                def exp(i, par):
                    s.wait_ge(maxed, i + 1)
                    nc.scalar.activation(masked(par), nb(par), ACT.Exp, bias=minus[:, 0:1], scale=1.0)
                    nc.scalar.activation(E[par][:, :], E[par][:, :], ACT.Exp, bias=nb(par), scale=sc[:, 0:1],
                                         accum_out=ssum(par)).then_inc(exped, 1)

                def evacuate(h, n):
                    with s.Fori(0, 2) as u:
                        for b in range(4):
                            s.wait_ge(proj, PER_HEAD * h + 8 * n + 4 * u + b + 1)
                            nc.scalar.activation(evacuated(kinds[n], n, 4 * u + b)[0], bank[b].rearrange("p (a b) -> p a b", a=2), ACT.Copy,
                                                 scale=VW_SCALE if n == 3 else 1.0).then_inc(proj_hi, 1)

                def begin(h):
                    s.wait_ge(wo_loaded, 16 * (h + 1))
                    nc.scalar.activation(WO[0][:, :, :], wo_st[:, :, :], ACT.Copy, scale=winv[:, 3:4]).then_inc(wo_hi_s, 1)
                    for n in range(3):
                        evacuate(h, n)

                def items(h):
                    with s.Fori(0, T // 2 - 1) as j:
                        for par in range(2):
                            i = 16 * h + 2 * j + par
                            for q in range(4):
                                hi(i, q)
                            exp(i + 1, 1 - par)
                    for q in range(4):
                        hi(16 * h + T - 2, q)
                    exp(16 * h + T - 1, 1)

                begin(0)
                exp(0, 0)
                evacuate(0, 3)
                with s.Fori(0, HEADS - 1) as h:
                    items(h)
                    begin(h + 1)
                    for q in range(4):
                        hi(16 * h + T - 1, q)
                    exp(16 * h + T, 0)
                    evacuate(h + 1, 3)
                items(HEADS - 1)
                for q in range(4):
                    hi(16 * HEADS - 1, q)

            @block.vector
            def _(v):
                nc.vector.memset(minus[:, :], MASKED).then_inc(bank_free, BANKS_FREE)
                nc.vector.memset(small[:, :, :], 0.0).then_inc(wo_lo_s, 1)
                v.wait_ge(wo_lo_s, 1)
                v.wait_ge(bank_free, BANKS_FREE)
                nc.vector.memset(small[:, :, :], 0.0).then_inc(logits_read, READS_FREE)
                v.wait_ge(logits_read, READS_FREE)
                nc.vector.memset(small[:, :, :], 0.0).then_inc(pt_free, PT_FREE)
                v.wait_ge(pt_free, PT_FREE)
                nc.vector.memset(small[:, :, :], 0.0).then_inc(av_free, AV_FREE)
                v.wait_ge(av_free, AV_FREE)

                def peak(i, par, half, link):
                    v.wait_ge(scores, 2 * i + half + 1)
                    if half == 0:
                        v.wait_ge(bias_par[par], 8 * (i - par) + 16)
                    link.note(nc.vector.tensor_copy(small[:, par, 6 + half:7 + half], B[par][:, N + 1 - half:N + 2 - half]))
                    cols = slice(half * 2 * BANK, (half + 1) * 2 * BANK)
                    return nc.vector.tensor_tensor_reduce(
                        E[par][:, cols], L[half][:, :], B[par][:, cols], 1.0, (B[par][:, N:N + 1], m0(par))[half],
                        ALU.add, ALU.max, (m0(par), m1(par))[half])

                def peaks_end(i, par, link):
                    peak(i, par, 1, link).then_inc(logits_read, 1)
                    v.wait_ge(logits_read, 2 * i + 2 + READS_FREE)
                    nc.vector.tensor_scalar(nb(par), m1(par), sc[:, 1:2], None, ALU.mult).then_inc(maxed, 1)

                def lo(i, q):
                    v.wait_ge(pt_hi, 4 * i + q + 1)
                    nc.vector.scalar_tensor_tensor(out=PT[1][:, 4 * q:4 * q + 4, :].rearrange("p a b -> p (a b)"), in0=TP[q % 2][:, :],
                                                   scalar=P_SCALE, in1=PT[0][:, 4 * q:4 * q + 4, :].rearrange("p a b -> p (a b)"),
                                                   op0=ALU.mult, op1=ALU.subtract).then_inc(pt_free, 1)

                def add(i, t, par, link):
                    v.wait_ge(exped, i + 1)
                    link(nc.vector.scalar_tensor_tensor(out=r(par), in0=masked(par), scalar=small[:, par, 6:7], in1=ssum(par),
                                                        op0=ALU.mult, op1=ALU.add))
                    link(nc.vector.reciprocal(r(par), r(par)))
                    link(nc.vector.tensor_scalar(r(par), r(par), sc[:, 4:5], None, ALU.mult))
                    v.wait_ge(av_done, i + 1)
                    nc.vector.scalar_tensor_tensor(out=acc[:, ds(t, 1), :].rearrange("p a d -> p (a d)"), in0=AV[par][:, :], scalar=r(par),
                                                   in1=acc[:, ds(t, 1), :].rearrange("p a d -> p (a d)"),
                                                   op0=ALU.mult, op1=ALU.add).then_inc(av_free, 1)

                def item(i, t, par, more, link):
                    if more:
                        peak(i + 1, 1 - par, 0, link).then_inc(logits_read, 1)
                        v.wait_ge(logits_read, 2 * i + 3 + READS_FREE)
                    lo(i, 0)
                    lo(i, 1)
                    if more:
                        peaks_end(i + 1, 1 - par, link)
                    lo(i, 2)
                    lo(i, 3)
                    add(i, t, par, link)

                def evacuate(h, n):
                    with v.Fori(0, 2) as u:
                        for b in range(4):
                            v.wait_ge(proj_hi, PER_HEAD * h + 8 * n + 4 * u + b + 1)
                            to = evacuated(kinds[n], n, 4 * u + b)
                            nc.vector.scalar_tensor_tensor(out=to[1], in0=bank[b].rearrange("p (a b) -> p a b", a=2),
                                                           scalar=VW_SCALE if n == 3 else 1.0, in1=to[0],
                                                           op0=ALU.mult, op1=ALU.subtract).then_inc(bank_free, 1)

                def begin(h):
                    v.wait_ge(wo_hi_s, h + 1)
                    nc.vector.scalar_tensor_tensor(out=WO[1][:, :, :], in0=wo_st[:, :, :], scalar=winv[:, 3:4], in1=WO[0][:, :, :],
                                                   op0=ALU.mult, op1=ALU.subtract).then_inc(wo_lo_s, 1)
                    for n in range(3):
                        evacuate(h, n)

                LINKS = 5
                def items(h):
                    with v.Fori(0, T // 2 - 1) as j:
                        link = Chain(v, chain, h * (LINKS * T) + 2 + j * (2 * LINKS))
                        item(16 * h + 2 * j, 2 * j, 0, True, link)
                        item(16 * h + 2 * j + 1, 2 * j + 1, 1, True, link)
                    link = Chain(v, chain, h * (LINKS * T) + 2 + (T - 2) * LINKS)
                    item(16 * h + T - 2, T - 2, 0, True, link)
                    return link

                begin(0)
                link = Chain(v, chain)
                peak(0, 0, 0, link).then_inc(logits_read, 1)
                v.wait_ge(logits_read, 1 + READS_FREE)
                peaks_end(0, 0, link)
                evacuate(0, 3)
                with v.Fori(0, HEADS - 1) as h:
                    link = items(h)
                    begin(h + 1)
                    item(16 * h + T - 1, T - 1, 1, True, link)
                    evacuate(h + 1, 3)
                link = items(HEADS - 1)
                item(16 * HEADS - 1, T - 1, 1, False, link)


def prepare(nc, sb, ps, sem, a, deg, scales, ident, ident16, halfp, w1, w2, w3, gb, sc, acc, x_d):
    loaded, stored, dve, bases, powed, vec_done, spread, ratios, largest = (sem("prep_" + s) for s in (
        "loaded", "stored", "dve", "bases", "powed", "vec", "spread", "ratios", "largest"))
    with ExitStack() as c:
        row = sb(c, "gamma_beta_row", [1, 2 * D])
        ones = sb(c, "ones_row", [1, P])
        base = sb(c, "deg_base", [P, 2, T])
        zero = sb(c, "deg_zero", [P, T])
        ratio, top = sb(c, "deg_ratio", [P, T]), sb(c, "deg_ratio_top", [P, 2])
        bc = ps(c, "gamma_beta_ps", [P, 2 * D])
        block = nc.Block()
        with block:
            @block.sync
            def _(sp):
                sp.dma_start(row[:, 0:D], a["L1_gnn_gamma"].rearrange("(a d) -> a d", a=1)).then_inc(loaded, 16)
                sp.dma_start(row[:, D:2 * D], a["L1_gnn_beta"].rearrange("(a d) -> a d", a=1)).then_inc(loaded, 16)
                sp.dma_start(w1[:, :, :], a["L1_gnn_W1"].rearrange("(k p) n -> p k n", p=P)).then_inc(loaded, 16)
                sp.dma_start(w3[:, :, :], a["L1_gnn_W3"].rearrange("(k p) n -> p k n", p=P)).then_inc(loaded, 16)
                sp.dma_start(w2[:, :], a["L1_gnn_W2"]).then_inc(loaded, 16)
                sp.dma_start(x_d, acc[:, :, :]).then_inc(stored, 16)
                sp.wait_ge(loaded, 16 * 5)
                sp.wait_ge(stored, 16)

            @block.vector
            def _(v):
                link = Chain(v, dve)
                link(nc.vector.memset(ones[:, :], 1.0))
                link(nc.vector.tensor_scalar(ident16[:, :], ident[:, :], A_SCALE, None, ALU.mult))
                link(nc.vector.tensor_scalar(scales[:, 0:2, :], deg[:, :, :], 1.0, 1e-12, ALU.add, ALU.max))
                link(nc.vector.reciprocal(scales[:, 0:2, :], scales[:, 0:2, :]))
                link(nc.vector.scalar_tensor_tensor(out=ratio[:, :], in0=deg[:, 0, :], scalar=1.0, in1=scales[:, 1, :],
                                                    op0=ALU.add, op1=ALU.mult))
                nc.vector.tensor_reduce(top[:, 0:1], ratio[:, :], X, ALU.max).then_inc(ratios, 1)
                link(nc.vector.tensor_scalar(base[:, 0, :], deg[:, 0, :], 1e-8, None, ALU.add))
                link(nc.vector.tensor_scalar(zero[:, :], deg[:, 0, :], 1.0, 0.0, ALU.add, ALU.is_equal))
                nc.vector.scalar_tensor_tensor(out=base[:, 1, :], in0=deg[:, 0, :], scalar=1.0, in1=zero[:, :],
                                               op0=ALU.add, op1=ALU.add).then_inc(bases, 1)
                v.wait_ge(powed, 1)
                link(nc.vector.tensor_scalar(zero[:, :], zero[:, :], -1.0, 1.0, ALU.mult, ALU.add))
                nc.vector.tensor_tensor(scales[:, 3, :], scales[:, 3, :], zero[:, :], ALU.mult).then_inc(vec_done, 1)
                v.wait_ge(largest, 1)
                link(nc.vector.tensor_scalar(top[:, 1:2].bitcast(U32), top[:, 1:2].bitcast(U32), 0x7F800000, None, ALU.bitwise_and))
                link(nc.vector.tensor_scalar(sc[:, 7:8], top[:, 1:2], 1.0 / X_SCALE, None, ALU.mult))
                nc.vector.reciprocal(sc[:, 6:7], sc[:, 7:8]).then_inc(vec_done, 1)
                v.wait_ge(spread, 1)
                nc.vector.tensor_copy(gb[:, :, :].rearrange("p a d -> p (a d)"), bc[:, :]).then_inc(vec_done, 1)

            @block.gpsimd
            def _(pl):
                pl.wait_ge(bases, 1)
                for n in range(2):
                    last = nc.gpsimd.tensor_tensor(scales[:, 2 + n, :], base[:, n, :], halfp[:, :], ALU.pow)
                last.then_inc(powed, 1)
                pl.wait_ge(ratios, 1)
                nc.gpsimd.partition_all_reduce(top[:, 1:2], top[:, 0:1], P, ABSMAX).then_inc(largest, 1)

            @block.tensor
            def _(pe):
                pe.wait_ge(loaded, 16 * 5)
                pe.wait_ge(dve, 1)
                nc.tensor.matmul(bc[:, :], ones[:, :], row[:, :], start=True, stop=True).then_inc(spread, 1)


def last_weights(nc, sb, ps, sem, a, ident, wT, bb, scales, l2_in, l3_in, l3_out):
    loaded, turned, copied, one, dve, extreme, largest = (
        sem("lastw_" + s) for s in ("loaded", "turned", "copied", "one", "dve", "extreme", "largest"))
    with ExitStack() as c:
        w0, w3 = sb(c, "l2_w", [P, KC, D]), sb(c, "l3_w", [P, KC, D])
        row, ones = sb(c, "l2_b_row", [1, D]), sb(c, "l2_ones", [1, P])
        ext, top = sb(c, "l3_ext", [P, 4]), sb(c, "l3_top", [P, 4])
        tp, bc = ps(c, "l2_tp", [P, BANK]), ps(c, "l2_bc", [P, D])
        block = nc.Block()
        with block:
            @block.sync
            def _(sp):
                sp.dma_start(w3[:, :, :], a["L3_gnn_weight"].rearrange("(k p) n -> p k n", p=P)).then_inc(loaded, 16)
                sp.dma_start(w0[:, :, :], a["L2_gnn_W"].rearrange("(k p) n -> p k n", p=P)).then_inc(loaded, 16)
                sp.dma_start(row[:, :], a["L2_gnn_b"].rearrange("(a d) -> a d", a=1)).then_inc(loaded, 16)
                sp.wait_ge(loaded, 48)

            @block.tensor
            def _(pe):
                pe.wait_ge(loaded, 48)
                pe.wait_ge(one, 1)
                for k in range(KC):
                    for o in range(KC):
                        nc.tensor.transpose(tp[:, k * D + o * P:k * D + (o + 1) * P], w0[:, o, k * P:(k + 1) * P], ident[:, :])
                nc.tensor.matmul(bc[:, :], ones[:, :], row[:, :], start=True, stop=True).then_inc(turned, 1)

            @block.gpsimd
            def _(pl):
                pl.wait_ge(extreme, 1)
                nc.gpsimd.partition_all_reduce(top[:, 0:1], ext[:, 2:3], P, ABSMAX).then_inc(largest, 1)

            @block.vector
            def _(v):
                link = Chain(v, dve)
                nc.vector.memset(ones[:, :], 1.0).then_inc(one, 1)
                link.note(nc.vector.tensor_scalar(l2_in[:, :], scales[:, 2, :], DEG_SCALE, None, ALU.mult))
                v.wait_ge(loaded, 48)
                link(nc.vector.tensor_reduce(ext[:, 0:1], w3[:, :, :], mybir.AxisListType.XY, ALU.max, apply_absolute_value=True))
                nc.vector.tensor_scalar(ext[:, 2:3], ext[:, 0:1], 1e-30, None, ALU.max).then_inc(extreme, 1)
                v.wait_ge(turned, 1)
                nc.vector.tensor_copy(wT[:, :, :].rearrange("p k d -> p (k d)"), tp[:, :]).then_inc(copied, 1)
                nc.vector.tensor_copy(bb[:, :], bc[:, :]).then_inc(copied, 1)
                v.wait_ge(largest, 1)
                link(nc.vector.tensor_scalar(top[:, 0:1].bitcast(U32), top[:, 0:1].bitcast(U32), 0x7F800000, None, ALU.bitwise_and))
                link(nc.vector.tensor_scalar(top[:, 1:2], top[:, 0:1], 1.0 / 64.0, None, ALU.mult))
                link(nc.vector.reciprocal(top[:, 2:3], top[:, 1:2]))
                link.note(nc.vector.tensor_scalar(l3_in[:, :], scales[:, 3, :], top[:, 2:3], None, ALU.mult))
                link.note(nc.vector.tensor_scalar(l3_out[:, :], scales[:, 3, :], top[:, 1:2], None, ALU.mult))


def normalize_onto(nc, sb, ps, sem, name, src, halfp, gb, add, stored):
    stats_done, rstd_done, dve, scaled, shifted, loaded, summed = (
        sem(f"{name}_{s}") for s in ("stats_done", "rstd_done", "dve", "scaled", "shifted", "loaded", "summed"))
    with ExitStack() as c:
        stats, mv, rstd = sb(c, name + "_stats", [P, T, 6]), sb(c, name + "_mv", [P, T, 2]), sb(c, name + "_rstd", [P, T])
        block = nc.Block()
        with block:
            @block.sync
            def _(sp):
                sp.dma_start(add[:, :, :], stored).then_inc(loaded, 16)

            @block.gpsimd
            def _(pl):
                pl.wait_ge(stats_done, 1)
                nc.gpsimd.tensor_tensor(rstd[:, :], rstd[:, :], halfp[:, :], ALU.pow).then_inc(rstd_done, 1)
                pl.wait_ge(loaded, 16)
                for t in range(T):
                    nc.gpsimd.tensor_tensor(add[:, t, :], add[:, t, :], gb[:, 1, :], ALU.add).then_inc(shifted, 1)

            @block.vector
            def _(v):
                link = Chain(v, dve)
                normalize_stats(nc, v, link, src, stats, mv)
                nc.vector.tensor_scalar(rstd[:, :], mv[:, :, 1], LN_EPS, None, ALU.add).then_inc(stats_done, 1)
                for t in range(T):
                    nc.vector.scalar_tensor_tensor(out=src[:, t, :], in0=src[:, t, :], scalar=mv[:, t, 0:1], in1=gb[:, 0, :],
                                                   op0=ALU.subtract, op1=ALU.mult).then_inc(scaled, 1)
                v.wait_ge(rstd_done, 1)
                v.wait_ge(scaled, T)
                for t in range(T):
                    v.wait_ge(shifted, t + 1)
                    nc.vector.scalar_tensor_tensor(out=add[:, t, :], in0=src[:, t, :], scalar=rstd[:, t:t + 1], in1=add[:, t, :],
                                                   op0=ALU.mult, op1=ALU.add).then_inc(summed, 1)


def refresh(nc, sb, ps, sem, name, src, dst, ident, halfp, norm=False, weight=None, onto=None, logits=None,
            parts=None, rows=None, bias=None, lo_gain=None):
    (stats_done, rstd_done, dve, centred, ready, tp_s, xt_s, prod_s, u_read, q_s, q_read, w_loaded, scaled, biased, w2_s, w2_read) = (
        sem(f"{name}_{s}") for s in ("stats_done", "rstd_done", "dve", "centred", "ready", "turned", "xT", "product", "u_read",
                                     "qk", "qk_read", "w_loaded", "scaled", "biased", "w2", "w2_read"))
    QUAD = 4
    QUADS = T // QUAD
    turn = weight is not None or logits is not None
    with ExitStack() as c:
        if norm:
            stats, mv, rstd = sb(c, name + "_stats", [P, T, 6]), sb(c, name + "_mv", [P, T, 2]), sb(c, name + "_rstd", [P, T])
        if parts:
            rest = sb(c, name + "_rest", [P, T, D])
        if turn:
            xT = [sb(c, f"{name}_xT{n}", [P, KC, BANK]) for n in range(2)]
            TP = [[ps(c, f"{name}_tp{n}{k}", [P, BANK]) for k in range(KC)] for n in range(2)]
        if weight is not None:
            W = sb(c, name + "_w", [P, KC, D])
            U = [ps(c, f"{name}_u{n}", [P, BANK]) for n in range(2)]
        if logits is not None:
            w1, w2, w3, QT, KT = logits
            Q, K = ps(c, name + "_q", [64, BANK]), ps(c, name + "_k", [64, BANK])
        block = nc.Block()
        with block:
            if weight is not None:
                @block.sync
                def _(sp):
                    sp.dma_start(W[:, :, :], weight.rearrange("(k p) d -> p k d", p=P)).then_inc(w_loaded, 16)

            @block.gpsimd
            def _(pl):
                if norm:
                    pl.wait_ge(stats_done, 1)
                    nc.gpsimd.tensor_tensor(rstd[:, :], rstd[:, :], halfp[:, :], ALU.pow).then_inc(rstd_done, 1)
                if bias is not None:
                    for t in range(T):
                        pl.wait_ge(centred, t + 1)
                        nc.gpsimd.tensor_tensor(bias[0][:, t, :], bias[0][:, t, :], bias[1][:, :], ALU.add).then_inc(biased, 1)

            if turn:
                @block.tensor
                def _(pe):
                    def turned(b):
                        if norm:
                            pe.wait_ge(ready, QUAD * b + QUAD)
                        if b >= 2:
                            pe.wait_ge(xt_s, KC * (b - 1))
                        for k in range(KC):
                            for m in range(QUAD):
                                last = nc.tensor.transpose(TP[b % 2][k][:, m * P:(m + 1) * P], dst[:, QUAD * b + m, k * P:(k + 1) * P], ident[:, :])
                        last.then_inc(tp_s, 1)

                    def products(b):
                        pe.wait_ge(xt_s, KC * (b + 1))
                        x = xT[b % 2]
                        if weight is not None:
                            if b:
                                pe.wait_ge(u_read, QUAD * b)
                            for m in range(QUAD):
                                for k in range(KC):
                                    last = nc.tensor.matmul(U[m // 2][:, m % 2 * D:(m % 2 + 1) * D], x[:, k, m * P:(m + 1) * P], W[:, k, :],
                                                            start=(k == 0), stop=(k == 1))
                        if logits is not None:
                            if b:
                                pe.wait_ge(q_read, 2 * b)
                            for o, w in ((Q, w1), (K, w3)):
                                for k in range(KC):
                                    last = nc.tensor.matmul(o[:, :], w[:, k, :], x[:, k, :], start=(k == 0), stop=(k == 1))
                        last.then_inc(prod_s, 1)

                    if weight is not None:
                        pe.wait_ge(w_loaded, 16)
                    for b in range(QUADS):
                        turned(b)
                        if b:
                            products(b - 1)
                    products(QUADS - 1)
                    if logits is not None:
                        pe.wait_ge(q_read, 2 * QUADS)
                        for b in range(QUADS):
                            nc.tensor.matmul(TP[b // 2][b % 2][0:64, :], w2[:, :], QT[:, b * BANK:(b + 1) * BANK],
                                             start=True, stop=True).then_inc(w2_s, 1)

            @block.scalar
            def _(s):
                for b in range(QUADS + 2):
                    if norm and b < QUADS:
                        for t in range(QUAD * b, QUAD * b + QUAD):
                            s.wait_ge(centred, t + 1)
                            nc.scalar.activation(dst[:, t, :], dst[:, t, :], ACT.Relu).then_inc(ready, 1)
                    if turn and 1 <= b <= QUADS:
                        s.wait_ge(tp_s, b)
                        if b >= 3:
                            s.wait_ge(prod_s, b - 2)
                        for k in range(KC):
                            nc.scalar.activation(xT[(b - 1) % 2][:, k, :], TP[(b - 1) % 2][k][:, :], ACT.Copy).then_inc(xt_s, 1)
                    if parts and b >= 2:
                        for t in range(QUAD * (b - 2), QUAD * (b - 1)):
                            if weight is not None:
                                s.wait_ge(u_read, t + 1)
                            elif norm:
                                s.wait_ge(ready, t + 1)
                            nc.scalar.activation(rest[:, t, :], dst[:, t, :], ACT.Copy,
                                                 scale=rows if isinstance(rows, float) else rows[:, t:t + 1]).then_inc(scaled, 1)

            @block.vector
            def _(v):
                link = Chain(v, dve)

                def read(b):
                    v.wait_ge(prod_s, b + 1)
                    if weight is not None:
                        for m in range(QUAD):
                            t, u = QUAD * b + m, U[m // 2][:, m % 2 * D:(m % 2 + 1) * D]
                            if onto is None:
                                nc.vector.tensor_copy(dst[:, t, :], u).then_inc(u_read, 1)
                            else:
                                nc.vector.tensor_tensor(onto[:, t, :], onto[:, t, :], u, ALU.add).then_inc(u_read, 1)
                    if logits is not None:
                        nc.vector.tensor_copy(QT[:, b * BANK:(b + 1) * BANK], Q[:, :]).then_inc(q_read, 1)
                        nc.vector.tensor_copy(in_order(KT[:, :])[:, QUAD // 2 * b:QUAD // 2 * (b + 1), :, :],
                                              K[:, :].rearrange("d (c q p) -> d c q p", q=2, p=P)).then_inc(q_read, 1)

                def cut(b):
                    tiles = range(QUAD * b, QUAD * b + QUAD)
                    v.wait_ge(scaled, QUAD * b + QUAD)
                    for t in tiles:
                        link.note(nc.vector.tensor_copy(parts[0][:, t, :], rest[:, t, :]))
                    link.wait()
                    for t in tiles:
                        to = parts[1] if lo_gain is None else rest
                        link.note(nc.vector.tensor_tensor(to[:, t, :], rest[:, t, :], parts[0][:, t, :], ALU.subtract))
                    if lo_gain is not None:
                        link.wait()
                        for t in tiles:
                            link.note(nc.vector.tensor_scalar(parts[1][:, t, :], rest[:, t, :], lo_gain, None, ALU.mult))

                if norm:
                    normalize_stats(nc, v, link, src, stats, mv)
                    nc.vector.tensor_scalar(rstd[:, :], mv[:, :, 1], LN_EPS, None, ALU.add).then_inc(stats_done, 1)
                    v.wait_ge(rstd_done, 1)
                    for t in range(T):
                        nc.vector.tensor_scalar(dst[:, t, :], src[:, t, :], mv[:, t, 0:1], rstd[:, t:t + 1],
                                                ALU.subtract, ALU.mult).then_inc(centred, 1)
                for b in range(QUADS):
                    if turn:
                        read(b)
                    if parts and b:
                        cut(b - 1)
                if parts:
                    cut(QUADS - 1)
                if logits is not None:
                    for b in range(QUADS):
                        v.wait_ge(w2_s, b + 1)
                        nc.vector.tensor_copy(QT[:, b * BANK:(b + 1) * BANK], TP[b // 2][b % 2][0:64, :]).then_inc(w2_read, 1)


def diffuse(nc, sb, ps, sem, name, at_d, ident, ident16, target, parts, scale, rows, weight, lo_gain):
    at_loaded = [sem(f"{name}_at_loaded{n}") for n in range(2)]
    prod, first_s, xs_s, tp_s, xt_s, u_s, u_free, dve = (sem(f"{name}_{s}") for s in (
        "product", "first", "scaled", "turned", "xt", "weighted", "free", "dve"))
    FREE = 2
    with ExitStack() as c:
        AT = [sb(c, f"{name}_at{n}", [P, 2, T, P], F16) for n in range(2)]
        xs = [sb(c, f"{name}_xs{n}", [P, D]) for n in range(2)]
        xT = [sb(c, f"{name}_xT{n}", [P, D]) for n in range(2)]
        rsc = sb(c, f"{name}_row_scales", [P, 2, T])
        PR = [ps(c, f"{name}_pr{m}", [P, BANK]) for m in range(2)]
        TP = [ps(c, f"{name}_tp{n}", [P, BANK]) for n in range(2)]
        UP = [ps(c, f"{name}_up{n}", [P, BANK]) for n in range(2)]
        block = nc.Block()
        with block:
            @block.sync
            def _(sp):
                with sp.Fori(0, T // 2) as j:
                    for b in range(2):
                        sp.wait_ge(xs_s, 2 * j + b + 1)
                        sp.dma_start(AT[b][:, :, :, :].rearrange("p x m n -> p (x m n)"),
                                     at_d[ds(2 * j + b, 1), :, :].rearrange("a p m -> p (a m)")).then_inc(at_loaded[b], 16)

            @block.tensor
            def _(pe):
                def multiply(t, b, half):
                    pe.wait_ge(at_loaded[b], 16 * (half + 1))
                    pe.wait_ge(xs_s, t + 1)
                    low_sum = 0 if lo_gain is None else 1
                    for o, pairs in enumerate([[(0, 0), (1, 0)] + [(0, 1)] * (1 - low_sum), [(0, 1)] * low_sum]):
                        for m in range(T if pairs else 0):
                            for x, y in pairs:
                                last = nc.tensor.matmul(PR[b][:, o * D:(o + 1) * D], AT[b][:, x, m, :], parts[y][:, m, :],
                                                        start=(m == 0 and (x, y) == pairs[0]),
                                                        stop=(ident16 is None and m == T - 1 and (x, y) == pairs[-1]))
                    if ident16 is not None:
                        for y, part in enumerate(parts):
                            last = nc.tensor.matmul(PR[b][:, 0:D], ident16[:, :], part[:, ds(t, 1), :].rearrange("p a d -> p (a d)"),
                                                    start=False, stop=(y == 1))
                    last.then_inc(prod, 1)

                def weigh(t, b):
                    if weight is None:
                        return
                    pe.wait_ge(xs_s, t + 1 + FREE)
                    pe.wait_ge(u_free, t + 1)
                    for k in range(KC):
                        last = nc.tensor.transpose(TP[b][:, k * P:(k + 1) * P], xs[b][:, k * P:(k + 1) * P], ident[:, :])
                    last.then_inc(tp_s, 1)
                    pe.wait_ge(xt_s, t + 1)
                    for k in range(KC):
                        last = nc.tensor.matmul(UP[b][:, 0:D], xT[b][:, k * P:(k + 1) * P], weight[:, k, :], start=(k == 0), stop=(k == 1))
                    last.then_inc(u_s, 1)

                multiply(0, 0, 0)
                with pe.Fori(0, T // 2 - 1) as j:
                    multiply(2 * j + 1, 1, j)
                    weigh(2 * j, 0)
                    multiply(2 * j + 2, 0, j + 1)
                    weigh(2 * j + 1, 1)
                multiply(T - 1, 1, T // 2 - 1)
                weigh(T - 2, 0)
                weigh(T - 1, 1)

            @block.scalar
            def _(s):
                def scale_rows(t, b):
                    s.wait_ge(prod, t + 1)
                    s.wait_ge(u_free, t + 1)
                    nc.scalar.activation(xs[b][:, :], PR[b][:, 0:D], ACT.Relu if weight is None else ACT.Copy,
                                         scale=rsc[:, 0, ds(t, 1)]).then_inc(xs_s if lo_gain is None else first_s, 1)

                def weighted(t, b):
                    if weight is None:
                        return
                    s.wait_ge(tp_s, t + 1)
                    nc.scalar.activation(xT[b][:, :], TP[b][:, 0:D], ACT.Copy).then_inc(xt_s, 1)

                s.wait_ge(u_free, FREE)
                scale_rows(0, 0)
                with s.Fori(0, T // 2 - 1) as j:
                    scale_rows(2 * j + 1, 1)
                    weighted(2 * j, 0)
                    scale_rows(2 * j + 2, 0)
                    weighted(2 * j + 1, 1)
                scale_rows(T - 1, 1)
                weighted(T - 2, 0)
                weighted(T - 1, 1)

            @block.vector
            def _(v):
                link = Chain(v, dve)
                link(nc.vector.tensor_scalar(rsc[:, 0, :], rows, 1.0 / (scale * A_SCALE), None, ALU.mult))
                link(nc.vector.tensor_scalar(rsc[:, 1, :], rsc[:, 0, :], 1.0 / (lo_gain or 1.0), None, ALU.mult))
                nc.vector.memset(xs[0][:, :], 0.0).then_inc(xs_s, FREE)
                v.wait_ge(xs_s, FREE)
                nc.vector.memset(xs[0][:, :], 0.0).then_inc(u_free, FREE)
                v.wait_ge(u_free, FREE)

                def here(x, t):
                    return x[:, ds(t, 1), :].rearrange("p a d -> p (a d)")

                def scaled(t, b):
                    if lo_gain is not None:
                        v.wait_ge(first_s, t + 1)
                        nc.vector.scalar_tensor_tensor(out=xs[b][:, :], in0=PR[b][:, D:2 * D], scalar=rsc[:, 1, ds(t, 1)], in1=xs[b][:, :],
                                                       op0=ALU.mult, op1=ALU.add).then_inc(xs_s, 1)
                    if weight is None:
                        v.wait_ge(xs_s, t + 1 + FREE)
                        nc.vector.tensor_tensor(here(target, t), here(target, t), xs[b][:, :], ALU.add).then_inc(u_free, 1)

                def add(t, b):
                    if weight is not None:
                        v.wait_ge(u_s, t + 1)
                        nc.vector.tensor_tensor(here(target, t), here(target, t), UP[b][:, 0:D], ALU.add).then_inc(u_free, 1)

                scaled(0, 0)
                with v.Fori(0, T // 2 - 1) as j:
                    scaled(2 * j + 1, 1)
                    add(2 * j, 0)
                    scaled(2 * j + 2, 0)
                    add(2 * j + 1, 1)
                scaled(T - 1, 1)
                add(T - 2, 0)
                add(T - 1, 1)


def nucleus(nc, sb, ps, sem, name, QT, KT, parts, out, ident, diffusion):
    weights, at_d, scales, ident16, y, sc, Xp, Xf, Xb, step = diffusion
    jobs = [(Xp, 2)] if step == 0 else [(Xf, 1), (Xb, 1)]
    (u_loaded, hi_loaded, lo_loaded, s_prod, rsc_s, xs_s, s_tp, s_xt, weighted, us_s, cut_s, added, pchain) = (
        sem(f"{name}_{s}") for s in ("u_loaded", "at_hi", "at_lo", "s_product", "row_scales", "xs", "xs_turned", "xs_T",
                                     "weighted", "us", "cut", "added", "pool_chain"))
    (scores, l_free, peaked, exped, masked_s, e_free, tp_s, hi_s, lo_s, prod_s, out_s) = (
        sem(f"{name}_{s}") for s in ("scores", "l_free", "peaked", "exped", "masked", "e_free", "turned", "hi", "lo", "product",
                                     "out"))
    GROUPS = T // G
    with ExitStack() as c:
        e = sb(c, name + "_e", [P, 2, G, N + 8])
        junk = sb(c, name + "_junk", [P, N + 8])
        eight = sb(c, name + "_eight", [P, 8])
        listed, spare = sb(c, name + "_listed", [P, G, 8]), sb(c, name + "_spare", [P, G, 8])
        void = junk[:, 0:N].bitcast(BF16).rearrange("p (a n) -> p a n", a=2)
        PT = [sb(c, f"{name}_pT{n}", [P, T, P], F16) for n in ("hi", "lo")]
        staging = [sb(c, f"{name}_stage{n}", [P, BANK]) for n in range(2)]
        nmax, Z = sb(c, name + "_nmax", [P, T]), sb(c, name + "_Z", [P, T])
        rs = sb(c, name + "_rs", [P, T])
        S = sb(c, name + "_small", [P, 18, G])
        top, kept = sb(c, name + "_top", [P, G, 8]), sb(c, name + "_kept", [P, G, 8])
        pre = sb(c, name + "_prefix", [P, G, 8])
        one = sb(c, name + "_one", [P, 8])
        und, undT = sb(c, name + "_und", [P, 32]), sb(c, name + "_undT", [P, 32])
        cell = sb(c, name + "_cell", [1, 8])
        flag = sb(c, name + "_flag", [1, 8], I32)
        FACTORS = len(weights)
        U = sb(c, name + "_u", [P, FACTORS, KC, D])
        AH, AL = sb(c, name + "_at_hi", [P, T, P], F16), sb(c, name + "_at_lo", [P, T, P], F16)
        rsc = sb(c, name + "_rsc", [P, 2, T])
        xs, xT = sb(c, name + "_xs", [P, 2, D]), sb(c, name + "_xsT", [P, FACTORS * D])
        us = sb(c, name + "_us", [P, D])
        scaled = sb(c, name + "_scaled", [P, D])
        L = [ps(c, f"{name}_l{n}", [P, N]) for n in range(2)]
        TP = [L[1][:, n * BANK:(n + 1) * BANK] for n in range(2)]
        PR = [L[1][:, 2 * BANK + n * D:2 * BANK + (n + 1) * D] for n in range(2)]
        SP = L[1][:, 3 * BANK:4 * BANK]
        lo, hi, t_, Gt, b_, target, M, R, tie, tstar, done, x_, m_lo, m_hi, short, y_, z_, w_ = (S[:, k, :] for k in range(18))

        def scores_in(i):
            return L[i % 2 if i < G else 0]

        block = nc.Block()
        with block:
            @block.sync
            def _(sp):
                for n, u in enumerate(weights):
                    sp.dma_start(U[:, n, :, :], u.rearrange("(k p) d -> p k d", p=P)).then_inc(u_loaded, 16)
                for t in range(T):
                    if t:
                        sp.wait_ge(s_prod, len(jobs) * t)
                    sp.dma_start(AH[:, :, :].rearrange("p m n -> p (m n)"), at_d[t, :, 0:N]).then_inc(hi_loaded, 16)
                    sp.dma_start(AL[:, :, :].rearrange("p m n -> p (m n)"), at_d[t, :, N:2 * N]).then_inc(lo_loaded, 16)

            @block.tensor
            def _(pe):
                def diffuse_tile(t):
                    pe.wait_ge(hi_loaded, 16 * t + 16)
                    pe.wait_ge(lo_loaded, 16 * t + 16)
                    if t:
                        pe.wait_ge(us_s, t)
                    for n, (rows, _) in enumerate(jobs):
                        o = SP[:, n * D:(n + 1) * D]
                        for x, A_ in enumerate((AH, AL)):
                            for m in range(T):
                                for y_part in rows[:2 - x]:
                                    nc.tensor.matmul(o, A_[:, m, :], y_part[:, m, :], start=(m == x == 0 and y_part is rows[0]), stop=False)
                        for part in rows:
                            last = nc.tensor.matmul(o, ident16[:, :], part[:, t, :], start=False, stop=(part is rows[1]))
                        last.then_inc(s_prod, 1)
                    pe.wait_ge(xs_s, 2 * t + 2)
                    for r in range(2):
                        for k in range(KC):
                            last = nc.tensor.transpose(TP[0][:, r * D + k * P:r * D + (k + 1) * P], xs[:, r, k * P:(k + 1) * P], ident[:, :])
                    for k in range(KC if FACTORS == 3 else 0):
                        last = nc.tensor.transpose(TP[1][:, k * P:(k + 1) * P], out[:, t, k * P:(k + 1) * P], ident[:, :])
                    last.then_inc(s_tp, 1)
                    pe.wait_ge(s_xt, (FACTORS - 1) * (t + 1))
                    if t == 0:
                        pe.wait_ge(u_loaded, 16 * FACTORS)
                    for r in range(FACTORS):
                        for k in range(KC):
                            last = nc.tensor.matmul(SP[:, 0:D], xT[:, r * D + k * P:r * D + (k + 1) * P], U[:, r, k, :],
                                                    start=(r == k == 0), stop=(r == FACTORS - 1 and k == 1))
                    last.then_inc(weighted, 1)

                def logits(g, k):
                    i = G * g + k
                    if g or k >= 2:
                        pe.wait_ge(exped, i if g else i - 1)
                    for b in range(4):
                        last = nc.tensor.matmul(scores_in(i)[:, b * BANK:(b + 1) * BANK], QT[:, i * P:(i + 1) * P], KT[:, b * BANK:(b + 1) * BANK],
                                                start=True, stop=True)
                    last.then_inc(scores, 1)

                def multiply(g, k):
                    i = G * g + k
                    pe.wait_ge(masked_s, i + 1)

                    def turn(q):
                        if 4 * i + q >= 2:
                            pe.wait_ge(lo_s, 4 * i + q - 1)
                        for m in range(4 * q, 4 * q + 4):
                            last = nc.tensor.transpose(TP[q % 2][:, m % 4 * P:(m % 4 + 1) * P], in_order(e[:, g % 2, k, 0:N])[:, m // 2, m % 2, :],
                                                       ident[:, :])
                        last.then_inc(tp_s, 1)

                    turn(0)
                    turn(1)
                    if i:
                        pe.wait_ge(out_s, i)
                    for q in range(4):
                        pe.wait_ge(lo_s, 4 * i + q + 1)
                        for m in range(4 * q, 4 * q + 4):
                            for x, y in ((0, 0), (0, 1), (1, 0)):
                                last = nc.tensor.matmul(PR[k % 2], PT[x][:, m, :], parts[y][:, m, :],
                                                        start=(m == 0 and x == y == 0), stop=(m == T - 1 and x == 1))
                        if q < 2:
                            turn(q + 2)
                    last.then_inc(prod_s, 1)

                for k in range(G):
                    logits(0, k)
                for g in range(GROUPS):
                    for k in range(G):
                        if g + 1 < GROUPS:
                            logits(g + 1, k)
                        if g:
                            multiply(g - 1, k)
                        diffuse_tile(G * g + k)
                for k in range(G):
                    multiply(GROUPS - 1, k)

            @block.scalar
            def _(s):
                def results(t):
                    if t == 0:
                        s.wait_ge(rsc_s, 2)
                    if t and step == 0:
                        s.wait_ge(cut_s, t)
                    s.wait_ge(s_prod, len(jobs) * (t + 1))
                    for r in range(2):
                        n = r if step else 0
                        nc.scalar.activation(xs[:, r, :], SP[:, n * D:(n + 1) * D], ACT.Copy, scale=rsc[:, r, t:t + 1]).then_inc(xs_s, 1)
                    s.wait_ge(s_tp, t + 1)
                    nc.scalar.activation(xT[:, 0:2 * D], TP[0], ACT.Copy).then_inc(s_xt, 1)
                    if FACTORS == 3:
                        nc.scalar.activation(xT[:, 2 * D:3 * D], TP[1][:, 0:D], ACT.Copy).then_inc(s_xt, 1)
                    s.wait_ge(weighted, t + 1)
                    if t:
                        s.wait_ge(added, t)
                    nc.scalar.activation(us[:, :], SP[:, 0:D], ACT.Copy).then_inc(us_s, 1)

                def exp(g, k):
                    i = G * g + k
                    s.wait_ge(peaked, i + 1)
                    if g >= 2:
                        s.wait_ge(prod_s, G * (g - 2) + k + 1)
                    nc.scalar.activation(e[:, g % 2, k, 0:N], scores_in(i)[:, :], ACT.Exp, bias=nmax[:, i:i + 1], scale=1.0,
                                         accum_out=Z[:, i:i + 1]).then_inc(exped, 1)

                def halves(g, k):
                    i = G * g + k
                    for q in range(4):
                        s.wait_ge(tp_s, 4 * i + q + 1)
                        nc.scalar.activation(PT[0][:, 4 * q:4 * q + 4, :].rearrange("p a b -> p (a b)"), TP[q % 2], ACT.Copy,
                                             scale=P_SCALE).then_inc(hi_s, 1)
                        if i >= T - G:
                            continue
                        stage = staging[q % 2]
                        if 4 * i + q >= 2:
                            s.wait_ge(lo_s, 4 * i + q - 1)
                        nc.scalar.activation(stage[:, :], TP[q % 2], ACT.Copy, scale=P_SCALE).then_inc(hi_s, 1)
                    s.wait_ge(prod_s, i + 1)
                    nc.scalar.activation(out[:, i, :], PR[k % 2], ACT.Copy, scale=rs[:, i:i + 1]).then_inc(out_s, 1)

                for k in range(G):
                    exp(0, k)
                for g in range(GROUPS):
                    for k in range(G):
                        if g:
                            halves(g - 1, k)
                        if g + 1 < GROUPS:
                            exp(g + 1, k)
                        results(G * g + k)
                for k in range(G):
                    halves(GROUPS - 1, k)

            @block.gpsimd
            def _(pl):
                def lows(i):
                    for q in range(4):
                        pl.wait_ge(hi_s, 2 * (4 * i + q + 1))
                        nc.gpsimd.tensor_tensor(PT[1][:, 4 * q:4 * q + 4, :].rearrange("p a b -> p (a b)"), staging[q % 2][:, :],
                                                PT[0][:, 4 * q:4 * q + 4, :].rearrange("p a b -> p (a b)"), ALU.subtract).then_inc(lo_s, 1)

                def cut_and_add(t, link):
                    pl.wait_ge(xs_s, 2 * t + 2)
                    if step == 0:
                        for r, (hi_part, lo_part) in enumerate((Xf, Xb)):
                            link(nc.gpsimd.tensor_scalar(scaled[:, :], xs[:, r, :], X_SCALE if r == 0 else sc[:, 6:7], None, ALU.mult))
                            link(nc.gpsimd.tensor_copy(hi_part[:, t, :], scaled[:, :]))
                            nc.gpsimd.tensor_tensor(lo_part[:, t, :], scaled[:, :], hi_part[:, t, :], ALU.subtract).then_inc(link.sem if r == 0 else cut_s, 1)
                            if r == 0:
                                link.n += 1
                                link.wait()
                            else:
                                pl.wait_ge(cut_s, t + 1)
                    pl.wait_ge(us_s, t + 1)
                    nc.gpsimd.tensor_tensor(y[:, t, :], y[:, t, :], us[:, :], ALU.add).then_inc(added, 1)

                link = Chain(pl, pchain)
                for t in range(T):
                    if t >= G:
                        lows(t - G)
                    cut_and_add(t, link)
            @block.vector
            def _(v):
                left = v.alloc_register(name + "_left")

                def link(ins):
                    v.drain()

                def peak(g, k):
                    i = G * g + k
                    v.wait_ge(scores, i + 1)
                    nc.vector.tensor_reduce(nmax[:, i:i + 1], scores_in(i)[:, :], X, ALU.max, negate=True).then_inc(peaked, 1)

                def mass(g, compare, bound, to):
                    for k in range(G):
                        nc.vector.scalar_tensor_tensor(out=void[:, k % 2, :], in0=e[:, g % 2, k, 0:N], scalar=bound[:, k:k + 1],
                                                       in1=e[:, g % 2, k, 0:N], op0=compare, op1=ALU.mult, accum_out=to[:, k:k + 1])
                        if k % 2:
                            v.drain()

                def together(*instructions):
                    v.drain()

                def evaluate(g):
                    mass(g, ALU.is_gt, t_, Gt)
                    together(nc.vector.tensor_tensor(b_, Gt, target, ALU.is_ge),
                             nc.vector.tensor_tensor(short, Gt, target, ALU.is_lt))
                    together(nc.vector.tensor_tensor(x_, b_, t_, ALU.mult),
                             nc.vector.scalar_tensor_tensor(out=y_, in0=b_, scalar=4.0, in1=t_, op0=ALU.mult, op1=ALU.add),
                             nc.vector.tensor_tensor(z_, short, Gt, ALU.mult),
                             nc.vector.scalar_tensor_tensor(out=w_, in0=short, scalar=4.0 * N, in1=Gt, op0=ALU.mult, op1=ALU.add))
                    together(nc.vector.tensor_tensor(lo, lo, x_, ALU.max),
                             nc.vector.tensor_tensor(hi, hi, y_, ALU.min),
                             nc.vector.tensor_tensor(m_hi, m_hi, z_, ALU.max),
                             nc.vector.tensor_tensor(m_lo, m_lo, w_, ALU.min))

                def bisect(g):
                    link(nc.vector.tensor_tensor(x_.bitcast(I32), lo.bitcast(I32), hi.bitcast(I32), ALU.add))
                    link(nc.vector.tensor_scalar(t_.bitcast(I32), x_.bitcast(I32), 0.5, None, ALU.mult))
                    evaluate(g)

                def interpolate(g):
                    together(nc.vector.tensor_tensor(x_, m_lo, m_hi, ALU.subtract),
                             nc.vector.tensor_tensor(y_, m_lo, target, ALU.subtract),
                             nc.vector.tensor_tensor(z_, hi.bitcast(I32), lo.bitcast(I32), ALU.subtract))
                    link(nc.vector.reciprocal(x_, x_))
                    link(nc.vector.tensor_tensor(x_, x_, y_, ALU.mult))
                    link(nc.vector.tensor_scalar(x_, x_, CLIP, 1.0 - CLIP, ALU.max, ALU.min))
                    link(nc.vector.tensor_tensor(x_, x_, z_, ALU.mult))
                    link(nc.vector.tensor_tensor(t_.bitcast(I32), x_, lo.bitcast(I32), ALU.add))
                    evaluate(g)

                def ties(g):
                    link(nc.vector.tensor_copy(x_, top[:, :, 7]))
                    mass(g, ALU.is_ge, x_, Gt)
                    together(nc.vector.tensor_tensor(b_, Gt, target, ALU.is_ge),
                             nc.vector.tensor_scalar(x_, x_, 1.0 - 2.0 ** -23, None, ALU.mult))
                    together(nc.vector.tensor_tensor(tie, tie, b_, ALU.max),
                             nc.vector.scalar_tensor_tensor(out=x_, in0=b_, scalar=4.0, in1=x_, op0=ALU.mult, op1=ALU.add))
                    link(nc.vector.tensor_tensor(hi, hi, x_, ALU.min))

                def look(g):
                    for k in range(G):
                        link(nc.vector.scalar_tensor_tensor(out=junk[:, 0:N], in0=e[:, g % 2, k, 0:N], scalar=hi[:, k:k + 1],
                                                            in1=e[:, g % 2, k, 0:N], op0=ALU.is_le, op1=ALU.mult, accum_out=M[:, k:k + 1]))
                        link(nc.vector.max(top[:, k, :], junk[:, 0:N]))
                    together(*[nc.vector.tensor_tensor_scan(pre[:, k, :], top[:, k, :], one[:, :], 0.0, ALU.add, ALU.mult) for k in range(G)],
                             nc.vector.tensor_tensor(x_, target, Z[:, G * g:G * g + G], ALU.subtract),
                             nc.vector.tensor_copy(kept[:, :, 0], top[:, :, 0]))
                    link(nc.vector.tensor_tensor(R, x_, M, ALU.add))
                    together(*[nc.vector.tensor_scalar(kept[:, k, 1:8], pre[:, k, 0:7], R[:, k:k + 1], 4.0, ALU.is_ge, ALU.mult) for k in range(G)],
                             nc.vector.tensor_tensor(done, pre[:, :, 7], R, ALU.is_ge))
                    together(nc.vector.tensor_tensor(kept[:, :, 1:8], kept[:, :, 1:8], top[:, :, 1:8], ALU.add),
                             nc.vector.tensor_tensor(done, done, tie, ALU.max))
                    link(nc.vector.tensor_reduce(tstar, kept[:, :, :], X, ALU.min))
                    link(nc.vector.tensor_scalar(x_, done, -1.0, 1.0, ALU.mult, ALU.add))
                    any_row(x_, flag)

                def any_row(rows, to):
                    link(nc.vector.tensor_reduce(und[:, 0:1], rows, X, ALU.max))
                    link(nc.vector.transpose(undT[:, :], und[:, :]))
                    link(nc.vector.tensor_reduce(und[:, 0:1], undT[:, :], X, ALU.max))
                    together(*[nc.vector.tensor_copy(cell[0:1, q:q + 1], und[32 * q:32 * q + 1, 0:1]) for q in range(4)])
                    link(nc.vector.tensor_reduce(cell[0:1, 4:5], cell[0:1, 0:4], X, ALU.max))
                    link(nc.vector.tensor_copy(to[0:1, 0:1], cell[0:1, 4:5]))

                def break_ties(g, kept_sum):
                    together(*[nc.vector.tensor_scalar(listed[:, k, :], kept[:, k, :], tstar[:, k:k + 1], None, ALU.is_equal) for k in range(G)],
                             nc.vector.tensor_tensor(x_, R, pre[:, :, 7], ALU.subtract),
                             nc.vector.reciprocal(z_, tstar))
                    together(nc.vector.tensor_reduce(y_, listed[:, :, :], X, ALU.add),
                             nc.vector.tensor_tensor(x_, x_, z_, ALU.mult))
                    link(nc.vector.scalar_tensor_tensor(out=y_, in0=x_, scalar=0.0, in1=y_, op0=ALU.max, op1=ALU.add))
                    link(nc.vector.tensor_scalar(x_, y_, 0.125, 0.5, ALU.mult, ALU.add))
                    any_row(x_, flag)
                    v.reg_load(left, flag[0:1, 0:1])

                    def mark(k, source):
                        together(nc.vector.tensor_scalar(listed[:, k, :], eight[:, :], y_[:, k:k + 1], tstar[:, k:k + 1], ALU.is_lt, ALU.mult),
                                 nc.vector.tensor_scalar(spare[:, k, :], eight[:, :], y_[:, k:k + 1], -1.0, ALU.is_ge, ALU.mult))
                        link(nc.vector.tensor_tensor(listed[:, k, :], listed[:, k, :], spare[:, k, :], ALU.add))
                        link(nc.vector.match_replace(out=junk[:, :], in_to_replace=listed[:, k, :], in_values=source, imm_value=4.0))
                        together(nc.vector.memset(junk[:, N:N + 8], -1.0),
                                 nc.vector.tensor_scalar(y_[:, k:k + 1], y_[:, k:k + 1], -8.0, None, ALU.add))

                    for k in range(G):
                        mark(k, e[:, g % 2, k, :])
                        with v.Fori(1, v.snap(left)):
                            mark(k, junk[:, :])
                        link(nc.vector.scalar_tensor_tensor(out=e[:, g % 2, k, 0:N], in0=junk[:, 0:N], scalar=tstar[:, k:k + 1],
                                                            in1=e[:, g % 2, k, 0:N], op0=ALU.is_gt, op1=ALU.mult,
                                                            accum_out=kept_sum[:, k:k + 1]))

                def search(g):
                    v.wait_ge(exped, G * g + G)
                    link(nc.vector.tensor_scalar(target, Z[:, G * g:G * g + G], P_NUC, None, ALU.mult))
                    link(nc.vector.tensor_scalar(lo, Z[:, G * g:G * g + G], (1 - P_NUC) * 0.999 / N, None, ALU.mult))
                    link(nc.vector.memset(hi, 1.001))
                    link(nc.vector.memset(tie, 0.0))
                    link(nc.vector.tensor_copy(m_lo, Z[:, G * g:G * g + G]))
                    link(nc.vector.memset(m_hi, 0.0))
                    for n in range(CUTS):
                        interpolate(g)
                        if n in PEAK_AFTER and g + 1 < GROUPS:
                            peak(g + 1, PEAK_AFTER.index(n))
                    look(g)
                    v.reg_load(left, flag[0:1, 0:1])
                    with v.If(v.snap(left) > 0):
                        ties(g)
                        look(g)
                        v.reg_load(left, flag[0:1, 0:1])
                    with v.While(lambda: v.snap(left) > 0):
                        ties(g)
                        bisect(g)
                        look(g)
                        v.reg_load(left, flag[0:1, 0:1])
                    kept_sum = rs[:, G * g:G * g + G]
                    for k in range(G):
                        nc.vector.scalar_tensor_tensor(out=e[:, g % 2, k, 0:N], in0=e[:, g % 2, k, 0:N], scalar=tstar[:, k:k + 1],
                                                       in1=e[:, g % 2, k, 0:N], op0=ALU.is_ge, op1=ALU.mult, accum_out=kept_sum[:, k:k + 1])
                    v.drain()
                    link(nc.vector.tensor_tensor(x_, kept_sum, target, ALU.subtract))
                    link(nc.vector.tensor_tensor(x_, x_, tstar, ALU.is_ge))
                    any_row(x_, flag)
                    v.reg_load(left, flag[0:1, 0:1])
                    with v.If(v.snap(left) > 0):
                        break_ties(g, kept_sum)
                    link(nc.vector.reciprocal(kept_sum, kept_sum))
                    nc.vector.tensor_scalar(kept_sum, kept_sum, 1.0 / (P_SCALE * X_SCALE), None, ALU.mult).then_inc(masked_s, G)
                    v.wait_ge(masked_s, G * g + G)

                nc.vector.tensor_scalar(rsc[:, 0, :], scales[:, 0, :], 1.0 / (X_SCALE * A_SCALE), None, ALU.mult).then_inc(rsc_s, 1)
                nc.vector.tensor_scalar(rsc[:, 1, :], scales[:, 1, :], 1.0 / (X_SCALE * A_SCALE) if step == 0 else sc[:, 7:8],
                                        1.0 if step == 0 else 1.0 / A_SCALE, ALU.mult, ALU.mult).then_inc(rsc_s, 1)
                link(nc.vector.memset(one[:, :], 1.0))
                for n in range(8):
                    link(nc.vector.memset(eight[:, n:n + 1], float(n)))
                link(nc.vector.memset(e[:, :, :, N:N + 8], -1.0))
                link(nc.vector.memset(und[:, :], 0.0))
                for k in range(G):
                    peak(0, k)
                for g in range(GROUPS):
                    search(g)
                for n in range(4 * G):
                    i, q = T - G + n // 4, n % 4
                    v.wait_ge(hi_s, 2 * 4 * (T - G) + n + 1)
                    nc.vector.scalar_tensor_tensor(out=PT[1][:, 4 * q:4 * q + 4, :].rearrange("p a b -> p (a b)"), in0=TP[q % 2],
                                                   scalar=P_SCALE, in1=PT[0][:, 4 * q:4 * q + 4, :].rearrange("p a b -> p (a b)"),
                                                   op0=ALU.mult, op1=ALU.subtract).then_inc(lo_s, 1)


def finish(nc, sb, ps, sem, acc, out):
    stored = sem("out_stored")
    block = nc.Block()
    with block:
        @block.sync
        def _(sp):
            for q in range(2):
                sp.dma_start(nodes(out)[:, :, q, :], acc[:, :, :].rearrange("p (c q) d -> p c q d", q=2)[:, :, q, :]).then_inc(stored, 16)
            sp.wait_ge(stored, 32)


_INS = ["x", "adj", "L0_gnn_Wq", "L0_gnn_Wk", "L0_gnn_Wv", "L0_gnn_Wout", "L1_gnn_W1", "L1_gnn_W2", "L1_gnn_W3", "L1_gnn_U1",
        "L1_gnn_U2", "L1_gnn_U3", "L1_gnn_gamma", "L1_gnn_beta", "L2_gnn_W", "L2_gnn_b", "L3_gnn_weight"]


def kernel(**inputs):
    import numpy as _np
    import concourse.bacc as _bacc
    from concourse import mybir as _mybir
    from concourse.bass_utils import run_bass_kernel_spmd as _run

    nc = _bacc.Bacc("TRN2", target_bir_lowering=False, num_devices=1)
    arrays, args = {}, {}
    for name in _INS:
        a = _np.ascontiguousarray(inputs[name])
        arrays[f"in_{name}_dram"] = a
        args[name] = nc.dram_tensor(f"in_{name}_dram", a.shape, _mybir.dt.from_np(a.dtype), kind="ExternalInput").ap()
    out = nc.dram_tensor("out_0_dram", (N, D), F32, kind="ExternalOutput").ap()
    build(nc, args, out)
    r = _run(nc, [arrays], core_ids=[0])
    return r.results[0]["out_0_dram"]
```
